# Optimizing a Trainium2 kernel written in Bass

```python
import numpy as np
import jax
import jax.numpy as jnp

def _softmax(x, axis=-1):
    return jax.nn.softmax(x, axis=axis)

def _gelu(x):
    return jax.nn.gelu(x, approximate=True)

def _silu(x):
    return jax.nn.silu(x)

def _sigmoid(x):
    return jax.nn.sigmoid(x)

def _layernorm(x, axis=-1, eps=1e-05):
    m = jnp.mean(x, axis=axis, keepdims=True)
    v = jnp.var(x, axis=axis, keepdims=True)
    return (x - m) / jnp.sqrt(v + eps)

def _scatter_add(tgt, idx, src, axis=0):
    return tgt.at[idx].add(src)

def _segment_sum(src, seg, n):
    return jax.ops.segment_sum(src, seg, n)
kernel_name = 'mk_lm_tower_d2_tok_ids256_r4_bc803a'

def setup_inputs(seed: int=0):
    np.random.seed(seed)
    _w = jnp.asarray

    def _rec_inputs():
        import jax
        import jax.numpy as jnp
        _rk = jax.random.key(seed)
        x = jax.random.randint(jax.random.fold_in(_rk, 1), (8, 1024), 0, 99990, jnp.int32)
        itok_BS_0_99998 = jax.random.randint(jax.random.fold_in(_rk, 21), (8, 1024), 0, 99999, jnp.int32)
        return (x, itok_BS_0_99998)
    x, itok_BS_0_99998 = _rec_inputs()

    def _L0_tok_setup():
        import jax, jax.numpy as jnp
        import numpy as np
        NUM_EMBEDDINGS = 25000
        EMBED_DIM = 64
        BATCH, SEQ = (16, 1024)
        key = jax.random.key(seed)
        k1, k2, k3 = jax.random.split(key, 3)
        input_one = jax.random.randint(k1, (BATCH, SEQ), 0, NUM_EMBEDDINGS, dtype=jnp.int64 if jax.config.jax_enable_x64 else jnp.int32)
        input_two = jax.random.randint(k2, (BATCH, SEQ), 0, NUM_EMBEDDINGS, dtype=input_one.dtype)
        weight = jax.random.normal(k3, (NUM_EMBEDDINGS, EMBED_DIM), dtype=jnp.float32)
        return {'input_one': input_one, 'input_two': input_two, 'weight': weight}
    _L0_tok_all = _L0_tok_setup()
    _L0_tok_in = {k: v for k, v in _L0_tok_all.items() if k in ('weight',)}
    del _L0_tok_all

    def _L0_attn_setup():
        import jax, jax.numpy as jnp
        import numpy as np

        def softcap(x, a=10.0):
            return a * jnp.tanh(x / a)
        key = jax.random.key(seed)
        B, T, D = (4, 512, 64)
        ks = jax.random.split(key, 5)
        w = lambda k, s: jax.random.normal(k, s, dtype=jnp.float32) * 0.02
        return {'x': jax.random.normal(ks[0], (B, T, D), dtype=jnp.float32), 'Wq': w(ks[1], (D, D)), 'bq': jnp.zeros((D,), jnp.float32), 'Wk': w(ks[2], (D, D)), 'bk': jnp.zeros((D,), jnp.float32), 'Wv': w(ks[3], (D, D)), 'bv': jnp.zeros((D,), jnp.float32), 'Wg': w(ks[4], (D, 3 * D)), 'bg': jnp.zeros((3 * D,), jnp.float32), 'input_bias': -jnp.ones((D,), jnp.float32), 'norm_scale': jnp.ones((D,), jnp.float32)}
    _L0_attn_all = _L0_attn_setup()
    _L0_attn_in = {k: v for k, v in _L0_attn_all.items() if k in ('Wq', 'bq', 'Wk', 'bk', 'Wv', 'bv', 'Wg', 'bg', 'input_bias', 'norm_scale')}
    del _L0_attn_all

    def _L0_ffn_setup():
        import jax, jax.numpy as jnp
        import numpy as np
        DIM = 64
        HEADS = 8
        NUM_KEYS = 64
        NUM_KV = NUM_KEYS ** 2
        PK_TOPK = 16
        FINAL_TOPK = 16
        DIM_KEY = DIM // 2
        P = 2

        def _pk(x, Wq_pk, pk_keys):
            b, n, _ = x.shape
            q = (x @ Wq_pk).reshape(b, n, P, HEADS, DIM_KEY).transpose(2, 0, 1, 3, 4)
            sim = jnp.einsum('pbnhd,pkhd->pbnhk', q, pk_keys)
            scores, idx = jax.lax.top_k(sim, PK_TOPK)
            idx0 = idx[0]
            idx1 = idx[1] * NUM_KEYS
            index = (idx0[..., :, None] + idx1[..., None, :]).reshape(b, n, HEADS, PK_TOPK * PK_TOPK)
            score = (scores[0][..., :, None] + scores[1][..., None, :]).reshape(b, n, HEADS, PK_TOPK * PK_TOPK)
            final_scores, pk_idx = jax.lax.top_k(score, FINAL_TOPK)
            final_indices = jnp.take_along_axis(index, pk_idx, axis=-1)
            final_scores = jax.nn.softmax(final_scores, axis=-1)
            return (final_scores, final_indices)
        key = jax.random.key(seed)
        ks = jax.random.split(key, 7)
        b, n = (2, 256)
        std = 0.02
        x = jax.random.normal(ks[0], (b, n, DIM), dtype=jnp.float32)
        Wq_pk = jax.random.normal(ks[1], (DIM, P * HEADS * DIM_KEY), dtype=jnp.float32) * std
        pk_keys = jax.random.normal(ks[2], (P, NUM_KEYS, HEADS, DIM_KEY), dtype=jnp.float32) * std
        Wq = jax.random.normal(ks[3], (DIM, HEADS * DIM), dtype=jnp.float32) * std
        keys_table = jax.random.normal(ks[4], (NUM_KV * HEADS, DIM), dtype=jnp.float32) * std
        values_table = jax.random.normal(ks[5], (NUM_KV * HEADS, DIM), dtype=jnp.float32) * std
        Wo = jax.random.normal(ks[6], (DIM * HEADS, DIM), dtype=jnp.float32) * std
        return {'x': x, 'Wq_pk': Wq_pk, 'pk_keys': pk_keys, 'Wq': Wq, 'keys_table': keys_table, 'values_table': values_table, 'Wo': Wo}
    _L0_ffn_all = _L0_ffn_setup()
    _L0_ffn_in = {k: v for k, v in _L0_ffn_all.items() if k in ('Wq_pk', 'pk_keys', 'Wq', 'keys_table', 'values_table', 'Wo')}
    del _L0_ffn_all

    def _L1_attn_setup():
        import jax, jax.numpy as jnp
        import numpy as np
        B, S, D = (8, 256, 64)

        def _linear_params(key, d):
            k1, k2 = jax.random.split(key)
            lim = 1.0 / np.sqrt(d)
            W = jax.random.uniform(k1, (d, d), jnp.float32, -lim, lim)
            b = jax.random.uniform(k2, (d,), jnp.float32, -lim, lim)
            return (W, b)
        key = jax.random.key(seed)
        ks = jax.random.split(key, 7)
        x = jax.random.normal(ks[0], (B, S, D), jnp.float32)
        Wq, bq = _linear_params(ks[1], D)
        Wk, bk = _linear_params(ks[2], D)
        Wv, bv = _linear_params(ks[3], D)
        Wf, bf = _linear_params(ks[4], D)
        Wi, bi = _linear_params(ks[5], D)
        Wo, bo = _linear_params(ks[6], D)
        return {'x': x, 'Wq': Wq, 'bq': bq, 'Wk': Wk, 'bk': bk, 'Wv': Wv, 'bv': bv, 'Wf': Wf, 'bf': bf, 'Wi': Wi, 'bi': bi, 'Wo': Wo, 'bo': bo}
    _L1_attn_all = _L1_attn_setup()
    _L1_attn_in = {k: v for k, v in _L1_attn_all.items() if k in ('Wq', 'bq', 'Wk', 'bk', 'Wv', 'bv', 'Wf', 'bf', 'Wi', 'bi', 'Wo', 'bo')}
    del _L1_attn_all

    def _L1_ffn_setup():
        import jax, jax.numpy as jnp
        import numpy as np
        NUM_EXPERTS = 8
        TOP_K = 2
        B, S, D = (8, 2048, 64)

        def _moe(tokens, router_w, w1, b1, w2, b2):
            N = tokens.shape[0]
            E = router_w.shape[0]
            logits = tokens.astype(jnp.float32) @ router_w.astype(jnp.float32).T
            probs = jax.nn.softmax(logits, axis=-1)
            rw, re = jax.lax.top_k(probs, TOP_K)
            if TOP_K > 1:
                rw = rw / jnp.maximum(rw.sum(-1, keepdims=True), 1e-12)
            rw = rw.astype(tokens.dtype)
            combine = jnp.zeros((N, E), tokens.dtype).at[jnp.arange(N)[:, None], re].set(rw)
            out = tokens
            for e in range(E):
                h = jax.nn.gelu(tokens @ w1[e] + b1[e], approximate=False)
                y = h @ w2[e] + b2[e]
                out = out + combine[:, e:e + 1] * y
            return out
        key = jax.random.key(seed)
        ks = jax.random.split(key, 4)
        scale = 1.0 / np.sqrt(D).astype(np.float32)
        return {'input_embeddings': jax.random.normal(ks[0], (B, S, D), jnp.float32), 'router_w': jax.random.normal(ks[1], (NUM_EXPERTS, D), jnp.float32) * scale, 'w1': jax.random.normal(ks[2], (NUM_EXPERTS, D, D), jnp.float32) * scale, 'b1': jnp.zeros((NUM_EXPERTS, D), jnp.float32), 'w2': jax.random.normal(ks[3], (NUM_EXPERTS, D, D), jnp.float32) * scale, 'b2': jnp.zeros((NUM_EXPERTS, D), jnp.float32)}
    _L1_ffn_all = _L1_ffn_setup()
    _L1_ffn_in = {k: v for k, v in _L1_ffn_all.items() if k in ('router_w', 'w1', 'b1', 'w2', 'b2')}
    del _L1_ffn_all
    return {'x': x, 'itok_BS_0_99998': itok_BS_0_99998, 'L0_tok_weight': _L0_tok_in['weight'], 'L0_attn_Wq': _L0_attn_in['Wq'], 'L0_attn_bq': _L0_attn_in['bq'], 'L0_attn_Wk': _L0_attn_in['Wk'], 'L0_attn_bk': _L0_attn_in['bk'], 'L0_attn_Wv': _L0_attn_in['Wv'], 'L0_attn_bv': _L0_attn_in['bv'], 'L0_attn_Wg': _L0_attn_in['Wg'], 'L0_attn_bg': _L0_attn_in['bg'], 'L0_attn_input_bias': _L0_attn_in['input_bias'], 'L0_attn_norm_scale': _L0_attn_in['norm_scale'], 'L0_ffn_Wq_pk': _L0_ffn_in['Wq_pk'], 'L0_ffn_pk_keys': _L0_ffn_in['pk_keys'], 'L0_ffn_Wq': _L0_ffn_in['Wq'], 'L0_ffn_keys_table': _L0_ffn_in['keys_table'], 'L0_ffn_values_table': _L0_ffn_in['values_table'], 'L0_ffn_Wo': _L0_ffn_in['Wo'], 'L1_attn_Wq': _L1_attn_in['Wq'], 'L1_attn_bq': _L1_attn_in['bq'], 'L1_attn_Wk': _L1_attn_in['Wk'], 'L1_attn_bk': _L1_attn_in['bk'], 'L1_attn_Wv': _L1_attn_in['Wv'], 'L1_attn_bv': _L1_attn_in['bv'], 'L1_attn_Wf': _L1_attn_in['Wf'], 'L1_attn_bf': _L1_attn_in['bf'], 'L1_attn_Wi': _L1_attn_in['Wi'], 'L1_attn_bi': _L1_attn_in['bi'], 'L1_attn_Wo': _L1_attn_in['Wo'], 'L1_attn_bo': _L1_attn_in['bo'], 'L1_ffn_router_w': _L1_ffn_in['router_w'], 'L1_ffn_w1': _L1_ffn_in['w1'], 'L1_ffn_b1': _L1_ffn_in['b1'], 'L1_ffn_w2': _L1_ffn_in['w2'], 'L1_ffn_b2': _L1_ffn_in['b2']}

def reference(x, itok_BS_0_99998, L0_tok_weight, L0_attn_Wq, L0_attn_bq, L0_attn_Wk, L0_attn_bk, L0_attn_Wv, L0_attn_bv, L0_attn_Wg, L0_attn_bg, L0_attn_input_bias, L0_attn_norm_scale, L0_ffn_Wq_pk, L0_ffn_pk_keys, L0_ffn_Wq, L0_ffn_keys_table, L0_ffn_values_table, L0_ffn_Wo, L1_attn_Wq, L1_attn_bq, L1_attn_Wk, L1_attn_bk, L1_attn_Wv, L1_attn_bv, L1_attn_Wf, L1_attn_bf, L1_attn_Wi, L1_attn_bi, L1_attn_Wo, L1_attn_bo, L1_ffn_router_w, L1_ffn_w1, L1_ffn_b1, L1_ffn_w2, L1_ffn_b2):
    import jax
    import jax.numpy as jnp

    def _L0_tok_ref(input_one, input_two, weight):
        import jax, jax.numpy as jnp
        import numpy as np
        NUM_EMBEDDINGS = 25000
        EMBED_DIM = 64
        BATCH, SEQ = (16, 1024)
        e1 = weight[input_one]
        e2 = weight[input_two]
        same = (input_one == input_two)[..., None]
        return jnp.where(same, e1, e1 + e2)

    def _L0_attn_ref(x, Wq, bq, Wk, bk, Wv, bv, Wg, bg, input_bias, norm_scale):
        import jax, jax.numpy as jnp
        import numpy as np

        def softcap(x, a=10.0):
            return a * jnp.tanh(x / a)
        B, T, D = x.shape
        inv_sqrt_d = 1.0 / jnp.sqrt(jnp.asarray(D, jnp.float32))
        q = x @ Wq + bq
        k = (x @ Wk + bk) * inv_sqrt_d
        v = x @ Wv + bv
        gates = x @ Wg + bg
        i_pre, f_pre, o_pre = jnp.split(gates, 3, axis=-1)
        log_i = softcap(i_pre + input_bias)
        log_f = -jax.nn.softplus(f_pre)

        def step(carry, inp):
            M, n, m = carry
            qt, kt, vt, li, lf, op = inp
            m_next = jnp.maximum(lf + m, li)
            i_s = jnp.exp(li - m_next)
            f_s = jnp.exp(lf + m - m_next)
            M = f_s[:, :, None] * M + i_s[:, :, None] * (vt[:, :, None] * kt[:, None, :])
            n = f_s * n + i_s * kt
            h_raw = jnp.einsum('bij,bj->bi', M, qt)
            denom = jnp.maximum(jnp.abs(jnp.einsum('bi,bi->b', n, qt))[:, None], 1e-06)
            h = jax.nn.sigmoid(op) * (h_raw / denom)
            return ((M, n, m_next), h)
        M0 = jnp.zeros((B, D, D), jnp.float32)
        n0 = jnp.zeros((B, D), jnp.float32)
        m0 = jnp.zeros((B, D), jnp.float32)
        xs = tuple((jnp.swapaxes(a, 0, 1) for a in (q, k, v, log_i, log_f, o_pre)))
        _, hs = jax.lax.scan(step, (M0, n0, m0), xs)
        out = jnp.swapaxes(hs, 0, 1)
        rms = jnp.sqrt(jnp.mean(out * out, axis=-1, keepdims=True) + 1e-08)
        return out / rms * norm_scale

    def _L0_ffn_ref(x, Wq_pk, pk_keys, Wq, keys_table, values_table, Wo):
        import jax, jax.numpy as jnp
        import numpy as np
        DIM = 64
        HEADS = 8
        NUM_KEYS = 64
        NUM_KV = NUM_KEYS ** 2
        PK_TOPK = 16
        FINAL_TOPK = 16
        DIM_KEY = DIM // 2
        P = 2

        def _pk(x, Wq_pk, pk_keys):
            b, n, _ = x.shape
            q = (x @ Wq_pk).reshape(b, n, P, HEADS, DIM_KEY).transpose(2, 0, 1, 3, 4)
            sim = jnp.einsum('pbnhd,pkhd->pbnhk', q, pk_keys)
            scores, idx = jax.lax.top_k(sim, PK_TOPK)
            idx0 = idx[0]
            idx1 = idx[1] * NUM_KEYS
            index = (idx0[..., :, None] + idx1[..., None, :]).reshape(b, n, HEADS, PK_TOPK * PK_TOPK)
            score = (scores[0][..., :, None] + scores[1][..., None, :]).reshape(b, n, HEADS, PK_TOPK * PK_TOPK)
            final_scores, pk_idx = jax.lax.top_k(score, FINAL_TOPK)
            final_indices = jnp.take_along_axis(index, pk_idx, axis=-1)
            final_scores = jax.nn.softmax(final_scores, axis=-1)
            return (final_scores, final_indices)
        b, n, d = x.shape
        q = (x @ Wq).reshape(b, n, HEADS, DIM) * DIM ** (-0.5)
        kv_scores, indices = _pk(x, Wq_pk, pk_keys)
        offsets = jnp.arange(HEADS, dtype=indices.dtype) * NUM_KV
        ind = indices + offsets[None, None, :, None]
        k = jnp.einsum('bnhk,bnhkd->bnhd', kv_scores, keys_table[ind])
        v = jnp.einsum('bnhk,bnhkd->bnhd', kv_scores, values_table[ind])
        sim = jnp.einsum('bihd,bjhd->bhij', q, k)
        neg = -jnp.finfo(sim.dtype).max
        causal = jnp.tril(jnp.ones((n, n), dtype=bool))
        sim = jnp.where(causal, sim, neg)
        attn = jax.nn.softmax(sim, axis=-1)
        out = jnp.einsum('bhij,bjhd->bhid', attn, v)
        out = out.transpose(0, 2, 1, 3).reshape(b, n, HEADS * DIM)
        return out @ Wo

    def _L1_attn_ref(x, Wq, bq, Wk, bk, Wv, bv, Wf, bf, Wi, bi, Wo, bo):
        import jax, jax.numpy as jnp
        import numpy as np
        B, S, D = (8, 256, 64)

        def _linear_params(key, d):
            k1, k2 = jax.random.split(key)
            lim = 1.0 / np.sqrt(d)
            W = jax.random.uniform(k1, (d, d), jnp.float32, -lim, lim)
            b = jax.random.uniform(k2, (d,), jnp.float32, -lim, lim)
            return (W, b)
        q = x @ Wq.T + bq
        k = x @ Wk.T + bk
        v = x @ Wq.T + bq
        f = jax.nn.sigmoid(x @ Wf.T + bf)
        i = jnp.exp(x @ Wi.T + bi)
        xs = tuple((jnp.swapaxes(a, 0, 1) for a in (f, i, k, v, q)))
        C0 = jnp.zeros((x.shape[0], x.shape[2], x.shape[2]), x.dtype)
        n0 = jnp.zeros((x.shape[0], x.shape[2]), x.dtype)

        def step(carry, t):
            C, n = carry
            ft, it, kt, vt, qt = t
            C = ft[:, :, None] * C + it[:, :, None] * (vt[:, :, None] * kt[:, None, :])
            n = ft * n + it * kt
            num = jnp.einsum('bik,bk->bi', C, qt)
            den = jnp.maximum(jnp.abs(jnp.einsum('bk,bk->b', n, qt)), 1.0)[:, None]
            return ((C, n), num / den)
        _, h = jax.lax.scan(step, (C0, n0), xs)
        h = jnp.swapaxes(h, 0, 1)
        return h @ Wo.T + bo

    def _L1_ffn_ref(input_embeddings, router_w, w1, b1, w2, b2):
        import jax, jax.numpy as jnp
        import numpy as np
        NUM_EXPERTS = 8
        TOP_K = 2
        B, S, D = (8, 2048, 64)

        def _moe(tokens, router_w, w1, b1, w2, b2):
            N = tokens.shape[0]
            E = router_w.shape[0]
            logits = tokens.astype(jnp.float32) @ router_w.astype(jnp.float32).T
            probs = jax.nn.softmax(logits, axis=-1)
            rw, re = jax.lax.top_k(probs, TOP_K)
            if TOP_K > 1:
                rw = rw / jnp.maximum(rw.sum(-1, keepdims=True), 1e-12)
            rw = rw.astype(tokens.dtype)
            combine = jnp.zeros((N, E), tokens.dtype).at[jnp.arange(N)[:, None], re].set(rw)
            out = tokens
            for e in range(E):
                h = jax.nn.gelu(tokens @ w1[e] + b1[e], approximate=False)
                y = h @ w2[e] + b2[e]
                out = out + combine[:, e:e + 1] * y
            return out
        b, s, d = input_embeddings.shape
        tokens = input_embeddings.reshape(b * s, d)
        return _moe(tokens, router_w, w1, b1, w2, b2).reshape(b, s, d)
    h = _L0_tok_ref(x, itok_BS_0_99998, L0_tok_weight)
    h = h + _L0_attn_ref(_layernorm(h, axis=-1), L0_attn_Wq, L0_attn_bq, L0_attn_Wk, L0_attn_bk, L0_attn_Wv, L0_attn_bv, L0_attn_Wg, L0_attn_bg, L0_attn_input_bias, L0_attn_norm_scale)
    h = h + _L0_ffn_ref(_layernorm(h, axis=-1), L0_ffn_Wq_pk, L0_ffn_pk_keys, L0_ffn_Wq, L0_ffn_keys_table, L0_ffn_values_table, L0_ffn_Wo)
    h = h + _L1_attn_ref(_layernorm(h, axis=-1), L1_attn_Wq, L1_attn_bq, L1_attn_Wk, L1_attn_bk, L1_attn_Wv, L1_attn_bv, L1_attn_Wf, L1_attn_bf, L1_attn_Wi, L1_attn_bi, L1_attn_Wo, L1_attn_bo)
    h = h + _L1_ffn_ref(_layernorm(h, axis=-1), L1_ffn_router_w, L1_ffn_w1, L1_ffn_b1, L1_ffn_w2, L1_ffn_b2)
    return h

_drawn_inputs = setup_inputs


def setup_inputs(seed=0):
    import zlib

    import numpy as np

    out = dict(_drawn_inputs(seed))
    spreads = {'L0_attn_bq': (0.0, 0.1),
     'L0_attn_bk': (0.0, 0.1),
     'L0_attn_bv': (0.0, 0.1),
     'L0_attn_bg': (0.0, 0.1),
     'L0_attn_input_bias': (-1.0, 0.6),
     'L0_attn_norm_scale': (1.0, 0.2),
     'L1_ffn_b1': (0.0, 0.506),
     'L1_ffn_b2': (0.0, 0.316)}
    factors = {'L0_ffn_Wq_pk': 8.0,
     'L0_ffn_pk_keys': 8.0,
     'L0_ffn_Wq': 64.0,
     'L0_ffn_keys_table': 64.0,
     'L0_ffn_values_table': 8.0,
     'L0_ffn_Wo': 8.0,
     'L1_attn_bf': 3.182}
    for name, (base, spread) in spreads.items():
        noise = np.random.default_rng([zlib.crc32(name.encode()), seed]).standard_normal(out[name].shape)
        drawn = base * np.exp(spread * noise) if base else spread * noise
        out[name] = jnp.asarray(drawn.astype(out[name].dtype))
    for name, factor in factors.items():
        out[name] = (out[name] * factor).astype(out[name].dtype)
    return out
```

```python
from contextlib import ExitStack

import concourse.bass as bass
from concourse import mybir
from concourse.alu_op_type import AluOpType as ALU

F32 = mybir.dt.float32
BF16 = mybir.dt.bfloat16
I32 = mybir.dt.int32
U32 = mybir.dt.uint32
ACT = mybir.ActivationFunctionType
AX = mybir.AxisListType.X

P = 128
D = 64
BATCH, SEQ = 8, 1024
TILES = BATCH * SEQ // P
ROW_TILES = SEQ // P
HEADS = 8
PAIRS = HEADS // 2
TOPK = 16
NUM_KEYS = 64
DIM_KEY = 32
EXPERTS = 8
HALF = D // 2
GROUPS = HALF // 2
QUARTERS = 4
RING = 4
EPS = 1e-5
LOWEST = -3.0e38
MASKED = -1.0e30
LOTS = [(0, 1, 16), (1, 1, 8), (2, 2, 5), (4, 4, 3), (8, 8, 1)]
STARTS = [s for s in [0]]
for _a0, _na, _nb in LOTS:
    for _ in range(_na):
        STARTS.append(STARTS[-1] + _nb)
CANDS = STARTS.pop()


def wait(eng, sem, value):
    if not isinstance(value, int) or value > 0:
        eng.wait_ge(sem, value)


class Parts:
    pass


class Steps:

    def __init__(self, eng, sem, done, total):
        self.eng, self.sem, self.done, self.total, self.n = eng, sem, done, total, 0

    def link(self, ins):
        self.n += 1
        ins.then_inc(self.sem, 1)
        self.eng.wait_ge(self.sem, self.done * self.total + self.n)

    def close(self):
        assert self.n == self.total, (self.n, self.total)


def tower(nc, x_ids, itok_ids, tok_w, w0, input_bias, norm_scale, wqpk, pk_keys, wq, kv_table, wo, w1, wo1,
          router, up, down, down_bias, out):
    V = tok_w.shape[0]
    ctx = ExitStack()
    with ctx:
        def sb(name, shape, dt=F32):
            return ctx.enter_context(nc.sbuf_tensor(name, shape, dt))

        def ps(name, shape, dt=F32):
            return ctx.enter_context(nc.psum_tensor(name, shape, dt))

        def sem(name):
            return ctx.enter_context(nc.semaphore(name))

        ident = sb("ident", [P, P])
        ident_b = sb("ident_b", [P, P], BF16)
        causal = sb("causal", [P, 2 * SEQ - P], BF16)
        row_sel = sb("row_sel", [D, HALF, 2, D])
        half_sel = sb("half_sel", [P, 2])
        ones_col = sb("ones_col", [D, 1])
        keep = sb("keep", [P, TILES])
        starts = sb("starts", [P, TOPK], BF16)
        start_steps = sb("start_steps", [P, TOPK], BF16)
        count16 = sb("count16", [P, TOPK], BF16)
        count8 = sb("count8", [P, EXPERTS])
        head_base = sb("head_base", [P, HEADS])
        w0_sb = sb("w0_sb", [D + 1, 8 * D])
        ib_sb = sb("ib_sb", [D, 1])
        ib5_sb = sb("ib5_sb", [D, 1])
        ns_sb = sb("ns_sb", [P, D])
        wqpk_sb = sb("wqpk_sb", [D, 512])
        pkk_sb = sb("pkk_sb", [P, 4, 4 * NUM_KEYS])
        wq_sb = sb("wq_sb", [D, HEADS * D])
        wo_sb = sb("wo_sb", [P, PAIRS, D])
        w1_sb = sb("w1_sb", [D + 1, 6 * D])
        wo1_sb = sb("wo1_sb", [D + 1, D])
        router_sb = sb("router_sb", [D, EXPERTS])
        up_sb = sb("up_sb", [D + 1, EXPERTS * D])
        down_sb = sb("down_sb", [P, 4, D])
        db_sb = sb("db_sb", [EXPERTS, D])
        ids = sb("ids", [P, 2, TILES], I32)
        idf = sb("idf", [P, 2, TILES])
        neg = sb("neg", [P, 2, TILES])
        differ = sb("differ", [P, TILES])
        rows = sb("rows", [P, 2, TILES + 1], I32)
        tok_idx = sb("tok_idx", [P, 2], I32)
        emb = sb("emb", [P, 2, D])
        x0, h0 = sb("x0", [P, D]), sb("h0", [P, D])
        x1 = sb("x1", [P, 4 * D])
        stat_f, mv_f = sb("stat_f", [P, 6]), sb("mv_f", [P, 2])
        xn_f = sb("xn_f", [P, 2 * D])
        xt0 = sb("xt0", [D + 1, P])
        xt2 = sb("xt2", [D, P])
        soft_in = sb("soft_in", [D, P])
        absf, expf, lnf = sb("absf", [D, P]), sb("expf", [D, P]), sb("lnf", [D, P])
        li, lf = sb("li", [D, P]), sb("lf", [D, P])
        mx = sb("mx", [D, P + 1])
        fe = sb("fe", [D, 2, P])
        osig = sb("osig", [P, D])
        qpk = sb("qpk", [P, 4, P])
        sims = sb("sims", [P, 2 * HEADS, NUM_KEYS])
        sims_left = sb("sims_left", [P, 2 * HEADS, NUM_KEYS])
        best = sb("best", [P, 2 * HEADS, TOPK])
        best_at = sb("best_at", [P, 2 * HEADS, TOPK], U32)
        at_f = sb("at_f", [P, 2 * HEADS, TOPK], BF16)
        at0_steps = sb("at0_steps", [P, HEADS, TOPK], BF16)
        cand = sb("cand", [P, HEADS, CANDS])
        cand_left = sb("cand_left", [P, HEADS, CANDS])
        fin = sb("fin", [P, HEADS, TOPK])
        fin_at = sb("fin_at", [P, HEADS, TOPK], U32)
        place = sb("place", [P, HEADS, TOPK], BF16)
        hot = sb("hot", [P, HEADS, TOPK, TOPK], BF16)
        hotv = sb("hotv", [P, HEADS, TOPK, TOPK], BF16)
        key0 = sb("key0", [P, HEADS, TOPK])
        off = sb("off", [P, HEADS, TOPK])
        rank1 = sb("rank1", [P, HEADS, TOPK], BF16)
        key1 = sb("key1", [P, HEADS, TOPK])
        wsum = sb("wsum", [P, HEADS])
        idx = [sb(f"idx{p}", [P, HEADS * TOPK], I32) for p in range(2)]
        wt = [sb(f"wt{p}", [P, HEADS, TOPK]) for p in range(2)]
        qs = sb("qs", [P, PAIRS, P])
        got = sb("got", [P, RING, TOPK, 2 * D])
        ktmp = sb("ktmp", [P, 2 * D])
        kt = sb("kt", [P, PAIRS, SEQ])
        vc = sb("vc", [P, ROW_TILES * HEADS * D])
        nmax = sb("nmax", [P, HEADS])
        rsum = sb("rsum", [P, HEADS])
        rrec = sb("rrec", [P, HEADS])
        pr = [sb(f"pr{s}", [P, SEQ]) for s in range(2)]
        prt = [sb(f"prt{s}", [P, ROW_TILES, P]) for s in range(2)]
        att = [sb(f"att{p}", [P, HEADS * D]) for p in range(2)]
        att_t = sb("att_t", [P, PAIRS, P])
        x2, x3 = sb("x2", [P, D]), sb("x3", [P, D])
        stat_t, mv_t = sb("stat_t", [P, 6]), sb("mv_t", [P, 2])
        xn_t, h_pad = sb("xn_t", [P, 2 * D]), sb("h_pad", [P, 2 * D])
        xt3 = sb("xt3", [D + 1, P])
        ht = sb("ht", [D + 1, P])
        xt4 = sb("xt4", [D + 1, P])
        lmax, esum, prob_scale = sb("lmax", [P, 1]), sb("esum", [P, 1]), sb("prob_scale", [P, 1])
        exps, probs, top8 = sb("exps", [P, EXPERTS]), sb("probs", [P, EXPERTS]), sb("top8", [P, 8])
        top_at, top_f = sb("top_at", [P, 8], U32), sb("top_f", [P, 8])
        two, two_rec = sb("two", [P, 1]), sb("two_rec", [P, 1])
        chosen, combine = sb("chosen", [P, EXPERTS]), sb("combine", [P, EXPERTS])
        hid = sb("hid", [P, EXPERTS, D])
        hid_t = sb("hid_t", [P, 4, P])
        comb_t = sb("comb_t", [EXPERTS, P])
        res = sb("res", [P, D])
        y_out = sb("y_out", [P, D])

        weighed, states = sb("weighed", [P, 2, 2, P]), sb("states", [P, HALF, P])
        den, den_rec = sb("den", [P, 1]), sb("den_rec", [P, 1])

        def layer(n):
            s = Parts()
            s.k2, s.q2 = sb(f"k2_{n}", [P, P]), sb(f"q2_{n}", [P, P])
            s.gates = sb(f"gates{n}", [D, 3, P])
            s.ik = sb(f"ik{n}", [D, P])
            s.nst, s.nq = sb(f"nst{n}", [D, P + 1]), sb(f"nq{n}", [D, P])
            s.mc, s.mc0 = sb(f"mc{n}", [P, HALF]), sb(f"mc0_{n}", [P, HALF])
            s.w, s.y, s.den, s.dr = weighed, states, den, den_rec
            s.proj, s.gated = sem(f"proj_ps{n}"), sem(f"gates_begun{n}")
            s.gates_ready, s.nq_ready = sem(f"gates_ready{n}"), sem(f"nq_ready{n}")
            s.spread, s.scanned = sem(f"spread_ps{n}"), sem(f"scanned{n}")
            s.yq_ready, s.hraw = sem(f"yq_ready{n}"), sem(f"read_out_ps{n}")
            return s

        lay = [layer(0), layer(1)]
        ss, sq = sb("ss", [P, 1]), sb("sq", [P, D])

        def root(n):
            s = Parts()
            s.v, s.l, s.g, s.a, s.y = (sb(f"root_{what}{n}", [P, 1]) for what in "vlgay")
            s.asked, s.logged, s.guess = sem(f"root_asked{n}"), sem(f"root_log{n}"), sem(f"root_guess{n}")
            return s

        root_f, root_t = root(0), root(1)

        score_ps = [ps(f"score_ps{s}", [P, SEQ]) for s in range(2)]
        head_ps = ps("head_ps", [P, 512])
        wide = [ps(f"wide{s}", [P, 512]) for s in range(2)]
        small = ps("small", [P, 512])
        xt_ps, h_ps, den_ps = small[:, 0:P], small[:, P:P + D], small[:, P + D:P + D + 1]
        xt_pt, h_pt, den_pt = small[:, 256:384], small[:, 384:448], small[:, 448:449]
        logit_ps = small[:, 456:456 + EXPERTS]
        kt_ps = head_ps[:, 256:384]

        s_w = sem("weights_in")
        s_ids = sem("ids_in")
        s_const_pool = sem("const_pool")
        s_const_dve = sem("const_dve")
        s_turn_dve, s_turn_pool = sem("turn_dve"), sem("turn_pool")
        s_start = sem("dve_start_steps")
        s_tokidx = sem("tok_idx_ready")
        s_tok = sem("tok_rows_in")
        s_tokused = sem("tok_rows_used")
        s_xn = sem("xn_front")
        s_xtps = sem("xt_front_ps")
        s_xt = sem("xt_front")
        s_fe = sem("gate_exponents")
        s_fi = sem("gate_exp")
        s_act0 = sem("act_steps0")
        s_fr = sem("front_steps")
        s_qpkps = sem("qpk_ps")
        s_qpk = sem("qpk_copied")
        s_simps = sem("sims_ps")
        s_sim = sem("sims_copied")
        s_top = sem("sims_used")
        s_wexp = sem("topk_weight_in")
        s_wexpd = sem("topk_weight_exp")
        s_tk = sem("topk_steps")
        s_idx = sem("idx_ready")
        s_got = [sem(f"rows_in{h}") for h in range(HEADS)]
        s_q = sem("q_ps")
        s_qs = sem("q_scaled")
        s_gw = sem("rows_weighted")
        s_kv = sem("kv_summed")
        s_kvc = sem("kv_copied")
        s_ktps = sem("kt_ps_full")
        s_kt = sem("kt_stored")
        s_sc = sem("scores_ps_full")
        s_nm = sem("max_ready")
        s_nms = sem("max_steps")
        s_p = sem("probs_ready")
        s_pps = sem("probs_t_ps")
        s_pt = sem("probs_t")
        s_o = sem("att_ps_full")
        s_os = sem("att_steps")
        s_att = sem("att_ready")
        s_atps = sem("att_t_ps")
        s_att_t = sem("att_t")
        s_wo = sem("wo_ps")
        s_ts = sem("tail_steps")
        s_xnt = sem("xn_tail")
        s_xtps_t = sem("xt_tail_ps")
        s_xt_t = sem("xt_tail")
        s_h1 = sem("h1_ready")
        s_wo1 = sem("wo1_ps")
        s_up = sem("up_ps")
        s_gelu = sem("gelu")
        s_lm = sem("logit_max")
        s_le = sem("logit_exp")
        s_cmb = sem("combine_ready")
        s_hid = sem("hidden_weighted")
        s_hps = sem("hidden_t_ps")
        s_hidt = sem("hidden_t")
        s_y = sem("moe_ps")
        s_yout = sem("y_ready")
        s_out = sem("stored")

        block = ctx.enter_context(nc.Block())

        def tile_loop(eng, heads_open, heads_slot, front_slot, tail_slot):
            for s in range(4):
                front_slot(s, 0, 0)

            def tile(t, p):
                heads_open(t)
                for s in range(HEADS + 2):
                    if s < 4 and not (isinstance(t, int) and t + 1 >= TILES):
                        front_slot(s, t + 1, 1 - p)
                    if 4 <= s < 8 and not (isinstance(t, int) and t < 1):
                        tail_slot(s - 4, t - 1, 1 - p)
                    heads_slot(s, t, p)

            tile(0, 0)
            with eng.Fori(0, (TILES - 2) // 2) as i:
                tile(2 * i + 1, 1)
                tile(2 * i + 2, 0)
            tile(TILES - 1, 1)
            for s in range(4):
                tail_slot(s, TILES - 1, 1)

        @block.sync
        def _(sp):
            sp.dma_start(ids[:, 0, :], x_ids).then_inc(s_ids, 16)
            sp.dma_start(ids[:, 1, :], itok_ids).then_inc(s_ids, 16)
            loads = [(w0_sb[:, :], w0), (ib_sb[:, :], input_bias), (ns_sb[:, :], norm_scale.broadcast_to([P, D])),
                     (wqpk_sb[:, :], wqpk), (wq_sb[:, :], wq),
                     (wo_sb[:, :, :], wo.rearrange("(c p) d -> p c d", p=P)),
                     (w1_sb[:, :], w1), (wo1_sb[:, :], wo1), (router_sb[:, :], router), (up_sb[:, :], up),
                     (down_sb[:, :, :], down.rearrange("(c p) d -> p c d", p=P)), (db_sb[:, :], down_bias)]
            for dst, src in loads:
                sp.dma_start(dst, src).then_inc(s_w, 16)
            sp.wait_ge(s_const_dve, 1)
            for c in range(4):
                for h in range(4):
                    sp.dma_start(pkk_sb[DIM_KEY * h:DIM_KEY * (h + 1), c, NUM_KEYS * h:NUM_KEYS * (h + 1)],
                                 pk_keys[4 * c + h]).then_inc(s_w, 16)

            def store(t):
                sp.wait_ge(s_yout, t + 2)
                sp.dma_start(out[bass.ts(t, P), :], y_out[:, :]).then_inc(s_out, 16)

            store(0)
            with sp.Fori(1, TILES) as t:
                store(t)
            sp.wait_ge(s_out, 16 * TILES)

        N_LOADS = 16 * (12 + 16)

        @block.gpsimd
        def _(pool):
            pool.memset(ident[:, :], 0.0)
            pool.memset(causal[:, :], 0.0)
            pool.memset(row_sel[:, :, :, :], 0.0).then_inc(s_const_pool, 1)
            pool.wait_ge(s_const_pool, 1)
            pool.affine_select(out=ident[:, :], in_=ident[:, :], compare_op=ALU.not_equal, fill=1.0, base=0,
                               pattern=[[-1, P]], channel_multiplier=1)
            pool.affine_select(out=causal[:, :], in_=causal[:, :], compare_op=ALU.is_ge, fill=MASKED,
                               base=SEQ - P, pattern=[[-1, 2 * SEQ - P]], channel_multiplier=1)
            pool.affine_select(out=row_sel[:, :, :, :], in_=row_sel[:, :, :, :], compare_op=ALU.not_equal,
                               fill=1.0, base=0, pattern=[[-1, HALF], [-HALF, 2], [0, D]],
                               channel_multiplier=1).then_inc(s_const_pool, 1)

            def embedding(t):
                pool.wait_ge(s_tokidx, t + 1)
                wait(pool, s_tokused, t)
                own_wait()
                for n in range(2):
                    pool.indirect_dma_start(emb[:, n, :], None, tok_w,
                                            bass.IndirectOffsetOnAxis(ap=tok_idx[:, n:n + 1], axis=0)
                                            ).then_inc(s_tok, 16)

            def gather_head(h, t, p):
                if not isinstance(t, int) or HEADS * t + h >= RING:
                    pool.wait_ge(s_kv, HEADS * t + h + 1 - RING)
                    own_wait()
                for r in range(TOPK):
                    n = h * TOPK + r
                    pool.indirect_dma_start(got[:, h % RING, r, :], None, kv_table,
                                            bass.IndirectOffsetOnAxis(ap=idx[p][:, n:n + 1], axis=0)
                                            ).then_inc(s_got[h], 16)

            def heads_open(t):
                if not isinstance(t, int) or t + 1 < TILES:
                    embedding(t + 1)
                pool.wait_ge(s_idx, t + 1)
                own_wait()

            def heads_slot(s, t, p):
                if s < HEADS:
                    gather_head(s, t, p)

            def own_wait():
                pool.sem_inc(s_turn_pool, 1)

            embedding(0)
            tile_loop(pool, heads_open, heads_slot, lambda s, t, p: None, lambda s, t, p: None)

        @block.vector
        def _(dve):
            dve.memset(pkk_sb[:, :, :], 0.0).then_inc(s_const_dve, 1)
            dve.memset(half_sel[:, :], 0.0)
            dve.memset(ones_col[:, :], 1.0)
            for a in range(TOPK):
                dve.memset(starts[:, a:a + 1], float(STARTS[a]))
                dve.memset(start_steps[:, a:a + 1], float(STARTS[a] - STARTS[a - 1] if a else 0))
                dve.memset(count16[:, a:a + 1], float(a))
            for h in range(HEADS):
                dve.memset(count8[:, h:h + 1], float(h))
                dve.memset(head_base[:, h:h + 1], float(h * NUM_KEYS * NUM_KEYS))
            dve.memset(xt0[D:D + 1, :], 1.0)
            dve.memset(xt3[D:D + 1, :], 1.0)
            dve.memset(ht[D:D + 1, :], 1.0)
            dve.memset(xt4[D:D + 1, :], 1.0)
            for padded in (xn_f, xn_t, h_pad):
                dve.memset(padded[:, :], 0.0)
            dve.memset(mx[:, :], 0.0)
            for s in lay:
                dve.memset(s.mc[:, :], 0.0)
                dve.memset(s.nst[:, :], 0.0)
            dve.memset(kt[:, :, :], 0.0)
            dve.memset(vc[:, :], 0.0)
            dve.memset(y_out[:, :], 0.0).then_inc(s_yout, 1)
            dve.memset(keep[:, :], 1.0)
            dve.memset(rows[:, :, :], 0).then_inc(s_start, 1)
            dve.wait_ge(s_start, 1)
            dve.memset(half_sel[0:D, 0:1], 1.0)
            dve.memset(half_sel[D:P, 1:2], 1.0)
            dve.memset(keep[:, :].rearrange("p (b j) -> p b j", j=ROW_TILES)[:, :, 0:1], 0.0)
            dve.wait_ge(s_ids, 32)
            dve.tensor_copy(idf[:, :, :], ids[:, :, :]).then_inc(s_start, 1)
            dve.wait_ge(s_start, 2)
            dve.tensor_tensor(differ[:, :], idf[:, 0, :], idf[:, 1, :], ALU.not_equal)
            dve.tensor_scalar(neg[:, :, :], idf[:, :, :], 0.0, float(V), ALU.is_lt, ALU.mult).then_inc(s_start, 1)
            dve.wait_ge(s_start, 3)
            dve.tensor_tensor(idf[:, :, :], idf[:, :, :], neg[:, :, :], ALU.add).then_inc(s_start, 1)
            dve.wait_ge(s_start, 4)
            dve.tensor_scalar(rows[:, :, 0:TILES], idf[:, :, :], 0.0, float(V - 1), ALU.max, ALU.min
                              ).then_inc(s_start, 1)
            dve.wait_ge(s_start, 5)
            dve.tensor_copy(tok_idx[:, :], rows[:, :, 0]).then_inc(s_tokidx, 1)
            dve.wait_ge(s_const_pool, 2)
            dve.tensor_copy(ident_b[:, :], ident[:, :])
            dve.wait_ge(s_w, N_LOADS)
            dve.tensor_scalar(ib5_sb[:, :], ib_sb[:, :], 0.2, None, ALU.mult).then_inc(s_const_dve, 1)

            def own_wait():
                dve.sem_inc(s_turn_dve, 1)

            def inverse_root(st, r, done):
                dve.wait_ge(r.guess, done)
                st.link(dve.scalar_tensor_tensor(out=r.a[:, :], in0=r.g[:, :], scalar=r.g[:, 0:1], in1=r.v[:, :],
                                                 op0=ALU.mult, op1=ALU.mult))
                st.link(dve.tensor_scalar(r.a[:, :], r.a[:, :], -0.5, 1.5, ALU.mult, ALU.add))
                st.link(dve.tensor_tensor(r.y[:, :], r.a[:, :], r.g[:, :], ALU.mult))

            def layer_norm(st, x, y, stat, mv, r, done):
                own_wait()
                st.link(dve.bn_stats(stat[:, :], x))
                own_wait()
                st.link(dve.bn_aggr(mv[:, :], stat[:, :]))
                dve.tensor_scalar(r.v[:, :], mv[:, 1:2], EPS, None, ALU.add).then_inc(r.asked, 1)
                inverse_root(st, r, done)
                return dve.tensor_scalar(y, x, mv[:, 0:1], r.y[:, 0:1], ALU.subtract, ALU.mult)

            def carry_state(s, t, st):
                st.link(dve.tensor_scalar(s.mc0[:, :], s.mc[:, :], keep[:, bass.ds(t, 1)], None, ALU.mult))

            def recur(s, groups, t, st):
                def weigh(g):
                    dve.wait_ge(s.spread, GROUPS * t + g + 1)
                    bank = wide[g % 2][:, :].rearrange("p (i a n) -> p i a n", i=2, a=2)
                    return dve.tensor_tensor(s.w[:, g % 2, :, :], bank[:, :, 1, :],
                                             s.k2[:, None, :].broadcast_to([P, 2, P]), ALU.mult)

                for g in groups:
                    st.link(weigh(g))
                    bank = wide[g % 2][:, :].rearrange("p (i a n) -> p i a n", i=2, a=2)
                    for i in range(2):
                        last = dve.tensor_tensor_scan(s.y[:, 2 * g + i, :], bank[:, i, 0, :], s.w[:, g % 2, i, :],
                                                      s.mc0[:, 2 * g + i:2 * g + i + 1], ALU.mult, ALU.add)
                    last.then_inc(s.scanned, 1)
                    if g % 4 == 3:
                        dve.wait_ge(s.scanned, GROUPS * t + g + 1)
                        a = slice(2 * (g - 3), 2 * (g + 1))
                        st.link(dve.tensor_copy(s.mc[:, a], s.y[:, a, P - 1]))
                        dve.tensor_tensor(s.y[:, a, :], s.y[:, a, :], s.q2[:, None, :].broadcast_to([P, 8, P]),
                                          ALU.mult).then_inc(s.yq_ready, 1)

            def magnitude(s, st, x, least):
                st.link(dve.tensor_copy(s.den[:, :], x))
                st.link(dve.scalar_tensor_tensor(out=s.den[:, :], in0=s.den[:, :], scalar=-1.0, in1=s.den[:, :],
                                                 op0=ALU.mult, op1=ALU.max))
                st.link(dve.tensor_scalar(s.den[:, :], s.den[:, :], least, None, ALU.max))

            def normaliser(s, t, st):
                st.link(dve.tensor_scalar(s.nst[:, 0:1], s.nst[:, P:P + 1], keep[0:D, bass.ds(t, 1)], None, ALU.mult))
                st.link(dve.tensor_tensor_scan(s.nst[:, 1:P + 1], s.gates[:, 0, :], s.ik[:, :], s.nst[:, 0:1],
                                               ALU.mult, ALU.add))
                dve.tensor_tensor(s.nq[:, :], s.nst[:, 1:P + 1], s.q2[0:D, :], ALU.mult).then_inc(s.nq_ready, 1)

            def front_slot(seg, t, p):
                if seg == 0:
                    st = Steps(dve, s_fr, t, FRONT_STEPS)
                    front_slot.st = st
                    dve.wait_ge(s_tok, 32 * (t + 1))
                    dve.scalar_tensor_tensor(out=x0[:, :], in0=emb[:, 1, :], scalar=differ[:, bass.ds(t, 1)],
                                             in1=emb[:, 0, :], op0=ALU.mult, op1=ALU.add).then_inc(s_tokused, 1)
                    dve.tensor_copy(tok_idx[:, :], rows[:, :, bass.ds(t + 1, 1)].rearrange("p a b -> p (a b)")
                                    ).then_inc(s_tokidx, 1)
                    dve.wait_ge(s_tokused, t + 1)
                    layer_norm(st, x0[:, :], xn_f[:, 0:D], stat_f, mv_f, root_f, 3 * t + 1).then_inc(s_xn, 1)
                    s = lay[0]
                    dve.wait_ge(s.gated, t + 1)
                    st.link(dve.tensor_scalar(soft_in[:, :], soft_in[:, :], 1.0, None, ALU.add))
                    st.link(dve.reciprocal(li[:, :], soft_in[:, :]))
                    st.link(dve.tensor_scalar(li[:, :], li[:, :], -20.0, 10.0, ALU.mult, ALU.add))
                    f_ps = wide[1][0:D, 2 * P:3 * P]
                    st.link(dve.scalar_tensor_tensor(out=lf[:, :], in0=f_ps, scalar=0.0, in1=lnf[:, :],
                                                     op0=ALU.max, op1=ALU.add))
                    st.link(dve.tensor_scalar(lf[:, :], lf[:, :], -1.0, None, ALU.mult))
                    st.link(dve.tensor_scalar(mx[:, 0:1], mx[:, P:P + 1], keep[0:D, bass.ds(t, 1)], None, ALU.mult))
                    st.link(dve.tensor_tensor_scan(mx[:, 1:P + 1], lf[:, :], li[:, :], mx[:, 0:1], ALU.add, ALU.max))
                    st.link(dve.tensor_tensor(fe[:, 0, :], lf[:, :], mx[:, 0:P], ALU.add))
                    dve.tensor_tensor(fe[:, 0, :], fe[:, 0, :], mx[:, 1:P + 1], ALU.subtract)
                    dve.tensor_tensor(fe[:, 1, :], li[:, :], mx[:, 1:P + 1], ALU.subtract).then_inc(s_fe, 1)
                    st.link(dve.tensor_scalar(osig[:, :], osig[:, :], 1.0, None, ALU.add))
                    st.link(dve.reciprocal(osig[:, :], osig[:, :]))
                    dve.wait_ge(s_fi, t + 1)
                    dve.tensor_tensor(s.gates[:, 1, :], s.gates[:, 2, :], wide[1][0:D, 0:P], ALU.mult
                                      ).then_inc(s.gates_ready, 1)
                    st.link(dve.tensor_tensor(s.ik[:, :], s.gates[:, 2, :], s.k2[0:D, :], ALU.mult))
                    wait(dve, s.hraw, t)
                    normaliser(s, t, st)
                    carry_state(s, t, st)
                if seg == 1:
                    recur(lay[0], range(0, GROUPS // 2), t, front_slot.st)
                if seg == 2:
                    s, st = lay[0], front_slot.st
                    recur(s, range(GROUPS // 2, GROUPS), t, st)
                    dve.wait_ge(s.hraw, t + 1)
                    magnitude(s, st, den_ps, 1e-6)
                    st.link(dve.reciprocal(s.dr[:, :], s.den[:, :]))
                    st.link(dve.scalar_tensor_tensor(out=h0[:, :].rearrange("p (a i) -> p a i", a=2),
                                                     in0=h_ps.rearrange("p (i a) -> p a i", a=2),
                                                     scalar=s.dr[:, 0:1],
                                                     in1=osig[:, :].rearrange("p (a i) -> p a i", a=2),
                                                     op0=ALU.mult, op1=ALU.mult))
                    st.link(dve.tensor_tensor_reduce(sq[:, :], h0[:, :], h0[:, :], 1.0, 0.0, ALU.mult, ALU.add,
                                                     ss[:, :]))
                    dve.tensor_scalar(root_f.v[:, :], ss[:, :], 1.0 / D, 1e-8, ALU.mult, ALU.add
                                      ).then_inc(root_f.asked, 1)
                    inverse_root(st, root_f, 3 * t + 2)
                    st.link(dve.scalar_tensor_tensor(out=h0[:, :], in0=h0[:, :], scalar=root_f.y[:, 0:1],
                                                     in1=ns_sb[:, :], op0=ALU.mult, op1=ALU.mult))
                    st.link(dve.tensor_tensor(x1[:, bass.ds((t & 3) * D, D)], h0[:, :], x0[:, :], ALU.add))
                    layer_norm(st, x1[:, bass.ds((t & 3) * D, D)], xn_f[:, 0:D], stat_f, mv_f,
                               root_f, 3 * t + 3).then_inc(s_xn, 1)
                    st.close()
                if seg == 3:
                    topk(t, p)

            def topk(t, p):
                st = Steps(dve, s_tk, t, TOPK_STEPS)
                dve.wait_ge(s_sim, 2 * (t + 1))
                def best8(lo, src):
                    own_wait()
                    for n in range(2 * HEADS):
                        last = dve.max(best[:, n, lo:lo + 8], src[:, n, :])
                    st.link(last)
                    own_wait()
                    for n in range(2 * HEADS):
                        last = dve.max_index(best_at[:, n, lo:lo + 8], best[:, n, lo:lo + 8], src[:, n, :])
                    return last
                best8(0, sims)
                for n in range(2 * HEADS):
                    last = dve.match_replace(sims_left[:, n, :], best[:, n, 0:8], sims[:, n, :], LOWEST)
                last.then_inc(s_top, 1)
                dve.wait_ge(s_top, t + 1)
                st.link(best8(8, sims_left))
                dve.tensor_copy(at_f[:, :, :], best_at[:, :, :])
                for (a0, na, nb), at in zip(LOTS, [0, 16, 24, 34, 46]):
                    last = dve.tensor_tensor(
                        cand[:, :, at:at + na * nb].rearrange("p h (a b) -> p h a b", a=na),
                        best[:, 0:HEADS, a0:a0 + na, None].broadcast_to([P, HEADS, na, nb]),
                        best[:, HEADS:2 * HEADS, None, 0:nb].broadcast_to([P, HEADS, na, nb]), ALU.add)
                st.link(last)
                def final8(lo, src):
                    own_wait()
                    for h in range(HEADS):
                        last = dve.max(fin[:, h, lo:lo + 8], src[:, h, :])
                    st.link(last)
                    own_wait()
                    for h in range(HEADS):
                        last = dve.max_index(fin_at[:, h, lo:lo + 8], fin[:, h, lo:lo + 8], src[:, h, :])
                    return last
                final8(0, cand)
                for h in range(HEADS):
                    last = dve.match_replace(cand_left[:, h, :], fin[:, h, 0:8], cand[:, h, :], LOWEST)
                st.link(last)
                st.link(final8(8, cand_left))
                dve.tensor_tensor(wt[p][:, :, :], fin[:, :, :], fin[:, :, 0:1].broadcast_to([P, HEADS, TOPK]),
                                  ALU.subtract).then_inc(s_wexp, 1)
                dve.tensor_copy(place[:, :, :], fin_at[:, :, :])
                dve.tensor_copy(at0_steps[:, :, 0:1], at_f[:, 0:HEADS, 0:1])
                st.link(dve.tensor_tensor(at0_steps[:, :, 1:TOPK], at_f[:, 0:HEADS, 1:TOPK],
                                          at_f[:, 0:HEADS, 0:TOPK - 1], ALU.subtract))
                full = [P, HEADS, TOPK, TOPK]
                flat = [P, HEADS * TOPK, TOPK]
                place_b = place[:, :, :].rearrange("p h r -> p (h r)")[:, :, None].broadcast_to(flat)
                hot_f = hot[:, :, :, :].rearrange("p h r a -> p (h r) a")
                hotv_f = hotv[:, :, :, :].rearrange("p h r a -> p (h r) a")
                st.link(dve.tensor_tensor(hot_f, place_b, starts[:, None, :].broadcast_to(flat), ALU.is_ge))
                st.link(dve.tensor_tensor(hotv[:, :, :, :], hot[:, :, :, :],
                                          at0_steps[:, :, None, :].broadcast_to(full), ALU.mult))
                st.link(dve.tensor_reduce(key0[:, :, :], hotv[:, :, :, :], AX, ALU.add))
                st.link(dve.tensor_tensor(hotv_f, hot_f, start_steps[:, None, :].broadcast_to(flat), ALU.mult))
                st.link(dve.tensor_reduce(off[:, :, :], hotv[:, :, :, :], AX, ALU.add))
                st.link(dve.tensor_tensor(rank1[:, :, :], place[:, :, :], off[:, :, :], ALU.subtract))
                rank_b = rank1[:, :, :].rearrange("p h r -> p (h r)")[:, :, None].broadcast_to(flat)
                st.link(dve.tensor_tensor(hot_f, rank_b, count16[:, None, :].broadcast_to(flat), ALU.is_equal))
                st.link(dve.tensor_tensor(hotv[:, :, :, :], hot[:, :, :, :],
                                          at_f[:, HEADS:2 * HEADS, None, :].broadcast_to(full), ALU.mult))
                st.link(dve.tensor_reduce(key1[:, :, :], hotv[:, :, :, :], AX, ALU.add))
                st.link(dve.scalar_tensor_tensor(out=key0[:, :, :], in0=key1[:, :, :], scalar=float(NUM_KEYS),
                                                 in1=key0[:, :, :], op0=ALU.mult, op1=ALU.add))
                dve.tensor_tensor(idx[p][:, :].rearrange("p (h r) -> p h r", h=HEADS), key0[:, :, :],
                                  head_base[:, :, None].broadcast_to([P, HEADS, TOPK]), ALU.add).then_inc(s_idx, 1)
                dve.wait_ge(s_wexpd, t + 1)
                st.link(dve.tensor_reduce(wsum[:, :], wt[p][:, :, :], AX, ALU.add))
                st.link(dve.reciprocal(wsum[:, :], wsum[:, :]))
                st.link(dve.tensor_tensor(wt[p][:, :, :], wt[p][:, :, :],
                                          wsum[:, :, None].broadcast_to([P, HEADS, TOPK]), ALU.mult))
                st.close()

            FRONT_STEPS, TOPK_STEPS = 55, 22

            def maxima(c, t):
                for h in (2 * c, 2 * c + 1):
                    n = HEADS * t + h + 1
                    dve.wait_ge(s_sc, n)
                    dve.tensor_reduce(nmax[:, h:h + 1], score_ps[h % 2][:, :], AX, ALU.max).then_inc(s_nms, 1)
                    dve.wait_ge(s_nms, n)
                    dve.tensor_scalar(nmax[:, h:h + 1], nmax[:, h:h + 1], -1.0, None, ALU.mult).then_inc(s_nm, 1)

            def normalise(c, t, p):
                for h in (2 * c, 2 * c + 1):
                    n = HEADS * t + h + 1
                    dve.wait_ge(s_o, n)
                    dve.reciprocal(rrec[:, h:h + 1], rsum[:, h:h + 1]).then_inc(s_os, 1)
                    dve.wait_ge(s_os, n)
                    if h == 0:
                        wait(dve, s_att_t, t if not isinstance(t, int) or t > 1 else 0)
                    dve.tensor_scalar(att[p][:, h * D:(h + 1) * D], score_ps[h % 2][:, 0:D], rrec[:, h:h + 1], None,
                                      ALU.mult).then_inc(s_att, 1)

            def heads_slot(s, t, p):
                if s < HEADS:
                    dve.wait_ge(s_got[s], 16 * TOPK * (t + 1))
                    dve.tensor_tensor(got[:, s % RING, :, :], got[:, s % RING, :, :],
                                      wt[p][:, s, :, None].broadcast_to([P, TOPK, 2 * D]), ALU.mult
                                      ).then_inc(s_gw, 1)
                if s >= 2 and s % 2 == 0:
                    maxima(s // 2 - 1, t)
                if s >= 3 and s % 2 == 1:
                    normalise((s - 3) // 2, t, p)

            def tail_slot(seg, t, p):
                s = lay[1]
                if seg == 0:
                    st = Steps(dve, s_ts, t, TAIL_STEPS)
                    tail_slot.st = st
                    dve.wait_ge(s_wo, t + 1)
                    st.link(dve.tensor_tensor(x2[:, :], h_pt, x1[:, bass.ds((t & 3) * D, D)], ALU.add))
                    layer_norm(st, x2[:, :], xn_t[:, 0:D], stat_t, mv_t, root_t, 2 * t + 1).then_inc(s_xnt, 1)
                    dve.wait_ge(s.gated, t + 1)
                    st.link(dve.tensor_scalar(s.gates[:, 0, :], s.gates[:, 0, :], 1.0, None, ALU.add))
                    st.link(dve.reciprocal(s.gates[:, 0, :], s.gates[:, 0, :]))
                    dve.tensor_tensor(s.gates[:, 1, :], s.gates[:, 2, :], s.q2[0:D, :], ALU.mult
                                      ).then_inc(s.gates_ready, 1)
                    st.link(dve.tensor_tensor(s.ik[:, :], s.gates[:, 2, :], s.k2[0:D, :], ALU.mult))
                    normaliser(s, t, st)
                    carry_state(s, t, st)
                if seg == 1:
                    recur(s, range(0, GROUPS // 2), t, tail_slot.st)
                if seg == 2:
                    st = tail_slot.st
                    recur(s, range(GROUPS // 2, GROUPS), t, st)
                    dve.wait_ge(s.hraw, t + 1)
                    magnitude(s, st, den_pt, 1.0)
                    st.link(dve.reciprocal(s.dr[:, :], s.den[:, :]))
                    dve.tensor_scalar(h_pad[:, 0:D].rearrange("p (a i) -> p a i", a=2),
                                      h_pt.rearrange("p (i a) -> p a i", a=2), s.dr[:, 0:1], None, ALU.mult
                                      ).then_inc(s_h1, 1)
                    dve.wait_ge(s_wo1, t + 1)
                    st.link(dve.tensor_tensor(x3[:, :], h_pt, x2[:, :], ALU.add))
                    layer_norm(st, x3[:, :], xn_t[:, 0:D], stat_t, mv_t, root_t, 2 * t + 2).then_inc(s_xnt, 1)
                if seg == 3:
                    st = tail_slot.st
                    dve.wait_ge(s_xnt, 2 * (t + 1))
                    st.link(dve.tensor_tensor(res[:, :], x3[:, :], xn_t[:, 0:D], ALU.add))
                    dve.wait_ge(s_up, t + 1)
                    st.link(dve.tensor_reduce(lmax[:, :], logit_ps, AX, ALU.max))
                    dve.tensor_scalar(lmax[:, :], lmax[:, :], -1.0, None, ALU.mult).then_inc(s_lm, 1)
                    dve.wait_ge(s_le, t + 1)
                    st.link(dve.reciprocal(prob_scale[:, :], esum[:, :]))
                    st.link(dve.tensor_scalar(probs[:, :], exps[:, :], prob_scale[:, 0:1], None, ALU.mult))
                    own_wait()
                    st.link(dve.max(top8[:, :], probs[:, :]))
                    own_wait()
                    dve.max_index(top_at[:, :], top8[:, :], probs[:, :])
                    st.link(dve.tensor_tensor(two[:, :], top8[:, 0:1], top8[:, 1:2], ALU.add))
                    dve.tensor_copy(top_f[:, :], top_at[:, :])
                    st.link(dve.tensor_scalar(two[:, :], two[:, :], 1e-12, None, ALU.max))
                    st.link(dve.tensor_scalar(chosen[:, :], count8[:, :], top_f[:, 0:1], None, ALU.is_equal))
                    dve.reciprocal(two_rec[:, :], two[:, :])
                    st.link(dve.scalar_tensor_tensor(out=chosen[:, :], in0=count8[:, :], scalar=top_f[:, 1:2],
                                                     in1=chosen[:, :], op0=ALU.is_equal, op1=ALU.add))
                    dve.scalar_tensor_tensor(out=combine[:, :], in0=probs[:, :], scalar=two_rec[:, 0:1],
                                             in1=chosen[:, :], op0=ALU.mult, op1=ALU.mult).then_inc(s_cmb, 1)
                    dve.wait_ge(s_cmb, t + 1)
                    dve.wait_ge(s_gelu, t + 1)
                    dve.tensor_tensor(hid[:, :, :], hid[:, :, :], combine[:, :, None].broadcast_to([P, EXPERTS, D]),
                                      ALU.mult).then_inc(s_hid, 1)
                    dve.wait_ge(s_y, t + 1)
                    wait(dve, s_out, 16 * t)
                    dve.tensor_tensor(y_out[:, :], res[:, :], h_pt, ALU.add).then_inc(s_yout, 1)
                    st.close()

            TAIL_STEPS = 51
            tile_loop(dve, lambda t: None, heads_slot, front_slot, tail_slot)

        @block.scalar
        def _(act):
            act.wait_ge(s_const_dve, 2)
            act.copy(att_t[:, 0, 0:1], half_sel[:, 0:1]).then_inc(s_att_t, 1)
            act.copy(hid_t[:, 0, 0:1], half_sel[:, 0:1]).then_inc(s_hidt, 1)

            def guess_root(r, done):
                act.wait_ge(r.asked, done)
                act.activation(r.l[:, :], r.v[:, :], ACT.Ln).then_inc(r.logged, 1)
                act.wait_ge(r.logged, done)
                act.activation(r.g[:, :], r.l[:, :], ACT.Exp, scale=-0.5).then_inc(r.guess, 1)

            def front_slot(seg, t, p):
                s = lay[0]
                if seg == 0:
                    guess_root(root_f, 3 * t + 1)
                    act.wait_ge(s_xtps, 2 * t + 1)
                    wait(act, s.proj, t)
                    act.copy(xt0[0:D, :], xt_ps[0:D, :]).then_inc(s_xt, 1)
                    act.wait_ge(s.proj, t + 1)
                    i_ps, f_ps = wide[1][0:D, P:2 * P], wide[1][0:D, 2 * P:3 * P]
                    wait(act, s.yq_ready, QUARTERS * t)
                    act.activation(absf[:, :], f_ps, ACT.Abs).then_inc(s_act0, 1)
                    act.activation(soft_in[:, :], i_ps, ACT.Exp, bias=ib5_sb[:, 0:1], scale=0.2)
                    act.wait_ge(s_act0, 2 * t + 1)
                    act.activation(expf[:, :], absf[:, :], ACT.Exp, scale=-1.0).then_inc(s_act0, 1)
                    act.activation(s.k2[:, :], wide[0][:, 0:P], ACT.Copy, scale=D ** -0.5)
                    act.wait_ge(s_act0, 2 * t + 2)
                    act.activation(lnf[:, :], expf[:, :], ACT.Ln, bias=1.0)
                    act.copy(s.q2[:, :], wide[0][:, P:2 * P])
                    act.activation(osig[:, :], wide[0][:, 2 * P:2 * P + D], ACT.Exp, scale=-1.0).then_inc(s.gated, 1)
                    act.wait_ge(s_fe, t + 1)
                    act.activation(s.gates[:, 0:3:2, :], fe[:, :, :], ACT.Exp).then_inc(s_fi, 1)
                if seg == 2:
                    guess_root(root_f, 3 * t + 2)
                    guess_root(root_f, 3 * t + 3)
                    act.wait_ge(s_xtps, 2 * t + 2)
                    wait(act, s_q, t)
                    act.copy(xt2[:, :], xt_ps[0:D, :]).then_inc(s_xt, 1)
                    act.wait_ge(s_qpkps, t + 1)
                    act.copy(qpk[:, :, :].rearrange("p c n -> p (c n)"), wide[0][:, :]).then_inc(s_qpk, 1)
                    wait(act, s_top, t)
                    for c in range(2):
                        act.wait_ge(s_simps, 2 * t + c + 1)
                        act.copy(sims[:, HEADS * c:HEADS * (c + 1), :].rearrange("p h k -> p (h k)"),
                                 wide[c][:, :]).then_inc(s_sim, 1)
                if seg == 3:
                    act.wait_ge(s_wexp, t + 1)
                    act.activation(wt[p][:, :, :], wt[p][:, :, :], ACT.Exp).then_inc(s_wexpd, 1)

            def heads_open(t):
                act.wait_ge(s_q, t + 1)
                wait(act, s_sc, HEADS * t)
                act.activation(qs[:, :, :].rearrange("p c n -> p (c n)"), wide[0][:, :], ACT.Copy,
                               scale=D ** -0.5).then_inc(s_qs, 1)

            def heads_slot(s, t, p):
                j = t & (ROW_TILES - 1)
                if s < HEADS:
                    h, n = s, HEADS * t + s + 1
                    act.wait_ge(s_kv, n)
                    if h % 2 == 0:
                        wait(act, s_ktps, PAIRS * t + h // 2)
                    o = P * (h % 2)
                    act.copy(ktmp[:, (h % 2) * D:(h % 2 + 1) * D], head_ps[:, o:o + D]).then_inc(s_kvc, 1)
                    if not isinstance(t, int) or t > 0:
                        act.wait_ge(s_o, n - HEADS)
                    act.copy(vc[:, bass.ds(j * (HEADS * D) + h * D, D)], head_ps[:, o + D:o + 2 * D]).then_inc(s_kvc, 1)
                    if h % 2 == 1:
                        c = h // 2
                        act.wait_ge(s_ktps, PAIRS * t + c + 1)
                        if not isinstance(t, int) or t > 0:
                            act.wait_ge(s_sc, n - HEADS)
                        act.copy(kt[:, c, bass.ds(j * P, P)], kt_ps).then_inc(s_kt, 1)
                if s >= 2 and s % 2 == 0:
                    for h in (s - 2, s - 1):
                        n = HEADS * t + h + 1
                        act.wait_ge(s_nm, n)
                        act.activation(pr[h % 2][:, :], score_ps[h % 2][:, :], ACT.Exp, bias=nmax[:, h:h + 1],
                                       accum_out=rsum[:, h:h + 1]).then_inc(s_p, 1)
                    for h in (s - 2, s - 1):
                        n = HEADS * t + h + 1
                        act.wait_ge(s_pps, n)
                        wait(act, s_o, n - 2)
                        act.copy(prt[h % 2][:, :, :].rearrange("p k n -> p (k n)"), score_ps[h % 2][:, :]
                                 ).then_inc(s_pt, 1)

            def tail_slot(seg, t, p):
                s = lay[1]
                if seg == 0:
                    act.wait_ge(s_atps, t + 1)
                    act.copy(att_t[:, :, :].rearrange("p c n -> p (c n)"), wide[0][:, :]).then_inc(s_att_t, 1)
                    guess_root(root_t, 2 * t + 1)
                    act.wait_ge(s_xtps_t, 3 * t + 1)
                    act.copy(xt3[0:D, :], xt_pt[0:D, :]).then_inc(s_xt_t, 1)
                    act.wait_ge(s.proj, t + 1)
                    act.activation(s.gates[:, 0, :], wide[1][0:D, P:2 * P], ACT.Exp, scale=-1.0)
                    act.activation(s.gates[:, 2, :], wide[1][0:D, 0:P], ACT.Exp)
                    act.copy(s.k2[:, :], wide[0][:, 0:P])
                    act.copy(s.q2[:, :], wide[0][:, P:2 * P]).then_inc(s.gated, 1)
                if seg == 2:
                    act.wait_ge(s_xtps_t, 3 * t + 2)
                    act.copy(ht[0:D, :], xt_pt[0:D, :]).then_inc(s_xt_t, 1)
                    guess_root(root_t, 2 * t + 2)
                    act.wait_ge(s_xtps_t, 3 * t + 3)
                    act.copy(xt4[0:D, :], xt_pt[0:D, :]).then_inc(s_xt_t, 1)
                if seg == 3:
                    act.wait_ge(s_lm, t + 1)
                    act.activation(exps[:, :], logit_ps, ACT.Exp, bias=lmax[:, 0:1], accum_out=esum[:, :]
                                   ).then_inc(s_le, 1)
                    act.activation(hid[:, :, :].rearrange("p e d -> p (e d)"), wide[0][:, :], ACT.Gelu
                                   ).then_inc(s_gelu, 1)
                    act.wait_ge(s_hps, t + 1)
                    act.copy(comb_t[:, :], xt_pt[0:EXPERTS, :])
                    act.copy(hid_t[:, :, :].rearrange("p c n -> p (c n)"), wide[1][:, :]).then_inc(s_hidt, 1)

            tile_loop(act, heads_open, heads_slot, front_slot, tail_slot)

        @block.tensor
        def _(pe):
            pe.wait_ge(s_w, N_LOADS)
            pe.wait_ge(s_const_pool, 2)
            pe.wait_ge(s_const_dve, 2)

            def spread(s, groups, t):
                for g in groups:
                    if g >= 2:
                        pe.wait_ge(s.scanned, GROUPS * t + g - 1)
                    for i in range(2):
                        last = pe.matmul(wide[g % 2][:, 2 * P * i:2 * P * (i + 1)],
                                         row_sel[:, 2 * g + i, :, :].rearrange("c a d -> c (a d)"),
                                         s.gates[:, 0:2, :].rearrange("c a n -> c (a n)"), start=True, stop=True)
                    last.then_inc(s.spread, 1)

            def read_out(s, quarters, t, h_out, den_out):
                for u in quarters:
                    pe.wait_ge(s.yq_ready, QUARTERS * t + u + 1)
                    for i in range(8 * u, 8 * u + 8):
                        last = pe.matmul(h_out[:, 2 * i:2 * i + 2], s.y[:, i, :], half_sel[:, :], start=True, stop=True)
                if QUARTERS - 1 in quarters:
                    pe.wait_ge(s.nq_ready, t + 1)
                    pe.matmul(den_out, s.nq[:, :], ones_col[:, :], start=True, stop=True).then_inc(s.hraw, 1)

            def front_slot(seg, t, p):
                s = lay[0]
                if seg == 0:
                    pe.wait_ge(s_xn, 2 * t + 1)
                    wait(pe, s_yout, t - 1)
                    pe.transpose(xt_ps, xn_f[:, :], ident[:, :]).then_inc(s_xtps, 1)
                    pe.wait_ge(s_xt, 2 * t + 1)
                    wait(pe, s_qs, t)
                    wait(pe, s_sim, 2 * t)
                    for dst, c in ((wide[0][:, 0:P], 0), (wide[0][:, P:2 * P], P)):
                        pe.matmul(dst, w0_sb[:, c:c + P], xt0[:, :], start=True, stop=True)
                    pe.matmul(wide[0][:, 2 * P:2 * P + D], xt0[:, :], w0_sb[:, 2 * P:2 * P + D], start=True, stop=True)
                    for n in range(3):
                        last = pe.matmul(wide[1][0:D, n * P:(n + 1) * P],
                                         w0_sb[:, 2 * P + D * (n + 1):2 * P + D * (n + 2)], xt0[:, :],
                                         start=True, stop=True)
                    last.then_inc(s.proj, 1)
                if seg == 1:
                    pe.wait_ge(s.gates_ready, t + 1)
                    spread(s, range(0, GROUPS // 2), t)
                    read_out(s, [0], t, h_ps, den_ps)
                if seg == 2:
                    spread(s, range(GROUPS // 2, GROUPS), t)
                    read_out(s, [1, 2, 3], t, h_ps, den_ps)
                    pe.wait_ge(s_xn, 2 * t + 2)
                    pe.transpose(xt_ps, xn_f[:, :], ident[:, :]).then_inc(s_xtps, 1)
                    pe.wait_ge(s_xt, 2 * t + 2)
                    pe.wait_ge(s.scanned, GROUPS * (t + 1))
                    for c in range(4):
                        last = pe.matmul(wide[0][:, c * P:(c + 1) * P], wqpk_sb[:, c * P:(c + 1) * P], xt2[:, :],
                                         start=True, stop=True)
                    last.then_inc(s_qpkps, 1)
                    pe.wait_ge(s_qpk, t + 1)
                    for c in range(4):
                        last = pe.matmul(wide[c // 2][:, 256 * (c % 2):256 * (c % 2 + 1)], qpk[:, c, :],
                                         pkk_sb[:, c, :], start=True, stop=True)
                        if c % 2:
                            last.then_inc(s_simps, 1)

            def heads_open(t):
                pe.wait_ge(s_sim, 2 * (t + 1))
                wait(pe, s_hidt, t if not isinstance(t, int) or t > 1 else 0)
                for c in range(PAIRS):
                    last = pe.matmul(wide[0][:, c * P:(c + 1) * P], wq_sb[:, c * P:(c + 1) * P], xt2[:, :],
                                     start=True, stop=True)
                last.then_inc(s_q, 1)

            def heads_slot(s, t, p):
                j = t & (ROW_TILES - 1)
                if s < HEADS:
                    h, n = s, HEADS * t + s + 1
                    pe.wait_ge(s_gw, n)
                    if h % 2 == 0:
                        wait(pe, s_kt, PAIRS * t + h // 2)
                    else:
                        pe.wait_ge(s_kvc, 2 * (n - 1))
                    for r in range(TOPK):
                        last = pe.matmul(head_ps[:, P * (h % 2):P * (h % 2 + 1)], ident[:, :], got[:, h % RING, r, :],
                                         start=(r == 0), stop=(r == TOPK - 1))
                    last.then_inc(s_kv, 1)
                    if h % 2 == 1:
                        c = h // 2
                        pe.wait_ge(s_kvc, 2 * n)
                        pe.transpose(kt_ps, ktmp[:, :], ident[:, :]).then_inc(s_ktps, 1)
                        pe.wait_ge(s_kt, PAIRS * t + c + 1)
                        pe.wait_ge(s_qs, t + 1)
                        for hh in (h - 1, h):
                            part = slice(D * (hh % 2), D * (hh % 2 + 1))
                            wait(pe, s_att, HEADS * t + hh - 1)
                            for b in range(2):
                                dst = score_ps[hh % 2][:, 512 * b:512 * (b + 1)]
                                pe.matmul(dst, ident_b[:, :], causal[:, bass.ds(SEQ - P + 512 * b - P * j, 512)],
                                          start=True, stop=False)
                                last = pe.matmul(dst, qs[part, c, :], kt[part, c, 512 * b:512 * (b + 1)],
                                                 start=False, stop=True)
                            last.then_inc(s_sc, 1)
                if s >= 2 and s % 2 == 0:
                    for h in (s - 2, s - 1):
                        n = HEADS * t + h + 1
                        pe.wait_ge(s_p, n)
                        for k in range(ROW_TILES):
                            last = pe.transpose(score_ps[h % 2][:, k * P:(k + 1) * P],
                                                pr[h % 2][:, k * P:(k + 1) * P], ident[:, :])
                        last.then_inc(s_pps, 1)
                    for h in (s - 2, s - 1):
                        n = HEADS * t + h + 1
                        pe.wait_ge(s_pt, n)
                        pe.wait_ge(s_kvc, 2 * n)
                        for k in range(ROW_TILES):
                            v = k * HEADS * D + h * D
                            last = pe.matmul(score_ps[h % 2][:, 0:D], prt[h % 2][:, k, :], vc[:, v:v + D],
                                             start=(k == 0), stop=(k == ROW_TILES - 1))
                        last.then_inc(s_o, 1)

            def tail_slot(seg, t, p):
                s = lay[1]
                if seg == 0:
                    pe.wait_ge(s_att, HEADS * (t + 1))
                    last_front = min(t + 3, TILES) if isinstance(t, int) else t + 3
                    pe.wait_ge(s_sim, 2 * last_front)
                    pe.wait_ge(s_qs, min(t + 2, TILES) if isinstance(t, int) else t + 2)
                    for c in range(PAIRS):
                        last = pe.transpose(wide[0][:, c * P:(c + 1) * P], att[p][:, c * P:(c + 1) * P], ident[:, :])
                    last.then_inc(s_atps, 1)
                    pe.wait_ge(s_att_t, t + 2)
                    pe.wait_ge(s_xt, 2 * last_front)
                    for c in range(PAIRS):
                        last = pe.matmul(h_pt, att_t[:, c, :], wo_sb[:, c, :], start=(c == 0), stop=(c == PAIRS - 1))
                    last.then_inc(s_wo, 1)
                    pe.wait_ge(s_xnt, 2 * t + 1)
                    wait(pe, s_hidt, t + 1)
                    pe.transpose(xt_pt, xn_t[:, :], ident[:, :]).then_inc(s_xtps_t, 1)
                    pe.wait_ge(s_xt_t, 3 * t + 1)
                    for n in range(2):
                        pe.matmul(wide[0][:, n * P:(n + 1) * P], w1_sb[:, n * P:(n + 1) * P], xt3[:, :],
                                  start=True, stop=True)
                    for n in range(2):
                        last = pe.matmul(wide[1][0:D, n * P:(n + 1) * P],
                                         w1_sb[:, 2 * P + D * n:2 * P + D * (n + 1)], xt3[:, :], start=True, stop=True)
                    last.then_inc(s.proj, 1)
                if seg == 1:
                    pe.wait_ge(s.gates_ready, t + 1)
                    spread(s, range(0, GROUPS // 2), t)
                    read_out(s, [0], t, h_pt, den_pt)
                if seg == 2:
                    spread(s, range(GROUPS // 2, GROUPS), t)
                    read_out(s, [1, 2, 3], t, h_pt, den_pt)
                    pe.wait_ge(s_h1, t + 1)
                    pe.transpose(xt_pt, h_pad[:, :], ident[:, :]).then_inc(s_xtps_t, 1)
                    pe.wait_ge(s_xt_t, 3 * t + 2)
                    pe.matmul(h_pt, ht[:, :], wo1_sb[:, :], start=True, stop=True).then_inc(s_wo1, 1)
                    pe.wait_ge(s_xnt, 2 * t + 2)
                    pe.transpose(xt_pt, xn_t[:, :], ident[:, :]).then_inc(s_xtps_t, 1)
                if seg == 3:
                    pe.wait_ge(s_xt_t, 3 * t + 3)
                    pe.wait_ge(s.scanned, GROUPS * (t + 1))
                    pe.matmul(logit_ps, xt4[0:D, :], router_sb[:, :], start=True, stop=True)
                    pe.matmul(wide[0][:, :], xt4[:, :], up_sb[:, :], start=True, stop=True).then_inc(s_up, 1)
                    pe.wait_ge(s_cmb, t + 1)
                    pe.transpose(xt_pt[0:EXPERTS, :], combine[:, :], ident[:, :])
                    pe.wait_ge(s_hid, t + 1)
                    for c in range(4):
                        last = pe.transpose(wide[1][:, c * P:(c + 1) * P],
                                            hid[:, 2 * c:2 * c + 2, :].rearrange("p e d -> p (e d)"), ident[:, :])
                    last.then_inc(s_hps, 1)
                    pe.wait_ge(s_hidt, t + 2)
                    for c in range(4):
                        pe.matmul(h_pt, hid_t[:, c, :], down_sb[:, c, :], start=(c == 0), stop=False)
                    pe.matmul(h_pt, comb_t[:, :], db_sb[:, :], start=False, stop=True).then_inc(s_y, 1)

            tile_loop(pe, heads_open, heads_slot, front_slot, tail_slot)


def kernel(**a):
    import numpy as np
    import concourse.bacc as bacc
    from concourse.bass_utils import run_bass_kernel_spmd

    a = {k: np.asarray(v) for k, v in a.items()}
    row = lambda w, b: np.concatenate([w, b[None, :]], axis=0)

    def ids(v):
        return np.ascontiguousarray(v.reshape(TILES, P).T)

    k0, q0 = (row(a[f"L0_attn_W{n}"], a[f"L0_attn_b{n}"]) for n in "kq")
    v0, g0 = row(a["L0_attn_Wv"], a["L0_attn_bv"]), row(a["L0_attn_Wg"], a["L0_attn_bg"])
    k1, q1, i1, f1 = (row(a[f"L1_attn_W{n}"].T, a[f"L1_attn_b{n}"]) for n in "kqif")
    feeds = {
        "x_ids": ids(a["x"]), "itok_ids": ids(a["itok_BS_0_99998"]), "tok_w": a["L0_tok_weight"],
        "w0": np.concatenate([k0, k0, q0, q0, g0[:, 2 * D:], v0, g0[:, :2 * D]], axis=1),
        "input_bias": a["L0_attn_input_bias"].reshape(D, 1), "norm_scale": a["L0_attn_norm_scale"].reshape(1, D),
        "wqpk": a["L0_ffn_Wq_pk"],
        "pk_keys": a["L0_ffn_pk_keys"].transpose(0, 2, 3, 1).reshape(2 * HEADS, DIM_KEY, NUM_KEYS),
        "wq": a["L0_ffn_Wq"],
        "kv_table": np.concatenate([a["L0_ffn_keys_table"], a["L0_ffn_values_table"]], axis=1),
        "wo": a["L0_ffn_Wo"],
        "w1": np.concatenate([k1, k1, q1, q1, i1, f1], axis=1),
        "wo1": row(a["L1_attn_Wo"].T, a["L1_attn_bo"]),
        "router": a["L1_ffn_router_w"].T,
        "up": row(a["L1_ffn_w1"].transpose(1, 0, 2).reshape(D, EXPERTS * D), a["L1_ffn_b1"].reshape(-1)),
        "down": a["L1_ffn_w2"].reshape(EXPERTS * D, D), "down_bias": a["L1_ffn_b2"],
    }
    nc = bacc.Bacc("TRN2", target_bir_lowering=False, num_devices=1)
    arrays, args = {}, []
    for name, v in feeds.items():
        v = np.ascontiguousarray(v)
        arrays[name] = v
        args.append(nc.dram_tensor(name, v.shape, mybir.dt.from_np(v.dtype), kind="ExternalInput").ap())
    out = nc.dram_tensor("out", (BATCH * SEQ, D), F32, kind="ExternalOutput").ap()
    tower(nc, *args, out)
    r = run_bass_kernel_spmd(nc, [arrays], core_ids=[0])
    return r.results[0]["out"].reshape(BATCH, SEQ, D)
```

```python
from contextlib import ExitStack

import concourse.bass as bass
from concourse import mybir
from concourse.alu_op_type import AluOpType as ALU

F32 = mybir.dt.float32
BF16 = mybir.dt.bfloat16
I32 = mybir.dt.int32
U32 = mybir.dt.uint32
ACT = mybir.ActivationFunctionType
AX = mybir.AxisListType.X

P = 128
D = 64
BATCH, SEQ = 8, 1024
TILES = BATCH * SEQ // P
ROW_TILES = SEQ // P
HEADS = 8
PAIRS = HEADS // 2
TOPK = 16
NUM_KEYS = 64
DIM_KEY = 32
EXPERTS = 8
HALF = D // 2
GROUPS = HALF // 2
QUARTERS = 4
TICKS = 32
HEAD_TICKS = TICKS // HEADS
TAIL_AT = 8
ATTEND = 8
RING = 4
EPS = 1e-5
LOWEST = -3.0e38
MASKED = -1.0e30
LOTS = [(0, 1, 16), (1, 1, 8), (2, 2, 5), (4, 4, 3), (8, 8, 1)]
STARTS = [0]
for _a0, _na, _nb in LOTS:
    for _ in range(_na):
        STARTS.append(STARTS[-1] + _nb)
CANDS = STARTS.pop()


def wait(eng, sem, value):
    if not isinstance(value, int) or value > 0:
        eng.wait_ge(sem, value)


class Parts:
    pass


class Steps:

    def __init__(self, eng, sem, done, total):
        self.eng, self.sem, self.done, self.total, self.n = eng, sem, done, total, 0

    def link(self, ins):
        self.n += 1
        ins.then_inc(self.sem, 1)
        self.eng.wait_ge(self.sem, self.done * self.total + self.n)

    def close(self):
        assert self.n == self.total, (self.n, self.total)


def tower(nc, x_ids, itok_ids, tok_w, w0, input_bias, norm_scale, wqpk, pk_keys, wq, kv_table, wo, w1, wo1,
          router, up, down, down_bias, out):
    V = tok_w.shape[0]
    ctx = ExitStack()
    with ctx:
        def sb(name, shape, dt=F32):
            return ctx.enter_context(nc.sbuf_tensor(name, shape, dt))

        def ps(name, shape, dt=F32):
            return ctx.enter_context(nc.psum_tensor(name, shape, dt))

        def sem(name):
            return ctx.enter_context(nc.semaphore(name))

        ident = sb("ident", [P, P])
        ident_b = sb("ident_b", [P, P], BF16)
        causal = sb("causal", [P, 2 * SEQ - P], BF16)
        row_sel = sb("row_sel", [D, HALF, 2, D])
        half_sel = sb("half_sel", [P, 2])
        ones_col = sb("ones_col", [D, 1])
        keep = sb("keep", [P, TILES])
        starts = sb("starts", [P, TOPK], BF16)
        start_steps = sb("start_steps", [P, TOPK], BF16)
        count16 = sb("count16", [P, TOPK], BF16)
        count8 = sb("count8", [P, EXPERTS])
        head_base = sb("head_base", [P, HEADS])
        w0_sb = sb("w0_sb", [D + 1, 8 * D])
        ib_sb = sb("ib_sb", [D, 1])
        ib5_sb = sb("ib5_sb", [D, 1])
        ns_sb = sb("ns_sb", [P, D])
        wqpk_sb = sb("wqpk_sb", [D, 512])
        pkk_sb = sb("pkk_sb", [P, 4, 4 * NUM_KEYS])
        wq_sb = sb("wq_sb", [D, HEADS * D])
        wo_sb = sb("wo_sb", [P, PAIRS, D])
        w1_sb = sb("w1_sb", [D + 1, 6 * D])
        wo1_sb = sb("wo1_sb", [D + 1, D])
        router_sb = sb("router_sb", [D, EXPERTS])
        up_sb = sb("up_sb", [D + 1, EXPERTS * D])
        down_sb = sb("down_sb", [P, 4, D])
        db_sb = sb("db_sb", [EXPERTS, D])
        ids = sb("ids", [P, 2, TILES], I32)
        idf = sb("idf", [P, 2, TILES])
        neg = sb("neg", [P, 2, TILES])
        differ = sb("differ", [P, TILES])
        rows = sb("rows", [P, 2, TILES + 1], I32)
        tok_idx = sb("tok_idx", [P, 2], I32)
        emb = sb("emb", [P, 2, D])
        x0, h0 = sb("x0", [P, D]), sb("h0", [P, D])
        x1 = sb("x1", [P, 4 * D])
        stat_f, mv_f = sb("stat_f", [P, 6]), sb("mv_f", [P, 2])
        xn_f = sb("xn_f", [P, 2 * D])
        xt0 = sb("xt0", [D + 1, P])
        xt2 = sb("xt2", [D, P])
        soft_in = sb("soft_in", [D, P])
        absf, expf, lnf = sb("absf", [D, P]), sb("expf", [D, P]), sb("lnf", [D, P])
        li, lf = sb("li", [D, P]), sb("lf", [D, P])
        mx = sb("mx", [D, P + 1])
        fe = sb("fe", [D, 2, P])
        osig = sb("osig", [P, D])
        qpk = sb("qpk", [P, 4, P])
        sims = sb("sims", [P, 2 * HEADS, NUM_KEYS])
        sims_left = sb("sims_left", [P, 2 * HEADS, NUM_KEYS])
        best = sb("best", [P, 2 * HEADS, TOPK])
        best_at = sb("best_at", [P, 2 * HEADS, TOPK], U32)
        at_f = sb("at_f", [P, 2 * HEADS, TOPK], BF16)
        at0_steps = sb("at0_steps", [P, HEADS, TOPK], BF16)
        cand = sb("cand", [P, HEADS, CANDS])
        cand_left = sb("cand_left", [P, HEADS, CANDS])
        fin = sb("fin", [P, HEADS, TOPK])
        fin_at = sb("fin_at", [P, HEADS, TOPK], U32)
        place = sb("place", [P, HEADS, TOPK], BF16)
        hot = sb("hot", [P, HEADS, TOPK, TOPK], BF16)
        hotv = sb("hotv", [P, HEADS, TOPK, TOPK], BF16)
        key0 = sb("key0", [P, HEADS, TOPK])
        off = sb("off", [P, HEADS, TOPK])
        rank1 = sb("rank1", [P, HEADS, TOPK], BF16)
        key1 = sb("key1", [P, HEADS, TOPK])
        wsum = sb("wsum", [P, HEADS])
        idx = [sb(f"idx{p}", [P, HEADS * TOPK], I32) for p in range(2)]
        wt = [sb(f"wt{p}", [P, HEADS, TOPK]) for p in range(2)]
        qs = [sb(f"qs{p}", [P, PAIRS, P]) for p in range(2)]
        got = sb("got", [P, RING, TOPK, 2 * D])
        ktmp = sb("ktmp", [P, 2 * D])
        kt = sb("kt", [P, PAIRS, SEQ])
        vc = sb("vc", [P, ROW_TILES * HEADS * D])
        nmax = sb("nmax", [P, HEADS])
        rsum = sb("rsum", [P, HEADS])
        rrec = sb("rrec", [P, HEADS])
        pr = sb("pr", [P, SEQ])
        prt = sb("prt", [P, ROW_TILES, P])
        att = sb("att", [P, HEADS * D])
        att_t = sb("att_t", [P, PAIRS, P])
        x2, x3 = sb("x2", [P, D]), sb("x3", [P, D])
        stat_t, mv_t = sb("stat_t", [P, 6]), sb("mv_t", [P, 2])
        xn_t, h_pad = sb("xn_t", [P, 2 * D]), sb("h_pad", [P, 2 * D])
        xt3 = sb("xt3", [D + 1, P])
        ht = sb("ht", [D + 1, P])
        xt4 = sb("xt4", [D + 1, P])
        lmax, esum, prob_scale = sb("lmax", [P, 1]), sb("esum", [P, 1]), sb("prob_scale", [P, 1])
        exps, probs, top8 = sb("exps", [P, EXPERTS]), sb("probs", [P, EXPERTS]), sb("top8", [P, 8])
        top_at, top_f = sb("top_at", [P, 8], U32), sb("top_f", [P, 8])
        two, two_rec = sb("two", [P, 1]), sb("two_rec", [P, 1])
        chosen, combine = sb("chosen", [P, EXPERTS]), sb("combine", [P, EXPERTS])
        hid = sb("hid", [P, EXPERTS, D])
        hid_t = sb("hid_t", [P, 4, P])
        comb_t = sb("comb_t", [EXPERTS, P])
        res = sb("res", [P, D])
        y_out = sb("y_out", [P, D])

        score_ps = ps("score_ps", [P, SEQ])
        head_ps = [ps(f"head_ps{s}", [P, 512]) for s in range(2)]
        wide_f = [ps(f"wide_f{s}", [P, 512]) for s in range(2)]
        wide_t = [ps(f"wide_t{s}", [P, 512]) for s in range(2)]
        logit_ps = wide_t[1][:, 256:256 + EXPERTS]

        weighed, states = sb("weighed", [P, 2, 2, P]), sb("states", [P, HALF, P])
        den, den_rec = sb("den", [P, 1]), sb("den_rec", [P, 1])

        def layer(n):
            s = Parts()
            s.wide = (wide_f, wide_t)[n]
            s.k2, s.q2 = sb(f"k2_{n}", [P, P]), sb(f"q2_{n}", [P, P])
            s.gates = sb(f"gates{n}", [D, 3, P])
            s.ik = sb(f"ik{n}", [D, P])
            s.nst, s.nq = sb(f"nst{n}", [D, P + 1]), sb(f"nq{n}", [D, P])
            s.mc, s.mc0 = sb(f"mc{n}", [P, HALF]), sb(f"mc0_{n}", [P, HALF])
            s.w, s.y, s.den, s.dr = weighed, states, den, den_rec
            s.proj, s.gated = sem(f"proj_ps{n}"), sem(f"gates_begun{n}")
            s.gates_ready, s.nq_ready = sem(f"gates_ready{n}"), sem(f"nq_ready{n}")
            s.spread, s.scanned = sem(f"spread_ps{n}"), sem(f"scanned{n}")
            s.yq_ready, s.hraw = sem(f"yq_ready{n}"), sem(f"read_out_ps{n}")
            return s

        lay = [layer(0), layer(1)]
        ss, sq = sb("ss", [P, 1]), sb("sq", [P, D])

        def root(n):
            s = Parts()
            s.v, s.l, s.g, s.a, s.y = (sb(f"root_{what}{n}", [P, 1]) for what in "vlgay")
            s.asked, s.logged, s.guess = sem(f"root_asked{n}"), sem(f"root_log{n}"), sem(f"root_guess{n}")
            return s

        root_f, root_t = root(0), root(1)

        s_w = sem("weights_in")
        s_ids = sem("ids_in")
        s_const_pool = sem("const_pool")
        s_const_dve = sem("const_dve")
        s_turn_dve, s_turn_pool = sem("turn_dve"), sem("turn_pool")
        s_start = sem("dve_start_steps")
        s_tokidx = sem("tok_idx_ready")
        s_tok = sem("tok_rows_in")
        s_tokused = sem("tok_rows_used")
        s_xn = sem("xn_front")
        s_xtps = sem("xt_front_ps")
        s_xt = sem("xt_front")
        s_fe = sem("gate_exponents")
        s_fi = sem("gate_exp")
        s_act0 = sem("act_steps0")
        s_fr = sem("front_steps")
        s_qpkps = sem("qpk_ps")
        s_qpk = sem("qpk_copied")
        s_simps = sem("sims_ps")
        s_sim = sem("sims_copied")
        s_top = sem("sims_used")
        s_wexp = sem("topk_weight_in")
        s_wexpd = sem("topk_weight_exp")
        s_tk = sem("topk_steps")
        s_idx = sem("idx_ready")
        s_got = [sem(f"rows_in{h}") for h in range(HEADS)]
        s_q = sem("q_ps")
        s_qs = sem("q_scaled")
        s_gw = sem("rows_weighted")
        s_kv = sem("kv_summed")
        s_kvc = sem("kv_copied")
        s_ktps = sem("kt_ps_full")
        s_kt = sem("kt_stored")
        s_sc = sem("scores_ps_full")
        s_nm = sem("max_ready")
        s_nms = sem("max_steps")
        s_p = sem("probs_ready")
        s_pps = sem("probs_t_ps")
        s_pt = sem("probs_t")
        s_o = sem("att_ps_full")
        s_os = sem("att_steps")
        s_att = sem("att_ready")
        s_atps = sem("att_t_ps")
        s_att_t = sem("att_t")  
        s_wo = sem("wo_ps")
        s_ts = sem("tail_steps")
        s_xnt = sem("xn_tail")
        s_xtps_t = sem("xt_tail_ps")
        s_xt_t = sem("xt_tail")
        s_h1 = sem("h1_ready")
        s_wo1 = sem("wo1_ps")
        s_up = sem("up_ps")
        s_gelu = sem("gelu")
        s_lm = sem("logit_max")
        s_le = sem("logit_exp")
        s_cmb = sem("combine_ready")
        s_hid = sem("hidden_weighted")
        s_hps = sem("hidden_t_ps")
        s_hidt = sem("hidden_t")
        s_y = sem("moe_ps")
        s_yout = sem("y_ready") 
        s_out = sem("stored")

        block = ctx.enter_context(nc.Block())

        def tile_loop(eng, front, heads, tail, heads_first=False):
            def there(t):
                return not isinstance(t, int) or 0 <= t < TILES

            def background(k, t, p):
                if there(t + 1):
                    front(k, t + 1, 1 - p)
                if k >= TAIL_AT and there(t - 1):
                    tail(k - TAIL_AT, t - 1)

            def foreground(k, t, p):
                if there(t - 1):
                    heads(k + TICKS, t - 1, 1 - p)
                if there(t):
                    heads(k, t, p)

            def tile(t, p):
                for k in range(TICKS):
                    if heads_first:
                        foreground(k, t, p)
                    background(k, t, p)
                    if not heads_first:
                        foreground(k, t, p)

            tile(-1, 1)
            tile(0, 0)
            tile(1, 1)
            with eng.Fori(0, (TILES - 4) // 2) as i:
                tile(2 * i + 2, 0)
                tile(2 * i + 3, 1)
            tile(TILES - 2, 0)
            tile(TILES - 1, 1)
            tile(TILES, 0)

        @block.sync
        def _(sp):
            sp.dma_start(ids[:, 0, :], x_ids).then_inc(s_ids, 16)
            sp.dma_start(ids[:, 1, :], itok_ids).then_inc(s_ids, 16)
            loads = [(w0_sb[:, :], w0), (ib_sb[:, :], input_bias), (ns_sb[:, :], norm_scale.broadcast_to([P, D])),
                     (wqpk_sb[:, :], wqpk), (wq_sb[:, :], wq),
                     (wo_sb[:, :, :], wo.rearrange("(c p) d -> p c d", p=P)),
                     (w1_sb[:, :], w1), (wo1_sb[:, :], wo1), (router_sb[:, :], router), (up_sb[:, :], up),
                     (down_sb[:, :, :], down.rearrange("(c p) d -> p c d", p=P)), (db_sb[:, :], down_bias)]
            for dst, src in loads:
                sp.dma_start(dst, src).then_inc(s_w, 16)
            sp.wait_ge(s_const_dve, 1)
            for c in range(4):
                for h in range(4):
                    sp.dma_start(pkk_sb[DIM_KEY * h:DIM_KEY * (h + 1), c, NUM_KEYS * h:NUM_KEYS * (h + 1)],
                                 pk_keys[4 * c + h]).then_inc(s_w, 16)

            def store(t):
                sp.wait_ge(s_yout, t + 1)
                sp.dma_start(out[bass.ts(t, P), :], y_out[:, :]).then_inc(s_out, 16)

            store(0)
            with sp.Fori(1, TILES) as t:
                store(t)
            sp.wait_ge(s_out, 16 * TILES)

        N_LOADS = 16 * (12 + 16)

        @block.gpsimd
        def _(pool):
            pool.memset(ident[:, :], 0.0)
            pool.memset(causal[:, :], 0.0)
            pool.memset(row_sel[:, :, :, :], 0.0).then_inc(s_const_pool, 1)
            pool.wait_ge(s_const_pool, 1)
            pool.affine_select(out=ident[:, :], in_=ident[:, :], compare_op=ALU.not_equal, fill=1.0, base=0,
                               pattern=[[-1, P]], channel_multiplier=1)
            pool.affine_select(out=causal[:, :], in_=causal[:, :], compare_op=ALU.is_ge, fill=MASKED,
                               base=SEQ - P, pattern=[[-1, 2 * SEQ - P]], channel_multiplier=1)
            pool.affine_select(out=row_sel[:, :, :, :], in_=row_sel[:, :, :, :], compare_op=ALU.not_equal,
                               fill=1.0, base=0, pattern=[[-1, HALF], [-HALF, 2], [0, D]],
                               channel_multiplier=1).then_inc(s_const_pool, 1)

            def embedding(t):
                pool.wait_ge(s_tokidx, t + 1)
                wait(pool, s_tokused, t)
                own_wait()
                for n in range(2):
                    pool.indirect_dma_start(emb[:, n, :], None, tok_w,
                                            bass.IndirectOffsetOnAxis(ap=tok_idx[:, n:n + 1], axis=0)
                                            ).then_inc(s_tok, 16)

            def gather_head(h, t, p):
                if not isinstance(t, int) or HEADS * t + h >= RING:
                    pool.wait_ge(s_kv, HEADS * t + h + 1 - RING)
                    own_wait()
                for r in range(TOPK):
                    n = h * TOPK + r
                    pool.indirect_dma_start(got[:, h % RING, r, :], None, kv_table,
                                            bass.IndirectOffsetOnAxis(ap=idx[p][:, n:n + 1], axis=0)
                                            ).then_inc(s_got[h], 16)

            def own_wait():
                pool.sem_inc(s_turn_pool, 1)

            def heads(k, t, p):
                if k == 0:
                    if not isinstance(t, int) or t + 1 < TILES:
                        embedding(t + 1)
                    pool.wait_ge(s_idx, t + 1)
                    own_wait()
                if k < TICKS and k % HEAD_TICKS == 0:
                    gather_head(k // HEAD_TICKS, t, p)

            embedding(0)
            tile_loop(pool, lambda k, t, p: None, heads, lambda k, t: None)

        @block.vector
        def _(dve):
            dve.memset(pkk_sb[:, :, :], 0.0).then_inc(s_const_dve, 1)
            dve.memset(half_sel[:, :], 0.0)
            dve.memset(ones_col[:, :], 1.0)
            for a in range(TOPK):
                dve.memset(starts[:, a:a + 1], float(STARTS[a]))
                dve.memset(start_steps[:, a:a + 1], float(STARTS[a] - STARTS[a - 1] if a else 0))
                dve.memset(count16[:, a:a + 1], float(a))
            for h in range(HEADS):
                dve.memset(count8[:, h:h + 1], float(h))
                dve.memset(head_base[:, h:h + 1], float(h * NUM_KEYS * NUM_KEYS))
            dve.memset(xt0[D:D + 1, :], 1.0)
            dve.memset(xt3[D:D + 1, :], 1.0)
            dve.memset(ht[D:D + 1, :], 1.0)
            dve.memset(xt4[D:D + 1, :], 1.0)
            for padded in (xn_f, xn_t, h_pad):
                dve.memset(padded[:, :], 0.0)
            dve.memset(mx[:, :], 0.0)
            for s in lay:
                dve.memset(s.mc[:, :], 0.0)
                dve.memset(s.nst[:, :], 0.0)
            dve.memset(kt[:, :, :], 0.0)
            dve.memset(vc[:, :], 0.0)
            dve.memset(keep[:, :], 1.0)
            dve.memset(rows[:, :, :], 0).then_inc(s_start, 1)
            dve.wait_ge(s_start, 1)
            dve.memset(half_sel[0:D, 0:1], 1.0)
            dve.memset(half_sel[D:P, 1:2], 1.0)
            dve.memset(keep[:, :].rearrange("p (b j) -> p b j", j=ROW_TILES)[:, :, 0:1], 0.0)
            dve.wait_ge(s_ids, 32)
            dve.tensor_copy(idf[:, :, :], ids[:, :, :]).then_inc(s_start, 1)
            dve.wait_ge(s_start, 2)
            dve.tensor_tensor(differ[:, :], idf[:, 0, :], idf[:, 1, :], ALU.not_equal)
            dve.tensor_scalar(neg[:, :, :], idf[:, :, :], 0.0, float(V), ALU.is_lt, ALU.mult).then_inc(s_start, 1)
            dve.wait_ge(s_start, 3)
            dve.tensor_tensor(idf[:, :, :], idf[:, :, :], neg[:, :, :], ALU.add).then_inc(s_start, 1)
            dve.wait_ge(s_start, 4)
            dve.tensor_scalar(rows[:, :, 0:TILES], idf[:, :, :], 0.0, float(V - 1), ALU.max, ALU.min
                              ).then_inc(s_start, 1)
            dve.wait_ge(s_start, 5)
            dve.tensor_copy(tok_idx[:, :], rows[:, :, 0]).then_inc(s_tokidx, 1)
            dve.wait_ge(s_const_pool, 2)
            dve.tensor_copy(ident_b[:, :], ident[:, :])
            dve.wait_ge(s_w, N_LOADS)
            dve.tensor_scalar(ib5_sb[:, :], ib_sb[:, :], 0.2, None, ALU.mult).then_inc(s_const_dve, 1)

            def own_wait():
                dve.sem_inc(s_turn_dve, 1)

            def ask_root(r, x, scale, add):
                dve.tensor_scalar(r.v[:, :], x, scale, add, ALU.mult, ALU.add).then_inc(r.asked, 1)

            def inverse_root(st, r, done):
                dve.wait_ge(r.guess, done)
                st.link(dve.scalar_tensor_tensor(out=r.a[:, :], in0=r.g[:, :], scalar=r.g[:, 0:1], in1=r.v[:, :],
                                                 op0=ALU.mult, op1=ALU.mult))
                st.link(dve.tensor_scalar(r.a[:, :], r.a[:, :], -0.5, 1.5, ALU.mult, ALU.add))
                st.link(dve.tensor_tensor(r.y[:, :], r.a[:, :], r.g[:, :], ALU.mult))

            def moments(st, x, stat, mv, r):
                own_wait()
                st.link(dve.bn_stats(stat[:, :], x))
                own_wait()
                st.link(dve.bn_aggr(mv[:, :], stat[:, :]))
                ask_root(r, mv[:, 1:2], 1.0, EPS)

            def layer_norm(st, x, y, mv, r, done):
                inverse_root(st, r, done)
                return dve.tensor_scalar(y, x, mv[:, 0:1], r.y[:, 0:1], ALU.subtract, ALU.mult)

            def carry_state(s, t, st):
                st.link(dve.tensor_scalar(s.mc0[:, :], s.mc[:, :], keep[:, bass.ds(t, 1)], None, ALU.mult))

            def recur(s, g0, t, st):
                banks = [s.wide[g][:, :].rearrange("p (i a n) -> p i a n", i=2, a=2) for g in range(2)]
                for g in (g0, g0 + 1):
                    dve.wait_ge(s.spread, GROUPS * t + g + 1)
                    st.link(dve.tensor_tensor(s.w[:, g % 2, :, :], banks[g % 2][:, :, 1, :],
                                              s.k2[:, None, :].broadcast_to([P, 2, P]), ALU.mult))
                    for i in range(2):
                        last = dve.tensor_tensor_scan(s.y[:, 2 * g + i, :], banks[g % 2][:, i, 0, :],
                                                      s.w[:, g % 2, i, :], s.mc0[:, 2 * g + i:2 * g + i + 1],
                                                      ALU.mult, ALU.add)
                    last.then_inc(s.scanned, 1)
                    if g % 4 == 3:
                        dve.wait_ge(s.scanned, GROUPS * t + g + 1)
                        a = slice(2 * (g - 3), 2 * (g + 1))
                        st.link(dve.tensor_copy(s.mc[:, a], s.y[:, a, P - 1]))
                        dve.tensor_tensor(s.y[:, a, :], s.y[:, a, :], s.q2[:, None, :].broadcast_to([P, 8, P]),
                                          ALU.mult).then_inc(s.yq_ready, 1)

            def magnitude(s, st, least):
                st.link(dve.tensor_copy(s.den[:, :], s.wide[0][:, D:D + 1]))
                st.link(dve.scalar_tensor_tensor(out=s.den[:, :], in0=s.den[:, :], scalar=-1.0, in1=s.den[:, :],
                                                 op0=ALU.mult, op1=ALU.max))
                st.link(dve.tensor_scalar(s.den[:, :], s.den[:, :], least, None, ALU.max))
                st.link(dve.reciprocal(s.dr[:, :], s.den[:, :]))

            def normaliser(s, t, st):
                st.link(dve.tensor_tensor(s.ik[:, :], s.gates[:, 2, :], s.k2[0:D, :], ALU.mult))
                st.link(dve.tensor_scalar(s.nst[:, 0:1], s.nst[:, P:P + 1], keep[0:D, bass.ds(t, 1)], None, ALU.mult))
                st.link(dve.tensor_tensor_scan(s.nst[:, 1:P + 1], s.gates[:, 0, :], s.ik[:, :], s.nst[:, 0:1],
                                               ALU.mult, ALU.add))
                dve.tensor_tensor(s.nq[:, :], s.nst[:, 1:P + 1], s.q2[0:D, :], ALU.mult).then_inc(s.nq_ready, 1)

            steps = Parts()

            def front(k, t, p):
                s = lay[0]
                x1_t = x1[:, bass.ds((t & 3) * D, D)]
                if k == 0:
                    steps.front = st = Steps(dve, s_fr, t, FRONT_STEPS)
                    dve.wait_ge(s_tok, 32 * (t + 1))
                    dve.scalar_tensor_tensor(out=x0[:, :], in0=emb[:, 1, :], scalar=differ[:, bass.ds(t, 1)],
                                             in1=emb[:, 0, :], op0=ALU.mult, op1=ALU.add).then_inc(s_tokused, 1)
                    dve.tensor_copy(tok_idx[:, :], rows[:, :, bass.ds(t + 1, 1)].rearrange("p a b -> p (a b)")
                                    ).then_inc(s_tokidx, 1)
                    dve.wait_ge(s_tokused, t + 1)
                    moments(st, x0[:, :], stat_f, mv_f, root_f)
                st = steps.front
                if k == 1:
                    layer_norm(st, x0[:, :], xn_f[:, 0:D], mv_f, root_f, 3 * t + 1).then_inc(s_xn, 1)
                if k == 4:
                    dve.wait_ge(s.gated, t + 1)
                    st.link(dve.tensor_scalar(soft_in[:, :], soft_in[:, :], 1.0, None, ALU.add))
                    st.link(dve.reciprocal(li[:, :], soft_in[:, :]))
                    st.link(dve.tensor_scalar(li[:, :], li[:, :], -20.0, 10.0, ALU.mult, ALU.add))
                    st.link(dve.scalar_tensor_tensor(out=lf[:, :], in0=wide_f[1][0:D, 2 * P:3 * P], scalar=0.0,
                                                     in1=lnf[:, :], op0=ALU.max, op1=ALU.add))
                    st.link(dve.tensor_scalar(lf[:, :], lf[:, :], -1.0, None, ALU.mult))
                    st.link(dve.tensor_scalar(mx[:, 0:1], mx[:, P:P + 1], keep[0:D, bass.ds(t, 1)], None, ALU.mult))
                    st.link(dve.tensor_tensor_scan(mx[:, 1:P + 1], lf[:, :], li[:, :], mx[:, 0:1], ALU.add, ALU.max))
                    st.link(dve.tensor_tensor(fe[:, 0, :], lf[:, :], mx[:, 0:P], ALU.add))
                    dve.tensor_tensor(fe[:, 0, :], fe[:, 0, :], mx[:, 1:P + 1], ALU.subtract)
                    dve.tensor_tensor(fe[:, 1, :], li[:, :], mx[:, 1:P + 1], ALU.subtract).then_inc(s_fe, 1)
                if k == 5:
                    dve.wait_ge(s_fi, t + 1)
                    dve.tensor_tensor(s.gates[:, 1, :], s.gates[:, 2, :], wide_f[1][0:D, 0:P], ALU.mult
                                      ).then_inc(s.gates_ready, 1)
                    normaliser(s, t, st)
                    carry_state(s, t, st)
                    st.link(dve.tensor_scalar(osig[:, :], osig[:, :], 1.0, None, ALU.add))
                    st.link(dve.reciprocal(osig[:, :], osig[:, :]))
                if 6 <= k < 6 + GROUPS // 2:
                    recur(s, 2 * (k - 6), t, st)
                if k == 14:
                    dve.wait_ge(s.hraw, t + 1)
                    magnitude(s, st, 1e-6)
                    st.link(dve.scalar_tensor_tensor(out=h0[:, :].rearrange("p (a i) -> p a i", a=2),
                                                     in0=s.wide[0][:, 0:D].rearrange("p (i a) -> p a i", a=2),
                                                     scalar=s.dr[:, 0:1],
                                                     in1=osig[:, :].rearrange("p (a i) -> p a i", a=2),
                                                     op0=ALU.mult, op1=ALU.mult))
                    st.link(dve.tensor_tensor_reduce(sq[:, :], h0[:, :], h0[:, :], 1.0, 0.0, ALU.mult, ALU.add,
                                                     ss[:, :]))
                    ask_root(root_f, ss[:, :], 1.0 / D, 1e-8)
                if k == 15:
                    inverse_root(st, root_f, 3 * t + 2)
                    st.link(dve.scalar_tensor_tensor(out=h0[:, :], in0=h0[:, :], scalar=root_f.y[:, 0:1],
                                                     in1=ns_sb[:, :], op0=ALU.mult, op1=ALU.mult))
                    st.link(dve.tensor_tensor(x1_t, h0[:, :], x0[:, :], ALU.add))
                    moments(st, x1_t, stat_f, mv_f, root_f)
                if k == 16:
                    layer_norm(st, x1_t, xn_f[:, 0:D], mv_f, root_f, 3 * t + 3).then_inc(s_xn, 1)
                    st.close()
                if k >= 20:
                    topk(k - 20, t, p)

            def best8(lo, src):
                own_wait()
                for n in range(2 * HEADS):
                    last = dve.max(best[:, n, lo:lo + 8], src[:, n, :])
                return last

            def best8_at(lo, src):
                own_wait()
                for n in range(2 * HEADS):
                    last = dve.max_index(best_at[:, n, lo:lo + 8], best[:, n, lo:lo + 8], src[:, n, :])
                return last

            def final8(st, lo, src):
                own_wait()
                for h in range(HEADS):
                    last = dve.max(fin[:, h, lo:lo + 8], src[:, h, :])
                st.link(last)
                own_wait()
                for h in range(HEADS):
                    last = dve.max_index(fin_at[:, h, lo:lo + 8], fin[:, h, lo:lo + 8], src[:, h, :])
                return last

            def topk(k, t, p):
                full = [P, HEADS, TOPK, TOPK]
                flat = [P, HEADS * TOPK, TOPK]
                hot_f = hot[:, :, :, :].rearrange("p h r a -> p (h r) a")
                hotv_f = hotv[:, :, :, :].rearrange("p h r a -> p (h r) a")
                if k == 0:
                    steps.topk = st = Steps(dve, s_tk, t, TOPK_STEPS)
                    dve.wait_ge(s_sim, 2 * (t + 1))
                    st.link(best8(0, sims))
                    best8_at(0, sims)
                st = steps.topk
                if k == 1:
                    for n in range(2 * HEADS):
                        last = dve.match_replace(sims_left[:, n, :], best[:, n, 0:8], sims[:, n, :], LOWEST)
                    last.then_inc(s_top, 1)
                    dve.wait_ge(s_top, t + 1)
                    st.link(best8(8, sims_left))
                if k == 2:
                    st.link(best8_at(8, sims_left))
                    dve.tensor_copy(at_f[:, :, :], best_at[:, :, :])
                    for (a0, na, nb), at in zip(LOTS, [0, 16, 24, 34, 46]):
                        last = dve.tensor_tensor(
                            cand[:, :, at:at + na * nb].rearrange("p h (a b) -> p h a b", a=na),
                            best[:, 0:HEADS, a0:a0 + na, None].broadcast_to([P, HEADS, na, nb]),
                            best[:, HEADS:2 * HEADS, None, 0:nb].broadcast_to([P, HEADS, na, nb]), ALU.add)
                    st.link(last)
                if k == 3:
                    final8(st, 0, cand)
                    for h in range(HEADS):
                        last = dve.match_replace(cand_left[:, h, :], fin[:, h, 0:8], cand[:, h, :], LOWEST)
                    st.link(last)
                if k == 4:
                    st.link(final8(st, 8, cand_left))
                    dve.tensor_tensor(wt[p][:, :, :], fin[:, :, :], fin[:, :, 0:1].broadcast_to([P, HEADS, TOPK]),
                                      ALU.subtract).then_inc(s_wexp, 1)
                    dve.tensor_copy(place[:, :, :], fin_at[:, :, :])
                    dve.tensor_copy(at0_steps[:, :, 0:1], at_f[:, 0:HEADS, 0:1])
                    st.link(dve.tensor_tensor(at0_steps[:, :, 1:TOPK], at_f[:, 0:HEADS, 1:TOPK],
                                              at_f[:, 0:HEADS, 0:TOPK - 1], ALU.subtract))
                if k == 5:
                    place_b = place[:, :, :].rearrange("p h r -> p (h r)")[:, :, None].broadcast_to(flat)
                    st.link(dve.tensor_tensor(hot_f, place_b, starts[:, None, :].broadcast_to(flat), ALU.is_ge))
                    st.link(dve.tensor_tensor(hotv[:, :, :, :], hot[:, :, :, :],
                                              at0_steps[:, :, None, :].broadcast_to(full), ALU.mult))
                    st.link(dve.tensor_reduce(key0[:, :, :], hotv[:, :, :, :], AX, ALU.add))
                if k == 6:
                    st.link(dve.tensor_tensor(hotv_f, hot_f, start_steps[:, None, :].broadcast_to(flat), ALU.mult))
                    st.link(dve.tensor_reduce(off[:, :, :], hotv[:, :, :, :], AX, ALU.add))
                    st.link(dve.tensor_tensor(rank1[:, :, :], place[:, :, :], off[:, :, :], ALU.subtract))
                    rank_b = rank1[:, :, :].rearrange("p h r -> p (h r)")[:, :, None].broadcast_to(flat)
                    st.link(dve.tensor_tensor(hot_f, rank_b, count16[:, None, :].broadcast_to(flat), ALU.is_equal))
                if k == 7:
                    st.link(dve.tensor_tensor(hotv[:, :, :, :], hot[:, :, :, :],
                                              at_f[:, HEADS:2 * HEADS, None, :].broadcast_to(full), ALU.mult))
                    st.link(dve.tensor_reduce(key1[:, :, :], hotv[:, :, :, :], AX, ALU.add))
                    st.link(dve.scalar_tensor_tensor(out=key0[:, :, :], in0=key1[:, :, :], scalar=float(NUM_KEYS),
                                                     in1=key0[:, :, :], op0=ALU.mult, op1=ALU.add))
                    dve.tensor_tensor(idx[p][:, :].rearrange("p (h r) -> p h r", h=HEADS), key0[:, :, :],
                                      head_base[:, :, None].broadcast_to([P, HEADS, TOPK]), ALU.add
                                      ).then_inc(s_idx, 1)
                if k == 8:
                    dve.wait_ge(s_wexpd, t + 1)
                    st.link(dve.tensor_reduce(wsum[:, :], wt[p][:, :, :], AX, ALU.add))
                    st.link(dve.reciprocal(wsum[:, :], wsum[:, :]))
                    st.link(dve.tensor_tensor(wt[p][:, :, :], wt[p][:, :, :],
                                              wsum[:, :, None].broadcast_to([P, HEADS, TOPK]), ALU.mult))
                    st.close()

            FRONT_STEPS, TOPK_STEPS = 55, 22

            def heads(k, t, p):
                if k < TICKS and k % HEAD_TICKS == 0:
                    h = k // HEAD_TICKS
                    dve.wait_ge(s_got[h], 16 * TOPK * (t + 1))
                    dve.tensor_tensor(got[:, h % RING, :, :], got[:, h % RING, :, :],
                                      wt[p][:, h, :, None].broadcast_to([P, TOPK, 2 * D]), ALU.mult
                                      ).then_inc(s_gw, 1)
                h, part = divmod(k - ATTEND, HEAD_TICKS)
                if part == 1 and 0 <= h < HEADS:
                    n = HEADS * t + h + 1
                    dve.wait_ge(s_sc, n)
                    dve.tensor_reduce(nmax[:, h:h + 1], score_ps[:, :], AX, ALU.max).then_inc(s_nms, 1)
                    dve.wait_ge(s_nms, n)
                    dve.tensor_scalar(nmax[:, h:h + 1], nmax[:, h:h + 1], -1.0, None, ALU.mult).then_inc(s_nm, 1)
                if part == 0 and 1 <= h <= HEADS:
                    h -= 1
                    n = HEADS * t + h + 1
                    dve.wait_ge(s_o, n)
                    dve.reciprocal(rrec[:, h:h + 1], rsum[:, h:h + 1]).then_inc(s_os, 1)
                    dve.wait_ge(s_os, n)
                    if h == 0:
                        wait(dve, s_atps, t)
                    dve.tensor_scalar(att[:, h * D:(h + 1) * D], score_ps[:, 0:D], rrec[:, h:h + 1], None,
                                      ALU.mult).then_inc(s_att, 1)

            def tail(k, t):
                s = lay[1]
                if k == 2:
                    steps.tail = st = Steps(dve, s_ts, t, TAIL_STEPS)
                    dve.wait_ge(s_wo, t + 1)
                    st.link(dve.tensor_tensor(x2[:, :], wide_t[1][:, 0:D], x1[:, bass.ds((t & 3) * D, D)], ALU.add))
                    moments(st, x2[:, :], stat_t, mv_t, root_t)
                if k < 3:
                    return
                st = steps.tail
                if k == 3:
                    layer_norm(st, x2[:, :], xn_t[:, 0:D], mv_t, root_t, 2 * t + 1).then_inc(s_xnt, 1)
                if k == 6:
                    dve.wait_ge(s.gated, t + 1)
                    st.link(dve.tensor_scalar(s.gates[:, 0, :], s.gates[:, 0, :], 1.0, None, ALU.add))
                    st.link(dve.reciprocal(s.gates[:, 0, :], s.gates[:, 0, :]))
                    dve.tensor_tensor(s.gates[:, 1, :], s.gates[:, 2, :], s.q2[0:D, :], ALU.mult
                                      ).then_inc(s.gates_ready, 1)
                    normaliser(s, t, st)
                    carry_state(s, t, st)
                if 7 <= k < 7 + GROUPS // 2:
                    recur(s, 2 * (k - 7), t, st)
                if k == 15:
                    dve.wait_ge(s.hraw, t + 1)
                    magnitude(s, st, 1.0)
                    dve.tensor_scalar(h_pad[:, 0:D].rearrange("p (a i) -> p a i", a=2),
                                      s.wide[0][:, 0:D].rearrange("p (i a) -> p a i", a=2), s.dr[:, 0:1], None,
                                      ALU.mult).then_inc(s_h1, 1)
                if k == 17:
                    dve.wait_ge(s_wo1, t + 1)
                    st.link(dve.tensor_tensor(x3[:, :], wide_t[0][:, 0:D], x2[:, :], ALU.add))
                    moments(st, x3[:, :], stat_t, mv_t, root_t)
                if k == 18:
                    layer_norm(st, x3[:, :], xn_t[:, 0:D], mv_t, root_t, 2 * t + 2).then_inc(s_xnt, 1)
                    dve.wait_ge(s_xnt, 2 * (t + 1))
                    st.link(dve.tensor_tensor(res[:, :], x3[:, :], xn_t[:, 0:D], ALU.add))
                if k == 20:
                    dve.wait_ge(s_up, t + 1)
                    st.link(dve.tensor_reduce(lmax[:, :], logit_ps, AX, ALU.max))
                    dve.tensor_scalar(lmax[:, :], lmax[:, :], -1.0, None, ALU.mult).then_inc(s_lm, 1)
                if k == 21:
                    dve.wait_ge(s_le, t + 1)
                    st.link(dve.reciprocal(prob_scale[:, :], esum[:, :]))
                    st.link(dve.tensor_scalar(probs[:, :], exps[:, :], prob_scale[:, 0:1], None, ALU.mult))
                    own_wait()
                    st.link(dve.max(top8[:, :], probs[:, :]))
                    own_wait()
                    dve.max_index(top_at[:, :], top8[:, :], probs[:, :])
                    st.link(dve.tensor_tensor(two[:, :], top8[:, 0:1], top8[:, 1:2], ALU.add))
                    dve.tensor_copy(top_f[:, :], top_at[:, :])
                    st.link(dve.tensor_scalar(two[:, :], two[:, :], 1e-12, None, ALU.max))
                    st.link(dve.tensor_scalar(chosen[:, :], count8[:, :], top_f[:, 0:1], None, ALU.is_equal))
                    dve.reciprocal(two_rec[:, :], two[:, :])
                    st.link(dve.scalar_tensor_tensor(out=chosen[:, :], in0=count8[:, :], scalar=top_f[:, 1:2],
                                                     in1=chosen[:, :], op0=ALU.is_equal, op1=ALU.add))
                    dve.scalar_tensor_tensor(out=combine[:, :], in0=probs[:, :], scalar=two_rec[:, 0:1],
                                             in1=chosen[:, :], op0=ALU.mult, op1=ALU.mult).then_inc(s_cmb, 1)
                    dve.wait_ge(s_cmb, t + 1)
                    dve.wait_ge(s_gelu, t + 1)
                    dve.tensor_tensor(hid[:, :, :], hid[:, :, :], combine[:, :, None].broadcast_to([P, EXPERTS, D]),
                                      ALU.mult).then_inc(s_hid, 1)
                if k == 23:
                    dve.wait_ge(s_y, t + 1)
                    wait(dve, s_out, 16 * t)
                    dve.tensor_tensor(y_out[:, :], res[:, :], wide_t[1][:, 0:D], ALU.add).then_inc(s_yout, 1)
                    st.close()

            TAIL_STEPS = 51
            tile_loop(dve, front, heads, tail)

        @block.scalar
        def _(act):
            act.wait_ge(s_const_dve, 2)

            def guess_root(r, done):
                act.wait_ge(r.asked, done)
                act.activation(r.l[:, :], r.v[:, :], ACT.Ln).then_inc(r.logged, 1)
                act.wait_ge(r.logged, done)
                act.activation(r.g[:, :], r.l[:, :], ACT.Exp, scale=-0.5).then_inc(r.guess, 1)

            def front(k, t, p):
                s = lay[0]
                if k == 0:
                    guess_root(root_f, 3 * t + 1)
                if k == 2:
                    act.wait_ge(s_xtps, 2 * t + 1)
                    act.copy(xt0[0:D, :], wide_f[1][0:D, 0:P]).then_inc(s_xt, 1)
                if k == 3:
                    act.wait_ge(s.proj, t + 1)
                    i_ps, f_ps = wide_f[1][0:D, P:2 * P], wide_f[1][0:D, 2 * P:3 * P]
                    wait(act, s.yq_ready, QUARTERS * t)
                    act.activation(absf[:, :], f_ps, ACT.Abs).then_inc(s_act0, 1)
                    act.activation(soft_in[:, :], i_ps, ACT.Exp, bias=ib5_sb[:, 0:1], scale=0.2)
                    act.wait_ge(s_act0, 2 * t + 1)
                    act.activation(expf[:, :], absf[:, :], ACT.Exp, scale=-1.0).then_inc(s_act0, 1)
                    act.activation(s.k2[:, :], wide_f[0][:, 0:P], ACT.Copy, scale=D ** -0.5)
                    act.wait_ge(s_act0, 2 * t + 2)
                    act.activation(lnf[:, :], expf[:, :], ACT.Ln, bias=1.0)
                    act.copy(s.q2[:, :], wide_f[0][:, P:2 * P])
                    act.activation(osig[:, :], wide_f[0][:, 2 * P:2 * P + D], ACT.Exp, scale=-1.0
                                   ).then_inc(s.gated, 1)
                if k == 4:
                    act.wait_ge(s_fe, t + 1)
                    act.activation(s.gates[:, 0:3:2, :], fe[:, :, :], ACT.Exp).then_inc(s_fi, 1)
                if k == 14:
                    guess_root(root_f, 3 * t + 2)
                if k == 15:
                    guess_root(root_f, 3 * t + 3)
                if k == 17:
                    act.wait_ge(s_xtps, 2 * t + 2)
                    act.copy(xt2[:, :], wide_f[1][0:D, 0:P]).then_inc(s_xt, 1)
                if k == 18:
                    act.wait_ge(s_qpkps, t + 1)
                    act.copy(qpk[:, :, :].rearrange("p c n -> p (c n)"), wide_f[0][:, :]).then_inc(s_qpk, 1)
                if k == 19:
                    wait(act, s_top, t)
                    for c in range(2):
                        act.wait_ge(s_simps, 2 * t + c + 1)
                        act.copy(sims[:, HEADS * c:HEADS * (c + 1), :].rearrange("p h k -> p (h k)"),
                                 wide_f[c][:, :]).then_inc(s_sim, 1)
                if k == 20:
                    act.wait_ge(s_q, t + 1)
                    wait(act, s_sc, HEADS * (t - 1))
                    act.activation(qs[p][:, :, :].rearrange("p c n -> p (c n)"), wide_f[0][:, :], ACT.Copy,
                                   scale=D ** -0.5).then_inc(s_qs, 1)
                if k == 24:
                    act.wait_ge(s_wexp, t + 1)
                    act.activation(wt[p][:, :, :], wt[p][:, :, :], ACT.Exp).then_inc(s_wexpd, 1)

            def heads(k, t, p):
                j = t & (ROW_TILES - 1)
                h, part = divmod(k, HEAD_TICKS)
                if h < HEADS and part == 2:
                    n = HEADS * t + h + 1
                    act.wait_ge(s_kv, n)
                    if h % 2 == 0:
                        wait(act, s_ktps, PAIRS * t + h // 2)
                    act.copy(ktmp[:, (h % 2) * D:(h % 2 + 1) * D], head_ps[h % 2][:, 0:D]).then_inc(s_kvc, 1)
                    if not isinstance(t, int) or t > 0:
                        act.wait_ge(s_o, n - HEADS)
                    act.copy(vc[:, bass.ds(j * (HEADS * D) + h * D, D)], head_ps[h % 2][:, D:2 * D]
                             ).then_inc(s_kvc, 1)
                if h < HEADS and part == 3 and h % 2 == 1:
                    c = h // 2
                    act.wait_ge(s_ktps, PAIRS * t + c + 1)
                    if not isinstance(t, int) or t > 0:
                        act.wait_ge(s_sc, HEADS * (t - 1) + h + 1)
                    act.copy(kt[:, c, bass.ds(j * P, P)], head_ps[1][:, P:2 * P]).then_inc(s_kt, 1)
                h, part = divmod(k - ATTEND, HEAD_TICKS)
                n = HEADS * t + h + 1
                if 0 <= h < HEADS and part == 1:
                    act.wait_ge(s_nm, n)
                    act.activation(pr[:, :], score_ps[:, :], ACT.Exp, bias=nmax[:, h:h + 1],
                                   accum_out=rsum[:, h:h + 1]).then_inc(s_p, 1)
                if 0 <= h < HEADS and part == 3:
                    act.wait_ge(s_pps, n)
                    act.copy(prt[:, :, :].rearrange("p k n -> p (k n)"), score_ps[:, :]).then_inc(s_pt, 1)

            def tail(k, t):
                s = lay[1]
                if k == 1:
                    act.wait_ge(s_atps, t + 1)
                    act.copy(att_t[:, :, :].rearrange("p c n -> p (c n)"), wide_t[0][:, :]).then_inc(s_att_t, 1)
                if k == 2:
                    guess_root(root_t, 2 * t + 1)
                if k == 4:
                    act.wait_ge(s_xtps_t, 3 * t + 1)
                    act.copy(xt3[0:D, :], wide_t[0][0:D, 0:P]).then_inc(s_xt_t, 1)
                if k == 5:
                    act.wait_ge(s.proj, t + 1)
                    act.activation(s.gates[:, 0, :], wide_t[1][0:D, P:2 * P], ACT.Exp, scale=-1.0)
                    act.activation(s.gates[:, 2, :], wide_t[1][0:D, 0:P], ACT.Exp)
                    act.copy(s.k2[:, :], wide_t[0][:, 0:P])
                    act.copy(s.q2[:, :], wide_t[0][:, P:2 * P]).then_inc(s.gated, 1)
                if k == 16:
                    act.wait_ge(s_xtps_t, 3 * t + 2)
                    act.copy(ht[0:D, :], wide_t[1][0:D, 0:P]).then_inc(s_xt_t, 1)
                if k == 17:
                    guess_root(root_t, 2 * t + 2)
                if k == 19:
                    act.wait_ge(s_xtps_t, 3 * t + 3)
                    act.copy(xt4[0:D, :], wide_t[1][0:D, 0:P]).then_inc(s_xt_t, 1)
                if k == 20:
                    act.wait_ge(s_lm, t + 1)
                    act.activation(exps[:, :], logit_ps, ACT.Exp, bias=lmax[:, 0:1], accum_out=esum[:, :]
                                   ).then_inc(s_le, 1)
                    act.activation(hid[:, :, :].rearrange("p e d -> p (e d)"), wide_t[0][:, :], ACT.Gelu
                                   ).then_inc(s_gelu, 1)
                if k == 22:
                    act.wait_ge(s_hps, t + 1)
                    act.copy(comb_t[:, :], wide_t[1][0:EXPERTS, 0:P])
                    act.copy(hid_t[:, :, :].rearrange("p c n -> p (c n)"), wide_t[0][:, :]).then_inc(s_hidt, 1)

            tile_loop(act, front, heads, tail)

        @block.tensor
        def _(pe):
            pe.wait_ge(s_w, N_LOADS)
            pe.wait_ge(s_const_pool, 2)
            pe.wait_ge(s_const_dve, 2)

            def spread(s, g0, t):
                for g in (g0, g0 + 1):
                    if g >= 2:
                        pe.wait_ge(s.scanned, GROUPS * t + g - 1)
                    for i in range(2):
                        last = pe.matmul(s.wide[g % 2][:, 2 * P * i:2 * P * (i + 1)],
                                         row_sel[:, 2 * g + i, :, :].rearrange("c a d -> c (a d)"),
                                         s.gates[:, 0:2, :].rearrange("c a n -> c (a n)"), start=True, stop=True)
                    last.then_inc(s.spread, 1)

            def read_out(s, t):
                pe.wait_ge(s.yq_ready, QUARTERS * (t + 1))
                pe.wait_ge(s.nq_ready, t + 1)
                for i in range(HALF):
                    pe.matmul(s.wide[0][:, 2 * i:2 * i + 2], s.y[:, i, :], half_sel[:, :], start=True, stop=True)
                pe.matmul(s.wide[0][:, D:D + 1], s.nq[:, :], ones_col[:, :], start=True, stop=True
                          ).then_inc(s.hraw, 1)

            def front(k, t, p):
                s = lay[0]
                if k in (1, 16):
                    pe.wait_ge(s_xn, 2 * t + (1 if k == 1 else 2))
                    pe.transpose(wide_f[1][:, 0:P], xn_f[:, :], ident[:, :]).then_inc(s_xtps, 1)
                if k == 2:
                    pe.wait_ge(s_xt, 2 * t + 1)
                    wait(pe, s_qs, t)
                    for c in (0, P):
                        pe.matmul(wide_f[0][:, c:c + P], w0_sb[:, c:c + P], xt0[:, :], start=True, stop=True)
                    pe.matmul(wide_f[0][:, 2 * P:2 * P + D], xt0[:, :], w0_sb[:, 2 * P:2 * P + D],
                              start=True, stop=True)
                    for n in range(3):
                        last = pe.matmul(wide_f[1][0:D, n * P:(n + 1) * P],
                                         w0_sb[:, 2 * P + D * (n + 1):2 * P + D * (n + 2)], xt0[:, :],
                                         start=True, stop=True)
                    last.then_inc(s.proj, 1)
                if k == 5:
                    pe.wait_ge(s.gates_ready, t + 1)
                if 5 <= k < 5 + GROUPS // 2:
                    spread(s, 2 * (k - 5), t)
                if k == 13:
                    read_out(s, t)
                if k == 17:
                    pe.wait_ge(s_xt, 2 * t + 2)
                    for c in range(4):
                        last = pe.matmul(wide_f[0][:, c * P:(c + 1) * P], wqpk_sb[:, c * P:(c + 1) * P], xt2[:, :],
                                         start=True, stop=True)
                    last.then_inc(s_qpkps, 1)
                if k == 18:
                    pe.wait_ge(s_qpk, t + 1)
                    for c in range(4):
                        last = pe.matmul(wide_f[c // 2][:, 256 * (c % 2):256 * (c % 2 + 1)], qpk[:, c, :],
                                         pkk_sb[:, c, :], start=True, stop=True)
                        if c % 2:
                            last.then_inc(s_simps, 1)
                if k == 19:
                    pe.wait_ge(s_sim, 2 * (t + 1))
                    for c in range(PAIRS):
                        last = pe.matmul(wide_f[0][:, c * P:(c + 1) * P], wq_sb[:, c * P:(c + 1) * P], xt2[:, :],
                                         start=True, stop=True)
                    last.then_inc(s_q, 1)

            def heads(k, t, p):
                j = t & (ROW_TILES - 1)
                h, part = divmod(k, HEAD_TICKS)
                n = HEADS * t + h + 1
                if h < HEADS and part == 1:
                    pe.wait_ge(s_gw, n)
                    if h % 2 == 0:
                        wait(pe, s_kvc, 2 * (n - 2))
                    else:
                        wait(pe, s_kt, PAIRS * t + h // 2)
                    for r in range(TOPK):
                        last = pe.matmul(head_ps[h % 2][:, 0:P], ident[:, :], got[:, h % RING, r, :],
                                         start=(r == 0), stop=(r == TOPK - 1))
                    last.then_inc(s_kv, 1)
                if h < HEADS and part == 2 and h % 2 == 1:
                    pe.wait_ge(s_kvc, 2 * n)
                    pe.transpose(head_ps[1][:, P:2 * P], ktmp[:, :], ident[:, :]).then_inc(s_ktps, 1)
                h, part = divmod(k - ATTEND, HEAD_TICKS)
                n = HEADS * t + h + 1
                if not 0 <= h < HEADS:
                    return
                c, half = h // 2, slice(D * (h % 2), D * (h % 2 + 1))
                if part == 0:
                    pe.wait_ge(s_kt, PAIRS * t + c + 1)
                    if h == 0:
                        pe.wait_ge(s_qs, t + 1)
                    wait(pe, s_att, n - 1)
                    for b in range(2):
                        dst = score_ps[:, 512 * b:512 * (b + 1)]
                        pe.matmul(dst, ident_b[:, :], causal[:, bass.ds(SEQ - P + 512 * b - P * j, 512)],
                                  start=True, stop=False)
                        last = pe.matmul(dst, qs[p][half, c, :], kt[half, c, 512 * b:512 * (b + 1)],
                                         start=False, stop=True)
                    last.then_inc(s_sc, 1)
                if part == 2:
                    pe.wait_ge(s_p, n)
                    for b in range(ROW_TILES):
                        last = pe.transpose(score_ps[:, b * P:(b + 1) * P], pr[:, b * P:(b + 1) * P], ident[:, :])
                    last.then_inc(s_pps, 1)
                if part == 3:
                    pe.wait_ge(s_pt, n)
                    for b in range(ROW_TILES):
                        v = b * HEADS * D + h * D
                        last = pe.matmul(score_ps[:, 0:D], prt[:, b, :], vc[:, v:v + D],
                                         start=(b == 0), stop=(b == ROW_TILES - 1))
                    last.then_inc(s_o, 1)

            def tail(k, t):
                s = lay[1]
                if k == 0:
                    pe.wait_ge(s_att, HEADS * (t + 1))
                    wait(pe, s_hidt, t)
                    for c in range(PAIRS):
                        last = pe.transpose(wide_t[0][:, c * P:(c + 1) * P], att[:, c * P:(c + 1) * P], ident[:, :])
                    last.then_inc(s_atps, 1)
                if k == 1:
                    pe.wait_ge(s_att_t, t + 1)
                    wait(pe, s_yout, t)
                    for c in range(PAIRS):
                        last = pe.matmul(wide_t[1][:, 0:D], att_t[:, c, :], wo_sb[:, c, :],
                                         start=(c == 0), stop=(c == PAIRS - 1))
                    last.then_inc(s_wo, 1)
                if k == 3:
                    pe.wait_ge(s_xnt, 2 * t + 1)
                    pe.transpose(wide_t[0][:, 0:P], xn_t[:, :], ident[:, :]).then_inc(s_xtps_t, 1)
                if k == 4:
                    pe.wait_ge(s_xt_t, 3 * t + 1)
                    for n in range(2):
                        pe.matmul(wide_t[0][:, n * P:(n + 1) * P], w1_sb[:, n * P:(n + 1) * P], xt3[:, :],
                                  start=True, stop=True)
                    for n in range(2):
                        last = pe.matmul(wide_t[1][0:D, n * P:(n + 1) * P],
                                         w1_sb[:, 2 * P + D * n:2 * P + D * (n + 1)], xt3[:, :], start=True, stop=True)
                    last.then_inc(s.proj, 1)
                if k == 6:
                    pe.wait_ge(s.gates_ready, t + 1)
                if 6 <= k < 6 + GROUPS // 2:
                    spread(s, 2 * (k - 6), t)
                if k == 14:
                    read_out(s, t)
                if k == 15:
                    pe.wait_ge(s_h1, t + 1)
                    pe.transpose(wide_t[1][:, 0:P], h_pad[:, :], ident[:, :]).then_inc(s_xtps_t, 1)
                if k == 16:
                    pe.wait_ge(s_xt_t, 3 * t + 2)
                    pe.matmul(wide_t[0][:, 0:D], ht[:, :], wo1_sb[:, :], start=True, stop=True).then_inc(s_wo1, 1)
                if k == 18:
                    pe.wait_ge(s_xnt, 2 * t + 2)
                    pe.transpose(wide_t[1][:, 0:P], xn_t[:, :], ident[:, :]).then_inc(s_xtps_t, 1)
                if k == 19:
                    pe.wait_ge(s_xt_t, 3 * t + 3)
                    pe.matmul(logit_ps, xt4[0:D, :], router_sb[:, :], start=True, stop=True)
                    pe.matmul(wide_t[0][:, :], xt4[:, :], up_sb[:, :], start=True, stop=True).then_inc(s_up, 1)
                if k == 21:
                    pe.wait_ge(s_cmb, t + 1)
                    pe.transpose(wide_t[1][0:EXPERTS, 0:P], combine[:, :], ident[:, :])
                    pe.wait_ge(s_hid, t + 1)
                    for c in range(4):
                        last = pe.transpose(wide_t[0][:, c * P:(c + 1) * P],
                                            hid[:, 2 * c:2 * c + 2, :].rearrange("p e d -> p (e d)"), ident[:, :])
                    last.then_inc(s_hps, 1)
                if k == 22:
                    pe.wait_ge(s_hidt, t + 1)
                    y_ps = wide_t[1][:, 0:D]
                    for c in range(4):
                        pe.matmul(y_ps, hid_t[:, c, :], down_sb[:, c, :], start=(c == 0), stop=False)
                    pe.matmul(y_ps, comb_t[:, :], db_sb[:, :], start=False, stop=True).then_inc(s_y, 1)

            tile_loop(pe, front, heads, tail, heads_first=True)


def kernel(**a):
    import numpy as np
    import concourse.bacc as bacc
    from concourse.bass_utils import run_bass_kernel_spmd

    a = {k: np.asarray(v) for k, v in a.items()}
    row = lambda w, b: np.concatenate([w, b[None, :]], axis=0)

    def ids(v):
        return np.ascontiguousarray(v.reshape(TILES, P).T)

    k0, q0 = (row(a[f"L0_attn_W{n}"], a[f"L0_attn_b{n}"]) for n in "kq")
    v0, g0 = row(a["L0_attn_Wv"], a["L0_attn_bv"]), row(a["L0_attn_Wg"], a["L0_attn_bg"])
    k1, q1, i1, f1 = (row(a[f"L1_attn_W{n}"].T, a[f"L1_attn_b{n}"]) for n in "kqif")
    feeds = {
        "x_ids": ids(a["x"]), "itok_ids": ids(a["itok_BS_0_99998"]), "tok_w": a["L0_tok_weight"],
        "w0": np.concatenate([k0, k0, q0, q0, g0[:, 2 * D:], v0, g0[:, :2 * D]], axis=1),
        "input_bias": a["L0_attn_input_bias"].reshape(D, 1), "norm_scale": a["L0_attn_norm_scale"].reshape(1, D),
        "wqpk": a["L0_ffn_Wq_pk"],
        "pk_keys": a["L0_ffn_pk_keys"].transpose(0, 2, 3, 1).reshape(2 * HEADS, DIM_KEY, NUM_KEYS),
        "wq": a["L0_ffn_Wq"],
        "kv_table": np.concatenate([a["L0_ffn_keys_table"], a["L0_ffn_values_table"]], axis=1),
        "wo": a["L0_ffn_Wo"],
        "w1": np.concatenate([k1, k1, q1, q1, i1, f1], axis=1),
        "wo1": row(a["L1_attn_Wo"].T, a["L1_attn_bo"]),
        "router": a["L1_ffn_router_w"].T,
        "up": row(a["L1_ffn_w1"].transpose(1, 0, 2).reshape(D, EXPERTS * D), a["L1_ffn_b1"].reshape(-1)),
        "down": a["L1_ffn_w2"].reshape(EXPERTS * D, D), "down_bias": a["L1_ffn_b2"],
    }
    nc = bacc.Bacc("TRN2", target_bir_lowering=False, num_devices=1)
    arrays, args = {}, []
    for name, v in feeds.items():
        v = np.ascontiguousarray(v)
        arrays[name] = v
        args.append(nc.dram_tensor(name, v.shape, mybir.dt.from_np(v.dtype), kind="ExternalInput").ap())
    out = nc.dram_tensor("out", (BATCH * SEQ, D), F32, kind="ExternalOutput").ap()
    tower(nc, *args, out)
    r = run_bass_kernel_spmd(nc, [arrays], core_ids=[0])
    return r.results[0]["out"].reshape(BATCH, SEQ, D)
```

```python
from contextlib import ExitStack

import concourse.bass as bass
from concourse import mybir
from concourse.alu_op_type import AluOpType as ALU

F32 = mybir.dt.float32
BF16 = mybir.dt.bfloat16
I32 = mybir.dt.int32
U32 = mybir.dt.uint32
ACT = mybir.ActivationFunctionType
AX = mybir.AxisListType.X

P = 128
D = 64
BATCH, SEQ = 8, 1024
TILES = BATCH * SEQ // P
ROW_TILES = SEQ // P
HEADS = 8
PAIRS = HEADS // 2
TOPK = 16
NUM_KEYS = 64
DIM_KEY = 32
EXPERTS = 8
HALF = D // 2
GROUPS = HALF // 2
PORTIONS = GROUPS // 2
TICKS = 32
HEAD_TICKS = TICKS // HEADS
EARLY = 14
EMBED_AT = 12
TOPK_AT = 20
TOPK_TICKS = 2
TAIL_AT = 8
ATTEND = 10
SUM_AT = (0, 6, 10, TOPK)
RING = 4
ACT_FROM = 8
EPS = 1e-5
LOWEST = -3.0e38
MASKED = -1.0e30
LOTS = [(0, 1, 16), (1, 1, 8), (2, 2, 5), (4, 4, 3), (8, 8, 1)]
STARTS = [0]
for _a0, _na, _nb in LOTS:
    for _ in range(_na):
        STARTS.append(STARTS[-1] + _nb)
CANDS = STARTS.pop()


def wait(eng, sem, value):
    if not isinstance(value, int) or value > 0:
        eng.wait_ge(sem, value)


class Parts:
    pass


class Steps:

    def __init__(self, eng, sem, done, total):
        self.eng, self.sem, self.done, self.total, self.n = eng, sem, done, total, 0

    def link(self, ins):
        self.n += 1
        ins.then_inc(self.sem, 1)
        self.eng.wait_ge(self.sem, self.done * self.total + self.n)

    def at(self, done):
        self.done = done
        return self

    def close(self):
        assert self.n == self.total, (self.n, self.total)


def tower(nc, x_ids, itok_ids, tok_w, w0, input_bias, norm_scale, wqpk, pk_keys, wq, kv_table, wo, w1, wo1,
          router, up, down, down_bias, out):
    V = tok_w.shape[0]
    ctx = ExitStack()
    with ctx:
        def sb(name, shape, dt=F32):
            return ctx.enter_context(nc.sbuf_tensor(name, shape, dt))

        def ps(name, shape, dt=F32):
            return ctx.enter_context(nc.psum_tensor(name, shape, dt))

        def sem(name):
            return ctx.enter_context(nc.semaphore(name))

        ident = sb("ident", [P, P])
        ident_b = sb("ident_b", [P, P], BF16)
        causal = sb("causal", [P, P], BF16)
        row_sel = sb("row_sel", [P, HALF, 2, D], BF16)
        half_sel = sb("half_sel", [P, 2])
        ones_col = sb("ones_col", [D, 1])
        keep = sb("keep", [P, TILES])
        starts = sb("starts", [P, TOPK], BF16)
        start_steps = sb("start_steps", [P, TOPK], BF16)
        count16 = sb("count16", [P, TOPK], BF16)
        count8 = sb("count8", [P, EXPERTS])
        head_base = sb("head_base", [P, HEADS])
        w0_sb = sb("w0_sb", [D + 1, 8 * D])
        ib_sb = sb("ib_sb", [D, 1])
        ib5_sb = sb("ib5_sb", [D, 1])
        ns_sb = sb("ns_sb", [P, D])
        wqpk_sb = sb("wqpk_sb", [D, 512])
        pkk_sb = sb("pkk_sb", [P, 4, 4 * NUM_KEYS])
        wq_sb = sb("wq_sb", [D, HEADS * D])
        wo_sb = sb("wo_sb", [P, PAIRS, D])
        w1_sb = sb("w1_sb", [D + 1, 6 * D])
        wo1_sb = sb("wo1_sb", [D + 1, D])
        router_sb = sb("router_sb", [D, EXPERTS])
        up_sb = sb("up_sb", [D + 1, EXPERTS * D])
        down_sb = sb("down_sb", [P, 4, D])
        db_sb = sb("db_sb", [EXPERTS, D])
        ids = sb("ids", [P, 2, TILES], I32)
        idf = sb("idf", [P, 2, TILES])
        neg = sb("neg", [P, 2, TILES])
        differ = sb("differ", [P, TILES])
        rows = sb("rows", [P, 2, TILES + 1], I32)
        tok_idx = sb("tok_idx", [P, 2], I32)
        emb = sb("emb", [P, 2, D])
        x0, h0 = sb("x0", [P, D]), sb("h0", [P, D])
        x1 = sb("x1", [P, 4 * D])
        stat_f, mv_f = sb("stat_f", [P, 6]), sb("mv_f", [P, 2])
        xn_f = sb("xn_f", [P, 2 * D])
        xt0 = sb("xt0", [D + 1, P])
        xt2 = sb("xt2", [D, P])
        soft_in = sb("soft_in", [D, P])
        absf, expf, lnf = sb("absf", [D, P]), sb("expf", [D, P]), sb("lnf", [D, P])
        li, lf = sb("li", [D, P]), sb("lf", [D, P])
        mx = sb("mx", [D, P + 1])
        fe = sb("fe", [D, 2, P])
        osig = sb("osig", [P, D])
        qpk = sb("qpk", [P, 4, P])
        sims = sb("sims", [P, 2 * HEADS, NUM_KEYS])
        sims_left = sb("sims_left", [P, 2 * HEADS, NUM_KEYS])
        best = sb("best", [P, 2 * HEADS, TOPK])
        best_at = sb("best_at", [P, 2 * HEADS, TOPK], U32)
        at_f = sb("at_f", [P, 2 * HEADS, TOPK], BF16)
        at0_steps = sb("at0_steps", [P, HEADS, TOPK], BF16)
        cand = sb("cand", [P, HEADS, CANDS])
        cand_left = sb("cand_left", [P, HEADS, CANDS])
        fin = sb("fin", [P, HEADS, TOPK])
        fin_at = sb("fin_at", [P, HEADS, TOPK], U32)
        place = sb("place", [P, HEADS, TOPK], BF16)
        laid_out = sb("laid_out", [P, HEADS * TOPK, TOPK], BF16)
        hot = sb("hot", [P, HEADS, TOPK, TOPK], BF16)
        hotv = sb("hotv", [P, HEADS, TOPK, TOPK], BF16)
        key0 = sb("key0", [P, HEADS, TOPK])
        off = sb("off", [P, HEADS, TOPK])
        rank1 = sb("rank1", [P, HEADS, TOPK], BF16)
        key1 = sb("key1", [P, HEADS, TOPK])
        wsum = sb("wsum", [P, HEADS])
        idx = [sb(f"idx{p}", [P, HEADS * TOPK], I32) for p in range(2)]
        wt = [sb(f"wt{p}", [P, HEADS, TOPK]) for p in range(2)]
        qs = [sb(f"qs{p}", [P, PAIRS, P]) for p in range(2)]
        got = sb("got", [P, RING, TOPK, 2 * D])
        ktmp = sb("ktmp", [P, 2 * D])
        kt = sb("kt", [P, PAIRS, SEQ])
        vc = sb("vc", [P, ROW_TILES * HEADS * D])
        nmax = sb("nmax", [P, HEADS])
        rsum = sb("rsum", [P, HEADS])
        rrec = sb("rrec", [P, HEADS])
        pr = sb("pr", [P, SEQ])
        prt = sb("prt", [P, ROW_TILES, P])
        att = sb("att", [P, HEADS * D])
        att_t = sb("att_t", [P, PAIRS, P])
        x2, x3 = sb("x2", [P, D]), sb("x3", [P, D])
        stat_t, mv_t = sb("stat_t", [P, 6]), sb("mv_t", [P, 2])
        xn_t, h_pad = sb("xn_t", [P, 2 * D]), sb("h_pad", [P, 2 * D])
        xt3 = sb("xt3", [D + 1, P])
        ht = sb("ht", [D + 1, P])
        xt4 = sb("xt4", [D + 1, P])
        lmax, esum, prob_scale = sb("lmax", [P, 1]), sb("esum", [P, 1]), sb("prob_scale", [P, 1])
        exps, probs, top8 = sb("exps", [P, EXPERTS]), sb("probs", [P, EXPERTS]), sb("top8", [P, 8])
        top_at, top_f = sb("top_at", [P, 8], U32), sb("top_f", [P, 8])
        two, two_rec = sb("two", [P, 1]), sb("two_rec", [P, 1])
        chosen, combine = sb("chosen", [P, EXPERTS]), sb("combine", [P, EXPERTS])
        hid = sb("hid", [P, EXPERTS, D])
        hid_t = sb("hid_t", [P, 4, P])
        comb_t = sb("comb_t", [EXPERTS, P])
        res = sb("res", [P, D])
        y_out = sb("y_out", [P, D])

        score_ps = ps("score_ps", [P, SEQ])
        head_ps = ps("head_ps", [P, 512])
        read_ps = ps("read_ps", [P, 512])
        wide_f = [ps(f"wide_f{s}", [P, 512]) for s in range(2)]
        wide_t = [ps(f"wide_t{s}", [P, 512]) for s in range(2)]
        logit_ps = wide_t[1][:, 256:256 + EXPERTS]

        weighed, states = sb("weighed", [P, 2, 2, P]), sb("states", [P, HALF, P])
        den, den_rec = sb("den", [P, 1]), sb("den_rec", [P, 1])

        def layer(n):
            s = Parts()
            s.wide = (wide_f, wide_t)[n]
            s.k2, s.q2 = sb(f"k2_{n}", [P, P]), sb(f"q2_{n}", [P, P])
            s.gates = sb(f"gates{n}", [D, 3, P])
            s.rest = sb(f"gates_rest{n}", [D, 2, P])
            s.top = sb(f"gates_top{n}", [P, 2, P], BF16)
            s.middle = sb(f"gates_middle{n}", [D, 2, P], BF16)
            s.low = sb(f"gates_low{n}", [D, 2, P], BF16)
            s.ik = sb(f"ik{n}", [D, P])
            s.nst, s.nq = sb(f"nst{n}", [D, P + 1]), sb(f"nq{n}", [D, P])
            s.mc, s.mc0 = sb(f"mc{n}", [P, HALF]), sb(f"mc0_{n}", [P, HALF])
            s.w, s.y, s.den, s.dr = weighed, states, den, den_rec
            s.proj, s.gated = sem(f"proj_ps{n}"), sem(f"gates_begun{n}")
            s.gates_ready, s.nq_ready = sem(f"gates_ready{n}"), sem(f"nq_ready{n}")
            s.spread, s.scanned = sem(f"spread_ps{n}"), sem(f"scanned{n}")
            s.yq_ready, s.hraw = sem(f"yq_ready{n}"), sem(f"read_out_ps{n}")
            return s

        lay = [layer(0), layer(1)]
        ss, sq = sb("ss", [P, 1]), sb("sq", [P, D])

        def root(n):
            s = Parts()
            s.v, s.l, s.g, s.a, s.y = (sb(f"root_{what}{n}", [P, 1]) for what in "vlgay")
            s.asked, s.logged, s.guess = sem(f"root_asked{n}"), sem(f"root_log{n}"), sem(f"root_guess{n}")
            return s

        root_f, root_t = root(0), root(1)

        s_w = sem("weights_in")
        s_ids = sem("ids_in")
        s_const_pool = sem("const_pool")
        s_const_dve = sem("const_dve")
        s_turn_dve, s_turn_pool = sem("turn_dve"), sem("turn_pool")
        s_start = sem("dve_start_steps")
        s_tokidx = sem("tok_idx_ready")
        s_tok = sem("tok_rows_in")
        s_tokused = sem("tok_rows_used")
        s_xn = sem("xn_front")
        s_xtps = sem("xt_front_ps")
        s_xt = sem("xt_front")
        s_fe = sem("gate_exponents")
        s_fi = sem("gate_exp")
        s_act0 = sem("act_steps0")
        s_fr = sem("front_steps")
        s_qpkps = sem("qpk_ps")
        s_qpk = sem("qpk_copied")
        s_simps = sem("sims_ps")
        s_sim = sem("sims_copied")
        s_top = sem("sims_used")
        s_wexp = sem("topk_weight_in")
        s_wexpd = sem("topk_weight_exp")
        s_place, s_placed = sem("places_ready"), sem("places_laid_out")
        s_tk = sem("topk_steps")
        s_idx = sem("idx_ready")
        s_got = [sem(f"rows_in{h}") for h in range(HEADS)]
        s_q = sem("q_ps")
        s_qs = sem("q_scaled")
        s_gw = sem("rows_weighted_dve")
        s_gwa = sem("rows_weighted_act")
        s_kv = sem("kv_summed")
        s_kvc = sem("kv_copied")
        s_ktps = sem("kt_ps_full")
        s_kt = sem("kt_stored")
        s_sc = sem("scores_ps_full")
        s_nm = sem("max_ready")
        s_nms = sem("max_steps")
        s_p = sem("probs_ready")
        s_pps = sem("probs_t_ps")
        s_pt = sem("probs_t")
        s_o = sem("att_ps_full")
        s_os = sem("att_steps")
        s_att = sem("att_ready")
        s_atps = sem("att_t_ps")
        s_att_t = sem("att_t")  
        s_wo = sem("wo_ps")
        s_ts = sem("tail_steps")
        s_xnt = sem("xn_tail")
        s_xtps_t = sem("xt_tail_ps")
        s_xt_t = sem("xt_tail")
        s_h1 = sem("h1_ready")
        s_wo1 = sem("wo1_ps")
        s_up = sem("up_ps")
        s_gelu = sem("gelu")
        s_lm = sem("logit_max")
        s_le = sem("logit_exp")
        s_cmb = sem("combine_ready")
        s_hid = sem("hidden_weighted")
        s_hps = sem("hidden_t_ps")
        s_hidt = sem("hidden_t")
        s_y = sem("moe_ps")
        s_yout = sem("y_ready") 
        s_out = sem("stored")

        block = ctx.enter_context(nc.Block())

        def tile_loop(eng, front, heads, tail, heads_first=False):
            def there(t):
                return not isinstance(t, int) or 0 <= t < TILES

            def background(k, t, p):
                if there(t + 1):
                    front(k + EARLY, t + 1, 1 - p)
                if there(t + 2) and k >= TICKS - EARLY:
                    front(k + EARLY - TICKS, t + 2, p)
                if k >= TAIL_AT and there(t - 1):
                    tail(k - TAIL_AT, t - 1)

            def foreground(k, t, j):
                if there(t - 1):
                    heads(k + TICKS, t - 1, (j - 1) % ROW_TILES)
                if there(t):
                    heads(k, t, j)

            def tile(t, j):
                for k in range(TICKS):
                    if heads_first:
                        foreground(k, t, j)
                    background(k, t, j % 2)
                    if not heads_first:
                        foreground(k, t, j)

            for t in (-2, -1, 0, 1):
                tile(t, t % ROW_TILES)
            at = eng.alloc_register("tile")
            with eng.Fori(0, BATCH - 1) as b:
                for n in range(ROW_TILES):
                    eng.reg_mov(at, ROW_TILES * b + n + 2)
                    t = eng.snap(at, min_val=n + 2, max_val=TILES - 2 * ROW_TILES + n + 2)
                    tile(t, (n + 2) % ROW_TILES)
            for t in range(TILES - ROW_TILES + 2, TILES + 1):
                tile(t, t % ROW_TILES)

        @block.sync
        def _(sp):
            sp.dma_start(ids[:, 0, :], x_ids).then_inc(s_ids, 16)
            sp.dma_start(ids[:, 1, :], itok_ids).then_inc(s_ids, 16)
            loads = [(w0_sb[:, :], w0), (ib_sb[:, :], input_bias), (ns_sb[:, :], norm_scale.broadcast_to([P, D])),
                     (wqpk_sb[:, :], wqpk), (wq_sb[:, :], wq),
                     (wo_sb[:, :, :], wo.rearrange("(c p) d -> p c d", p=P)),
                     (w1_sb[:, :], w1), (wo1_sb[:, :], wo1), (router_sb[:, :], router), (up_sb[:, :], up),
                     (down_sb[:, :, :], down.rearrange("(c p) d -> p c d", p=P)), (db_sb[:, :], down_bias)]
            for dst, src in loads:
                sp.dma_start(dst, src).then_inc(s_w, 16)
            sp.wait_ge(s_const_dve, 1)
            for c in range(4):
                for h in range(4):
                    sp.dma_start(pkk_sb[DIM_KEY * h:DIM_KEY * (h + 1), c, NUM_KEYS * h:NUM_KEYS * (h + 1)],
                                 pk_keys[4 * c + h]).then_inc(s_w, 16)

            def store(t):
                sp.wait_ge(s_yout, t + 1)
                sp.dma_start(out[bass.ts(t, P), :], y_out[:, :]).then_inc(s_out, 16)

            store(0)
            with sp.Fori(1, TILES) as t:
                store(t)
            sp.wait_ge(s_out, 16 * TILES)

        N_LOADS = 16 * (12 + 16)

        @block.gpsimd
        def _(pool):
            pool.memset(ident[:, :], 0.0)
            pool.memset(causal[:, :], 0.0)
            pool.memset(row_sel[:, :, :, :], 0.0).then_inc(s_const_pool, 1)
            pool.wait_ge(s_const_pool, 1)
            pool.affine_select(out=ident[:, :], in_=ident[:, :], compare_op=ALU.not_equal, fill=1.0, base=0,
                               pattern=[[-1, P]], channel_multiplier=1)
            pool.affine_select(out=causal[:, :], in_=causal[:, :], compare_op=ALU.is_ge, fill=MASKED,
                               base=0, pattern=[[-1, P]], channel_multiplier=1)
            for part in range(2):
                pool.affine_select(out=row_sel[:, :, :, :], in_=row_sel[:, :, :, :], compare_op=ALU.not_equal,
                                   fill=1.0, base=-D * part, pattern=[[-1, HALF], [-HALF, 2], [0, D]],
                                   channel_multiplier=1).then_inc(s_const_pool, 1)
                pool.wait_ge(s_const_pool, 2 + part)

            def embedding(t):
                pool.wait_ge(s_tokidx, t + 1)
                wait(pool, s_tokused, t)
                own_wait()
                for n in range(2):
                    pool.indirect_dma_start(emb[:, n, :], None, tok_w,
                                            bass.IndirectOffsetOnAxis(ap=tok_idx[:, n:n + 1], axis=0)
                                            ).then_inc(s_tok, 16)

            def gather_head(h, t, p):
                if not isinstance(t, int) or HEADS * t + h >= RING:
                    pool.wait_ge(s_kv, HEADS * t + h + 1 - RING)
                    own_wait()
                for r in range(TOPK):
                    n = h * TOPK + r
                    pool.indirect_dma_start(got[:, h % RING, r, :], None, kv_table,
                                            bass.IndirectOffsetOnAxis(ap=idx[p][:, n:n + 1], axis=0)
                                            ).then_inc(s_got[h], 16)

            def own_wait():
                pool.sem_inc(s_turn_pool, 1)

            def heads(k, t, j):
                if k == EMBED_AT and (not isinstance(t, int) or t + 2 < TILES):
                    embedding(t + 2)
                if k == 0:
                    pool.wait_ge(s_idx, t + 1)
                    own_wait()
                if k < TICKS and k % HEAD_TICKS == 0:
                    gather_head(k // HEAD_TICKS, t, j % 2)

            embedding(0)
            embedding(1)
            tile_loop(pool, lambda k, t, p: None, heads, lambda k, t: None)

        @block.vector
        def _(dve):
            dve.memset(pkk_sb[:, :, :], 0.0).then_inc(s_const_dve, 1)
            dve.memset(half_sel[:, :], 0.0)
            dve.memset(ones_col[:, :], 1.0)
            for a in range(TOPK):
                dve.memset(starts[:, a:a + 1], float(STARTS[a]))
                dve.memset(start_steps[:, a:a + 1], float(STARTS[a] - STARTS[a - 1] if a else 0))
                dve.memset(count16[:, a:a + 1], float(a))
            for h in range(HEADS):
                dve.memset(count8[:, h:h + 1], float(h))
                dve.memset(head_base[:, h:h + 1], float(h * NUM_KEYS * NUM_KEYS))
            dve.memset(xt0[D:D + 1, :], 1.0)
            dve.memset(xt3[D:D + 1, :], 1.0)
            dve.memset(ht[D:D + 1, :], 1.0)
            dve.memset(xt4[D:D + 1, :], 1.0)
            for padded in (xn_f, xn_t, h_pad):
                dve.memset(padded[:, :], 0.0)
            dve.memset(mx[:, :], 0.0)
            for s in lay:
                dve.memset(s.mc[:, :], 0.0)
                dve.memset(s.nst[:, :], 0.0)
            dve.memset(keep[:, :], 1.0)
            dve.memset(rows[:, :, :], 0).then_inc(s_start, 1)
            dve.wait_ge(s_start, 1)
            dve.memset(half_sel[0:D, 0:1], 1.0)
            dve.memset(half_sel[D:P, 1:2], 1.0)
            dve.memset(keep[:, :].rearrange("p (b j) -> p b j", j=ROW_TILES)[:, :, 0:1], 0.0)
            dve.wait_ge(s_ids, 32)
            dve.tensor_copy(idf[:, :, :], ids[:, :, :]).then_inc(s_start, 1)
            dve.wait_ge(s_start, 2)
            dve.tensor_tensor(differ[:, :], idf[:, 0, :], idf[:, 1, :], ALU.not_equal)
            dve.tensor_scalar(neg[:, :, :], idf[:, :, :], 0.0, float(V), ALU.is_lt, ALU.mult).then_inc(s_start, 1)
            dve.wait_ge(s_start, 3)
            dve.tensor_tensor(idf[:, :, :], idf[:, :, :], neg[:, :, :], ALU.add).then_inc(s_start, 1)
            dve.wait_ge(s_start, 4)
            dve.tensor_scalar(rows[:, :, 0:TILES], idf[:, :, :], 0.0, float(V - 1), ALU.max, ALU.min
                              ).then_inc(s_start, 1)
            dve.wait_ge(s_start, 5)
            dve.tensor_copy(tok_idx[:, :], rows[:, :, 0]).then_inc(s_tokidx, 1)
            dve.wait_ge(s_const_pool, 3)
            dve.tensor_copy(ident_b[:, :], ident[:, :])
            dve.wait_ge(s_w, N_LOADS)
            dve.tensor_scalar(ib5_sb[:, :], ib_sb[:, :], 0.2, None, ALU.mult).then_inc(s_const_dve, 1)

            def own_wait():
                dve.sem_inc(s_turn_dve, 1)

            def ask_root(r, x, scale, add):
                dve.tensor_scalar(r.v[:, :], x, scale, add, ALU.mult, ALU.add).then_inc(r.asked, 1)

            def inverse_root(st, r, done):
                dve.wait_ge(r.guess, done)
                st.link(dve.scalar_tensor_tensor(out=r.a[:, :], in0=r.g[:, :], scalar=r.g[:, 0:1], in1=r.v[:, :],
                                                 op0=ALU.mult, op1=ALU.mult))
                st.link(dve.tensor_scalar(r.a[:, :], r.a[:, :], -0.5, 1.5, ALU.mult, ALU.add))
                st.link(dve.tensor_tensor(r.y[:, :], r.a[:, :], r.g[:, :], ALU.mult))

            def moments(st, x, stat, mv, r):
                own_wait()
                st.link(dve.bn_stats(stat[:, :], x))
                own_wait()
                st.link(dve.bn_aggr(mv[:, :], stat[:, :]))
                ask_root(r, mv[:, 1:2], 1.0, EPS)

            def layer_norm(st, x, y, mv, r, done):
                inverse_root(st, r, done)
                return dve.tensor_scalar(y, x, mv[:, 0:1], r.y[:, 0:1], ALU.subtract, ALU.mult)

            def carry_state(s, t, st):
                st.link(dve.tensor_scalar(s.mc0[:, :], s.mc[:, :], keep[:, bass.ds(t, 1)], None, ALU.mult))

            def recur(s, g0, t, st):
                banks = [s.wide[g][:, :].rearrange("p (i a n) -> p i a n", i=2, a=2) for g in range(2)]
                for g in (g0, g0 + 1):
                    dve.wait_ge(s.spread, GROUPS * t + g + 1)
                    st.link(dve.tensor_tensor(s.w[:, g % 2, :, :], banks[g % 2][:, :, 1, :],
                                              s.k2[:, None, :].broadcast_to([P, 2, P]), ALU.mult))
                    for i in range(2):
                        last = dve.tensor_tensor_scan(s.y[:, 2 * g + i, :], banks[g % 2][:, i, 0, :],
                                                      s.w[:, g % 2, i, :], s.mc0[:, 2 * g + i:2 * g + i + 1],
                                                      ALU.mult, ALU.add)
                    last.then_inc(s.scanned, 1)
                dve.wait_ge(s.scanned, GROUPS * t + g0 + 2)
                a = slice(2 * g0, 2 * g0 + 4)
                st.link(dve.tensor_copy(s.mc[:, a], s.y[:, a, P - 1]))
                dve.tensor_tensor(s.y[:, a, :], s.y[:, a, :], s.q2[:, None, :].broadcast_to([P, 4, P]),
                                  ALU.mult).then_inc(s.yq_ready, 1)

            def magnitude(s, st, least):
                st.link(dve.tensor_copy(s.den[:, :], read_ps[:, D:D + 1]))
                st.link(dve.scalar_tensor_tensor(out=s.den[:, :], in0=s.den[:, :], scalar=-1.0, in1=s.den[:, :],
                                                 op0=ALU.mult, op1=ALU.max))
                st.link(dve.tensor_scalar(s.den[:, :], s.den[:, :], least, None, ALU.max))
                st.link(dve.reciprocal(s.dr[:, :], s.den[:, :]))

            def split_gates(s, st):
                g = s.gates[:, 0:2, :]
                st.link(dve.tensor_copy(s.top[0:D, :, :], g))
                st.link(dve.tensor_tensor(s.rest[:, :, :], g, s.top[0:D, :, :], ALU.subtract))
                st.link(dve.tensor_copy(s.middle[:, :, :], s.rest[:, :, :]))
                dve.tensor_copy(s.top[D:P, :, :], s.middle[:, :, :])
                dve.tensor_tensor(s.low[:, :, :], s.rest[:, :, :], s.middle[:, :, :], ALU.subtract
                                  ).then_inc(s.gates_ready, 1)

            def normaliser(s, t, st):
                st.link(dve.tensor_tensor(s.ik[:, :], s.gates[:, 2, :], s.k2[0:D, :], ALU.mult))
                st.link(dve.tensor_scalar(s.nst[:, 0:1], s.nst[:, P:P + 1], keep[0:D, bass.ds(t, 1)], None, ALU.mult))
                st.link(dve.tensor_tensor_scan(s.nst[:, 1:P + 1], s.gates[:, 0, :], s.ik[:, :], s.nst[:, 0:1],
                                               ALU.mult, ALU.add))
                dve.tensor_tensor(s.nq[:, :], s.nst[:, 1:P + 1], s.q2[0:D, :], ALU.mult).then_inc(s.nq_ready, 1)

            steps = Parts()

            def front(k, t, p):
                s = lay[0]
                x1_t = x1[:, bass.ds((t & 3) * D, D)]
                if k == 0:
                    steps.front = st = Steps(dve, s_fr, t, FRONT_STEPS)
                    dve.wait_ge(s_tok, 32 * (t + 1))
                    dve.scalar_tensor_tensor(out=x0[:, :], in0=emb[:, 1, :], scalar=differ[:, bass.ds(t, 1)],
                                             in1=emb[:, 0, :], op0=ALU.mult, op1=ALU.add).then_inc(s_tokused, 1)
                    dve.tensor_copy(tok_idx[:, :], rows[:, :, bass.ds(t + 1, 1)].rearrange("p a b -> p (a b)")
                                    ).then_inc(s_tokidx, 1)
                    dve.wait_ge(s_tokused, t + 1)
                    moments(st, x0[:, :], stat_f, mv_f, root_f)
                st = steps.front.at(t)
                if k == 1:
                    layer_norm(st, x0[:, :], xn_f[:, 0:D], mv_f, root_f, 3 * t + 1).then_inc(s_xn, 1)
                if k == 4:
                    dve.wait_ge(s.gated, t + 1)
                    st.link(dve.tensor_scalar(soft_in[:, :], soft_in[:, :], 1.0, None, ALU.add))
                    st.link(dve.reciprocal(li[:, :], soft_in[:, :]))
                    st.link(dve.tensor_scalar(li[:, :], li[:, :], -20.0, 10.0, ALU.mult, ALU.add))
                    st.link(dve.scalar_tensor_tensor(out=lf[:, :], in0=wide_f[1][0:D, 2 * P:3 * P], scalar=0.0,
                                                     in1=lnf[:, :], op0=ALU.max, op1=ALU.add))
                    st.link(dve.tensor_scalar(lf[:, :], lf[:, :], -1.0, None, ALU.mult))
                    st.link(dve.tensor_scalar(mx[:, 0:1], mx[:, P:P + 1], keep[0:D, bass.ds(t, 1)], None, ALU.mult))
                    st.link(dve.tensor_tensor_scan(mx[:, 1:P + 1], lf[:, :], li[:, :], mx[:, 0:1], ALU.add, ALU.max))
                    st.link(dve.tensor_tensor(fe[:, 0, :], lf[:, :], mx[:, 0:P], ALU.add))
                    dve.tensor_tensor(fe[:, 0, :], fe[:, 0, :], mx[:, 1:P + 1], ALU.subtract)
                    dve.tensor_tensor(fe[:, 1, :], li[:, :], mx[:, 1:P + 1], ALU.subtract).then_inc(s_fe, 1)
                if k == 5:
                    dve.wait_ge(s_fi, t + 1)
                    st.link(dve.tensor_tensor(s.gates[:, 1, :], s.gates[:, 2, :], wide_f[1][0:D, 0:P], ALU.mult))
                    split_gates(s, st)
                    normaliser(s, t, st)
                    carry_state(s, t, st)
                    st.link(dve.tensor_scalar(osig[:, :], osig[:, :], 1.0, None, ALU.add))
                    st.link(dve.reciprocal(osig[:, :], osig[:, :]))
                if 6 <= k < 6 + GROUPS // 2:
                    recur(s, 2 * (k - 6), t, st)
                if k == 14:
                    dve.wait_ge(s.hraw, t + 1)
                    magnitude(s, st, 1e-6)
                    st.link(dve.scalar_tensor_tensor(out=h0[:, :].rearrange("p (a i) -> p a i", a=2),
                                                     in0=read_ps[:, 0:D].rearrange("p (i a) -> p a i", a=2),
                                                     scalar=s.dr[:, 0:1],
                                                     in1=osig[:, :].rearrange("p (a i) -> p a i", a=2),
                                                     op0=ALU.mult, op1=ALU.mult))
                    st.link(dve.tensor_tensor_reduce(sq[:, :], h0[:, :], h0[:, :], 1.0, 0.0, ALU.mult, ALU.add,
                                                     ss[:, :]))
                    ask_root(root_f, ss[:, :], 1.0 / D, 1e-8)
                if k == 15:
                    inverse_root(st, root_f, 3 * t + 2)
                    st.link(dve.scalar_tensor_tensor(out=h0[:, :], in0=h0[:, :], scalar=root_f.y[:, 0:1],
                                                     in1=ns_sb[:, :], op0=ALU.mult, op1=ALU.mult))
                    st.link(dve.tensor_tensor(x1_t, h0[:, :], x0[:, :], ALU.add))
                    moments(st, x1_t, stat_f, mv_f, root_f)
                if k == 16:
                    layer_norm(st, x1_t, xn_f[:, 0:D], mv_f, root_f, 3 * t + 3).then_inc(s_xn, 1)
                    st.close()
                if k >= TOPK_AT and (k - TOPK_AT) % TOPK_TICKS == 0:
                    topk((k - TOPK_AT) // TOPK_TICKS, t, p)

            def best8(lo, src):
                own_wait()
                for n in range(2 * HEADS):
                    last = dve.max(best[:, n, lo:lo + 8], src[:, n, :])
                return last

            def best8_at(lo, src):
                own_wait()
                for n in range(2 * HEADS):
                    last = dve.max_index(best_at[:, n, lo:lo + 8], best[:, n, lo:lo + 8], src[:, n, :])
                return last

            def final8(st, lo, src):
                own_wait()
                for h in range(HEADS):
                    last = dve.max(fin[:, h, lo:lo + 8], src[:, h, :])
                st.link(last)
                own_wait()
                for h in range(HEADS):
                    last = dve.max_index(fin_at[:, h, lo:lo + 8], fin[:, h, lo:lo + 8], src[:, h, :])
                return last

            def topk(k, t, p):
                full = [P, HEADS, TOPK, TOPK]
                flat = [P, HEADS * TOPK, TOPK]
                hot_f = hot[:, :, :, :].rearrange("p h r a -> p (h r) a")
                hotv_f = hotv[:, :, :, :].rearrange("p h r a -> p (h r) a")
                if k == 0:
                    steps.topk = st = Steps(dve, s_tk, t, TOPK_STEPS)
                    dve.wait_ge(s_sim, 2 * (t + 1))
                    st.link(best8(0, sims))
                    best8_at(0, sims)
                st = steps.topk.at(t)
                if k == 1:
                    for n in range(2 * HEADS):
                        last = dve.match_replace(sims_left[:, n, :], best[:, n, 0:8], sims[:, n, :], LOWEST)
                    last.then_inc(s_top, 1)
                    dve.wait_ge(s_top, t + 1)
                    st.link(best8(8, sims_left))
                if k == 2:
                    st.link(best8_at(8, sims_left))
                    dve.tensor_copy(at_f[:, :, :], best_at[:, :, :])
                    for (a0, na, nb), at in zip(LOTS, [0, 16, 24, 34, 46]):
                        last = dve.tensor_tensor(
                            cand[:, :, at:at + na * nb].rearrange("p h (a b) -> p h a b", a=na),
                            best[:, 0:HEADS, a0:a0 + na, None].broadcast_to([P, HEADS, na, nb]),
                            best[:, HEADS:2 * HEADS, None, 0:nb].broadcast_to([P, HEADS, na, nb]), ALU.add)
                    st.link(last)
                if k == 3:
                    final8(st, 0, cand)
                    for h in range(HEADS):
                        last = dve.match_replace(cand_left[:, h, :], fin[:, h, 0:8], cand[:, h, :], LOWEST)
                    st.link(last)
                if k == 4:
                    st.link(final8(st, 8, cand_left))
                    dve.tensor_tensor(wt[p][:, :, :], fin[:, :, :], fin[:, :, 0:1].broadcast_to([P, HEADS, TOPK]),
                                      ALU.subtract).then_inc(s_wexp, 1)
                    dve.tensor_copy(place[:, :, :], fin_at[:, :, :]).then_inc(s_place, 1)
                    dve.tensor_copy(at0_steps[:, :, 0:1], at_f[:, 0:HEADS, 0:1])
                    st.link(dve.tensor_tensor(at0_steps[:, :, 1:TOPK], at_f[:, 0:HEADS, 1:TOPK],
                                              at_f[:, 0:HEADS, 0:TOPK - 1], ALU.subtract))
                if k == 5:
                    dve.wait_ge(s_placed, 2 * t + 1)
                    st.link(dve.tensor_tensor(hot_f, laid_out[:, :, :], starts[:, None, :].broadcast_to(flat), ALU.is_ge))
                    st.link(dve.tensor_tensor(hotv[:, :, :, :], hot[:, :, :, :],
                                              at0_steps[:, :, None, :].broadcast_to(full), ALU.mult))
                    st.link(dve.tensor_reduce(key0[:, :, :], hotv[:, :, :, :], AX, ALU.add))
                if k == 6:
                    st.link(dve.tensor_tensor(hotv_f, hot_f, start_steps[:, None, :].broadcast_to(flat), ALU.mult))
                    st.link(dve.tensor_reduce(off[:, :, :], hotv[:, :, :, :], AX, ALU.add))
                    dve.tensor_tensor(rank1[:, :, :], place[:, :, :], off[:, :, :], ALU.subtract).then_inc(s_place, 1)
                if k == 7:
                    dve.wait_ge(s_placed, 2 * (t + 1))
                    st.link(dve.tensor_tensor(hot_f, laid_out[:, :, :], count16[:, None, :].broadcast_to(flat),
                                              ALU.is_equal))
                    st.link(dve.tensor_tensor(hotv[:, :, :, :], hot[:, :, :, :],
                                              at_f[:, HEADS:2 * HEADS, None, :].broadcast_to(full), ALU.mult))
                    st.link(dve.tensor_reduce(key1[:, :, :], hotv[:, :, :, :], AX, ALU.add))
                    st.link(dve.scalar_tensor_tensor(out=key0[:, :, :], in0=key1[:, :, :], scalar=float(NUM_KEYS),
                                                     in1=key0[:, :, :], op0=ALU.mult, op1=ALU.add))
                    dve.tensor_tensor(idx[p][:, :].rearrange("p (h r) -> p h r", h=HEADS), key0[:, :, :],
                                      head_base[:, :, None].broadcast_to([P, HEADS, TOPK]), ALU.add
                                      ).then_inc(s_idx, 1)
                if k == 8:
                    dve.wait_ge(s_wexpd, t + 1)
                    st.link(dve.tensor_reduce(wsum[:, :], wt[p][:, :, :], AX, ALU.add))
                    st.link(dve.reciprocal(wsum[:, :], wsum[:, :]))
                    st.link(dve.tensor_tensor(wt[p][:, :, :], wt[p][:, :, :],
                                              wsum[:, :, None].broadcast_to([P, HEADS, TOPK]), ALU.mult))
                    st.close()

            FRONT_STEPS, TOPK_STEPS = 63, 21

            def heads(k, t, j):
                p, keys = j % 2, P * (j + 1)
                if k < TICKS and k % HEAD_TICKS == 0:
                    h = k // HEAD_TICKS
                    dve.wait_ge(s_got[h], 16 * TOPK * (t + 1))
                    dve.tensor_tensor(got[:, h % RING, 0:ACT_FROM, :], got[:, h % RING, 0:ACT_FROM, :],
                                      wt[p][:, h, 0:ACT_FROM, None].broadcast_to([P, ACT_FROM, 2 * D]), ALU.mult
                                      ).then_inc(s_gw, 1)
                h, part = divmod(k - ATTEND, HEAD_TICKS)
                if part == 0 and 0 <= h < HEADS:
                    n = HEADS * t + h + 1
                    dve.wait_ge(s_sc, n)
                    dve.tensor_reduce(nmax[:, h:h + 1], score_ps[:, 0:keys], AX, ALU.max).then_inc(s_nms, 1)
                    dve.wait_ge(s_nms, n)
                    dve.tensor_scalar(nmax[:, h:h + 1], nmax[:, h:h + 1], -1.0, None, ALU.mult).then_inc(s_nm, 1)
                if part == 2 and 0 <= h < HEADS:
                    n = HEADS * t + h + 1
                    dve.wait_ge(s_o, n)
                    dve.reciprocal(rrec[:, h:h + 1], rsum[:, h:h + 1]).then_inc(s_os, 1)
                    dve.wait_ge(s_os, n)
                    if h == 0:
                        wait(dve, s_atps, t)
                    dve.tensor_scalar(att[:, h * D:(h + 1) * D], score_ps[:, 0:D], rrec[:, h:h + 1], None,
                                      ALU.mult).then_inc(s_att, 1)

            def tail(k, t):
                s = lay[1]
                if k == 2:
                    steps.tail = st = Steps(dve, s_ts, t, TAIL_STEPS)
                    dve.wait_ge(s_wo, t + 1)
                    st.link(dve.tensor_tensor(x2[:, :], wide_t[1][:, 0:D], x1[:, bass.ds((t & 3) * D, D)], ALU.add))
                    moments(st, x2[:, :], stat_t, mv_t, root_t)
                if k < 3:
                    return
                st = steps.tail.at(t)
                if k == 3:
                    layer_norm(st, x2[:, :], xn_t[:, 0:D], mv_t, root_t, 2 * t + 1).then_inc(s_xnt, 1)
                if k == 6:
                    dve.wait_ge(s.gated, t + 1)
                    st.link(dve.tensor_scalar(s.gates[:, 0, :], s.gates[:, 0, :], 1.0, None, ALU.add))
                    st.link(dve.reciprocal(s.gates[:, 0, :], s.gates[:, 0, :]))
                    st.link(dve.tensor_tensor(s.gates[:, 1, :], s.gates[:, 2, :], s.q2[0:D, :], ALU.mult))
                    split_gates(s, st)
                    normaliser(s, t, st)
                    carry_state(s, t, st)
                if 7 <= k < 7 + GROUPS // 2:
                    recur(s, 2 * (k - 7), t, st)
                if k == 15:
                    dve.wait_ge(s.hraw, t + 1)
                    magnitude(s, st, 1.0)
                    dve.tensor_scalar(h_pad[:, 0:D].rearrange("p (a i) -> p a i", a=2),
                                      read_ps[:, 0:D].rearrange("p (i a) -> p a i", a=2), s.dr[:, 0:1], None,
                                      ALU.mult).then_inc(s_h1, 1)
                if k == 17:
                    dve.wait_ge(s_wo1, t + 1)
                    st.link(dve.tensor_tensor(x3[:, :], wide_t[0][:, 0:D], x2[:, :], ALU.add))
                    moments(st, x3[:, :], stat_t, mv_t, root_t)
                if k == 18:
                    layer_norm(st, x3[:, :], xn_t[:, 0:D], mv_t, root_t, 2 * t + 2).then_inc(s_xnt, 1)
                    dve.wait_ge(s_xnt, 2 * (t + 1))
                    st.link(dve.tensor_tensor(res[:, :], x3[:, :], xn_t[:, 0:D], ALU.add))
                if k == 20:
                    dve.wait_ge(s_up, t + 1)
                    st.link(dve.tensor_reduce(lmax[:, :], logit_ps, AX, ALU.max))
                    dve.tensor_scalar(lmax[:, :], lmax[:, :], -1.0, None, ALU.mult).then_inc(s_lm, 1)
                if k == 21:
                    dve.wait_ge(s_le, t + 1)
                    st.link(dve.reciprocal(prob_scale[:, :], esum[:, :]))
                    st.link(dve.tensor_scalar(probs[:, :], exps[:, :], prob_scale[:, 0:1], None, ALU.mult))
                    own_wait()
                    st.link(dve.max(top8[:, :], probs[:, :]))
                    own_wait()
                    dve.max_index(top_at[:, :], top8[:, :], probs[:, :])
                    st.link(dve.tensor_tensor(two[:, :], top8[:, 0:1], top8[:, 1:2], ALU.add))
                    dve.tensor_copy(top_f[:, :], top_at[:, :])
                    st.link(dve.tensor_scalar(two[:, :], two[:, :], 1e-12, None, ALU.max))
                    st.link(dve.tensor_scalar(chosen[:, :], count8[:, :], top_f[:, 0:1], None, ALU.is_equal))
                    dve.reciprocal(two_rec[:, :], two[:, :])
                    st.link(dve.scalar_tensor_tensor(out=chosen[:, :], in0=count8[:, :], scalar=top_f[:, 1:2],
                                                     in1=chosen[:, :], op0=ALU.is_equal, op1=ALU.add))
                    dve.scalar_tensor_tensor(out=combine[:, :], in0=probs[:, :], scalar=two_rec[:, 0:1],
                                             in1=chosen[:, :], op0=ALU.mult, op1=ALU.mult).then_inc(s_cmb, 1)
                    dve.wait_ge(s_cmb, t + 1)
                    dve.wait_ge(s_gelu, t + 1)
                    dve.tensor_tensor(hid[:, :, :], hid[:, :, :], combine[:, :, None].broadcast_to([P, EXPERTS, D]),
                                      ALU.mult).then_inc(s_hid, 1)
                if k == 23:
                    dve.wait_ge(s_y, t + 1)
                    wait(dve, s_out, 16 * t)
                    dve.tensor_tensor(y_out[:, :], res[:, :], wide_t[1][:, 0:D], ALU.add).then_inc(s_yout, 1)
                    st.close()

            TAIL_STEPS = 59
            tile_loop(dve, front, heads, tail)

        @block.scalar
        def _(act):
            act.wait_ge(s_const_dve, 2)

            def guess_root(r, done):
                act.wait_ge(r.asked, done)
                act.activation(r.l[:, :], r.v[:, :], ACT.Ln).then_inc(r.logged, 1)
                act.wait_ge(r.logged, done)
                act.activation(r.g[:, :], r.l[:, :], ACT.Exp, scale=-0.5).then_inc(r.guess, 1)

            def front(k, t, p):
                s = lay[0]
                if k == 0:
                    guess_root(root_f, 3 * t + 1)
                if k == 2:
                    act.wait_ge(s_xtps, 2 * t + 1)
                    act.copy(xt0[0:D, :], wide_f[1][0:D, 0:P]).then_inc(s_xt, 1)
                if k == 3:
                    act.wait_ge(s.proj, t + 1)
                    i_ps, f_ps = wide_f[1][0:D, P:2 * P], wide_f[1][0:D, 2 * P:3 * P]
                    wait(act, s.yq_ready, PORTIONS * t)
                    act.activation(absf[:, :], f_ps, ACT.Abs).then_inc(s_act0, 1)
                    act.activation(soft_in[:, :], i_ps, ACT.Exp, bias=ib5_sb[:, 0:1], scale=0.2)
                    act.wait_ge(s_act0, 2 * t + 1)
                    act.activation(expf[:, :], absf[:, :], ACT.Exp, scale=-1.0).then_inc(s_act0, 1)
                    act.activation(osig[:, :], wide_f[0][:, 2 * P:2 * P + D], ACT.Exp, scale=-1.0)
                    act.activation(s.k2[:, :], wide_f[0][:, 0:P], ACT.Copy, scale=D ** -0.5)
                    act.copy(s.q2[:, :], wide_f[0][:, P:2 * P])
                    act.wait_ge(s_act0, 2 * t + 2)
                    act.activation(lnf[:, :], expf[:, :], ACT.Ln, bias=1.0).then_inc(s.gated, 1)
                if k == 4:
                    act.wait_ge(s_fe, t + 1)
                    act.activation(s.gates[:, 0:3:2, :], fe[:, :, :], ACT.Exp).then_inc(s_fi, 1)
                if k == 14:
                    guess_root(root_f, 3 * t + 2)
                if k == 15:
                    guess_root(root_f, 3 * t + 3)
                if k == 17:
                    act.wait_ge(s_xtps, 2 * t + 2)
                    act.copy(xt2[:, :], wide_f[1][0:D, 0:P]).then_inc(s_xt, 1)
                if k == 18:
                    act.wait_ge(s_qpkps, t + 1)
                    act.copy(qpk[:, :, :].rearrange("p c n -> p (c n)"), wide_f[0][:, :]).then_inc(s_qpk, 1)
                if k == 19:
                    wait(act, s_top, t)
                    for c in range(2):
                        act.wait_ge(s_simps, 2 * t + c + 1)
                        act.copy(sims[:, HEADS * c:HEADS * (c + 1), :].rearrange("p h k -> p (h k)"),
                                 wide_f[c][:, :]).then_inc(s_sim, 1)
                if k == 20:
                    act.wait_ge(s_q, t + 1)
                    wait(act, s_sc, HEADS * (t - 1))
                    act.activation(qs[p][:, :, :].rearrange("p c n -> p (c n)"), wide_f[0][:, :], ACT.Copy,
                                   scale=D ** -0.5).then_inc(s_qs, 1)
                if k == TOPK_AT + 4 * TOPK_TICKS:
                    act.wait_ge(s_wexp, t + 1)
                    act.activation(wt[p][:, :, :], wt[p][:, :, :], ACT.Exp).then_inc(s_wexpd, 1)
                for part, (at, what) in enumerate(((4, place), (6, rank1))):
                    if k == TOPK_AT + at * TOPK_TICKS:
                        act.wait_ge(s_place, 2 * t + part + 1)
                        act.copy(laid_out[:, :, :], what[:, :, :].rearrange("p h r -> p (h r)")[:, :, None]
                                 .broadcast_to([P, HEADS * TOPK, TOPK])).then_inc(s_placed, 1)

            def heads(k, t, j):
                p, keys = j % 2, P * (j + 1)
                h, part = divmod(k, HEAD_TICKS)
                n = HEADS * t + h + 1
                if h < HEADS and part == 0:
                    act.wait_ge(s_got[h], 16 * TOPK * (t + 1))
                    for r in range(ACT_FROM, TOPK):
                        row = got[:, h % RING, r, :]
                        last = act.activation(row, row, ACT.Copy, scale=wt[p][:, h, r:r + 1])
                    last.then_inc(s_gwa, 1)
                if h < HEADS and part == 3:
                    act.wait_ge(s_kv, n)
                    if h % 2 == 0:
                        wait(act, s_ktps, PAIRS * t + h // 2)
                    act.copy(ktmp[:, (h % 2) * D:(h % 2 + 1) * D], head_ps[:, 0:D]).then_inc(s_kvc, 1)
                    if not isinstance(t, int) or t > 0:
                        act.wait_ge(s_o, n - HEADS)
                    act.copy(vc[:, (j * HEADS + h) * D:(j * HEADS + h + 1) * D], head_ps[:, D:2 * D]
                             ).then_inc(s_kvc, 1)
                if part == 0 and h in (2, 4, 6, 8):
                    c = h // 2 - 1
                    act.wait_ge(s_ktps, PAIRS * t + c + 1)
                    if not isinstance(t, int) or t > 0:
                        act.wait_ge(s_sc, HEADS * (t - 1) + h)
                    act.copy(kt[:, c, j * P:(j + 1) * P], head_ps[:, P:2 * P]).then_inc(s_kt, 1)
                h, part = divmod(k - ATTEND, HEAD_TICKS)
                n = HEADS * t + h + 1
                if 0 <= h < HEADS and part == 0:
                    act.wait_ge(s_nm, n)
                    act.activation(pr[:, 0:keys], score_ps[:, 0:keys], ACT.Exp, bias=nmax[:, h:h + 1],
                                   accum_out=rsum[:, h:h + 1]).then_inc(s_p, 1)
                if 0 <= h < HEADS and part == 1:
                    act.wait_ge(s_pps, n)
                    act.copy(prt[:, 0:j + 1, :].rearrange("p k n -> p (k n)"), score_ps[:, 0:keys]).then_inc(s_pt, 1)

            def tail(k, t):
                s = lay[1]
                if k == 1:
                    act.wait_ge(s_atps, t + 1)
                    act.copy(att_t[:, :, :].rearrange("p c n -> p (c n)"), wide_t[0][:, :]).then_inc(s_att_t, 1)
                if k == 2:
                    guess_root(root_t, 2 * t + 1)
                if k == 4:
                    act.wait_ge(s_xtps_t, 3 * t + 1)
                    act.copy(xt3[0:D, :], wide_t[0][0:D, 0:P]).then_inc(s_xt_t, 1)
                if k == 5:
                    act.wait_ge(s.proj, t + 1)
                    act.activation(s.gates[:, 0, :], wide_t[1][0:D, P:2 * P], ACT.Exp, scale=-1.0)
                    act.activation(s.gates[:, 2, :], wide_t[1][0:D, 0:P], ACT.Exp)
                    act.copy(s.k2[:, :], wide_t[0][:, 0:P])
                    act.copy(s.q2[:, :], wide_t[0][:, P:2 * P]).then_inc(s.gated, 1)
                if k == 16:
                    act.wait_ge(s_xtps_t, 3 * t + 2)
                    act.copy(ht[0:D, :], wide_t[1][0:D, 0:P]).then_inc(s_xt_t, 1)
                if k == 17:
                    guess_root(root_t, 2 * t + 2)
                if k == 19:
                    act.wait_ge(s_xtps_t, 3 * t + 3)
                    act.copy(xt4[0:D, :], wide_t[1][0:D, 0:P]).then_inc(s_xt_t, 1)
                if k == 20:
                    act.wait_ge(s_lm, t + 1)
                    act.activation(exps[:, :], logit_ps, ACT.Exp, bias=lmax[:, 0:1], accum_out=esum[:, :]
                                   ).then_inc(s_le, 1)
                    act.activation(hid[:, :, :].rearrange("p e d -> p (e d)"), wide_t[0][:, :], ACT.Gelu
                                   ).then_inc(s_gelu, 1)
                if k == 22:
                    act.wait_ge(s_hps, t + 1)
                    act.copy(comb_t[:, :], wide_t[1][0:EXPERTS, 0:P])
                    act.copy(hid_t[:, :, :].rearrange("p c n -> p (c n)"), wide_t[0][:, :]).then_inc(s_hidt, 1)

            tile_loop(act, front, heads, tail)

        @block.tensor
        def _(pe):
            pe.wait_ge(s_w, N_LOADS)
            pe.wait_ge(s_const_pool, 3)
            pe.wait_ge(s_const_dve, 2)

            def spread(s, g0, t):
                for g in (g0, g0 + 1):
                    if g >= 2:
                        pe.wait_ge(s.scanned, GROUPS * t + g - 1)
                    for i in range(2):
                        dst = s.wide[g % 2][:, 2 * P * i:2 * P * (i + 1)]
                        pe.matmul(dst, row_sel[:, 2 * g + i, :, :].rearrange("c a d -> c (a d)"),
                                  s.top[:, :, :].rearrange("c a n -> c (a n)"), start=True, stop=False)
                        last = pe.matmul(dst, row_sel[0:D, 2 * g + i, :, :].rearrange("c a d -> c (a d)"),
                                         s.low[:, :, :].rearrange("c a n -> c (a n)"), start=False, stop=True)
                    last.then_inc(s.spread, 1)

            def read_out(s, u, t):
                pe.wait_ge(s.yq_ready, PORTIONS * t + u + 1)
                for i in range(HALF // PORTIONS * u, HALF // PORTIONS * (u + 1)):
                    pe.matmul(read_ps[:, 2 * i:2 * i + 2], s.y[:, i, :], half_sel[:, :], start=True, stop=True)
                if u == PORTIONS - 1:
                    pe.wait_ge(s.nq_ready, t + 1)
                    pe.matmul(read_ps[:, D:D + 1], s.nq[:, :], ones_col[:, :], start=True, stop=True
                              ).then_inc(s.hraw, 1)

            def front(k, t, p):
                s = lay[0]
                if k in (1, 16):
                    pe.wait_ge(s_xn, 2 * t + (1 if k == 1 else 2))
                    pe.transpose(wide_f[1][:, 0:P], xn_f[:, :], ident[:, :]).then_inc(s_xtps, 1)
                if k == 2:
                    pe.wait_ge(s_xt, 2 * t + 1)
                    wait(pe, s_qs, t)
                    for c in (0, P):
                        pe.matmul(wide_f[0][:, c:c + P], w0_sb[:, c:c + P], xt0[:, :], start=True, stop=True)
                    pe.matmul(wide_f[0][:, 2 * P:2 * P + D], xt0[:, :], w0_sb[:, 2 * P:2 * P + D],
                              start=True, stop=True)
                    for n in range(3):
                        last = pe.matmul(wide_f[1][0:D, n * P:(n + 1) * P],
                                         w0_sb[:, 2 * P + D * (n + 1):2 * P + D * (n + 2)], xt0[:, :],
                                         start=True, stop=True)
                    last.then_inc(s.proj, 1)
                if k == 5:
                    pe.wait_ge(s.gates_ready, t + 1)
                if 5 <= k < 5 + GROUPS // 2:
                    spread(s, 2 * (k - 5), t)
                if 6 <= k < 6 + PORTIONS:
                    read_out(s, k - 6, t)
                if k == 17:
                    pe.wait_ge(s_xt, 2 * t + 2)
                    for c in range(4):
                        last = pe.matmul(wide_f[0][:, c * P:(c + 1) * P], wqpk_sb[:, c * P:(c + 1) * P], xt2[:, :],
                                         start=True, stop=True)
                    last.then_inc(s_qpkps, 1)
                if k == 18:
                    pe.wait_ge(s_qpk, t + 1)
                    for c in range(4):
                        last = pe.matmul(wide_f[c // 2][:, 256 * (c % 2):256 * (c % 2 + 1)], qpk[:, c, :],
                                         pkk_sb[:, c, :], start=True, stop=True)
                        if c % 2:
                            last.then_inc(s_simps, 1)
                if k == 19:
                    pe.wait_ge(s_sim, 2 * (t + 1))
                    for c in range(PAIRS):
                        last = pe.matmul(wide_f[0][:, c * P:(c + 1) * P], wq_sb[:, c * P:(c + 1) * P], xt2[:, :],
                                         start=True, stop=True)
                    last.then_inc(s_q, 1)

            def heads(k, t, j):
                p, diagonal = j % 2, slice(P * j, P * (j + 1))
                h, part = divmod(k, HEAD_TICKS)
                n = HEADS * t + h + 1
                if h < HEADS and part > 0:
                    if part == 1:
                        pe.wait_ge(s_gw, n)
                        pe.wait_ge(s_gwa, n)
                        if h % 2 == 0:
                            wait(pe, s_kt, PAIRS * t + h // 2)
                        else:
                            pe.wait_ge(s_kvc, 2 * (n - 1))
                    for r in range(SUM_AT[part - 1], SUM_AT[part]):
                        last = pe.matmul(head_ps[:, 0:P], ident[:, :], got[:, h % RING, r, :],
                                         start=(r == 0), stop=(r == TOPK - 1))
                    if part == 3:
                        last.then_inc(s_kv, 1)
                if part == 0 and h in (2, 4, 6, 8):
                    pe.wait_ge(s_kvc, 2 * (n - 1))
                    pe.transpose(head_ps[:, P:2 * P], ktmp[:, :], ident[:, :]).then_inc(s_ktps, 1)
                h, part = divmod(k - ATTEND, HEAD_TICKS)
                n = HEADS * t + h + 1
                if not 0 <= h < HEADS:
                    return
                c, half = h // 2, slice(D * (h % 2), D * (h % 2 + 1))
                if part == 0:
                    pe.wait_ge(s_kt, PAIRS * t + c + 1)
                    if h == 0:
                        pe.wait_ge(s_qs, t + 1)
                    wait(pe, s_att, n - 1)
                    q = qs[p][half, c, :]
                    for lo in range(0, P * j, 512):
                        hi = min(lo + 512, P * j)
                        pe.matmul(score_ps[:, lo:hi], q, kt[half, c, lo:hi], start=True, stop=True)
                    pe.matmul(score_ps[:, diagonal], ident_b[:, :], causal[:, :], start=True, stop=False)
                    last = pe.matmul(score_ps[:, diagonal], q, kt[half, c, diagonal], start=False, stop=True)
                    last.then_inc(s_sc, 1)
                if part == 1:
                    pe.wait_ge(s_p, n)
                    for b in range(j + 1):
                        last = pe.transpose(score_ps[:, b * P:(b + 1) * P], pr[:, b * P:(b + 1) * P], ident[:, :])
                    last.then_inc(s_pps, 1)
                if part == 2:
                    pe.wait_ge(s_pt, n)
                    for b in range(j + 1):
                        v = b * HEADS * D + h * D
                        last = pe.matmul(score_ps[:, 0:D], prt[:, b, :], vc[:, v:v + D],
                                         start=(b == 0), stop=(b == j))
                    last.then_inc(s_o, 1)

            def tail(k, t):
                s = lay[1]
                if k == 0:
                    pe.wait_ge(s_att, HEADS * (t + 1))
                    wait(pe, s_hidt, t)
                    for c in range(PAIRS):
                        last = pe.transpose(wide_t[0][:, c * P:(c + 1) * P], att[:, c * P:(c + 1) * P], ident[:, :])
                    last.then_inc(s_atps, 1)
                if k == 1:
                    pe.wait_ge(s_att_t, t + 1)
                    wait(pe, s_yout, t)
                    for c in range(PAIRS):
                        last = pe.matmul(wide_t[1][:, 0:D], att_t[:, c, :], wo_sb[:, c, :],
                                         start=(c == 0), stop=(c == PAIRS - 1))
                    last.then_inc(s_wo, 1)
                if k == 3:
                    pe.wait_ge(s_xnt, 2 * t + 1)
                    pe.transpose(wide_t[0][:, 0:P], xn_t[:, :], ident[:, :]).then_inc(s_xtps_t, 1)
                if k == 4:
                    pe.wait_ge(s_xt_t, 3 * t + 1)
                    for n in range(2):
                        pe.matmul(wide_t[0][:, n * P:(n + 1) * P], w1_sb[:, n * P:(n + 1) * P], xt3[:, :],
                                  start=True, stop=True)
                    for n in range(2):
                        last = pe.matmul(wide_t[1][0:D, n * P:(n + 1) * P],
                                         w1_sb[:, 2 * P + D * n:2 * P + D * (n + 1)], xt3[:, :], start=True, stop=True)
                    last.then_inc(s.proj, 1)
                if k == 6:
                    pe.wait_ge(s.gates_ready, t + 1)
                if 6 <= k < 6 + GROUPS // 2:
                    spread(s, 2 * (k - 6), t)
                if 7 <= k < 7 + PORTIONS:
                    read_out(s, k - 7, t)
                if k == 15:
                    pe.wait_ge(s_h1, t + 1)
                    pe.transpose(wide_t[1][:, 0:P], h_pad[:, :], ident[:, :]).then_inc(s_xtps_t, 1)
                if k == 16:
                    pe.wait_ge(s_xt_t, 3 * t + 2)
                    pe.matmul(wide_t[0][:, 0:D], ht[:, :], wo1_sb[:, :], start=True, stop=True).then_inc(s_wo1, 1)
                if k == 18:
                    pe.wait_ge(s_xnt, 2 * t + 2)
                    pe.transpose(wide_t[1][:, 0:P], xn_t[:, :], ident[:, :]).then_inc(s_xtps_t, 1)
                if k == 19:
                    pe.wait_ge(s_xt_t, 3 * t + 3)
                    pe.matmul(logit_ps, xt4[0:D, :], router_sb[:, :], start=True, stop=True)
                    pe.matmul(wide_t[0][:, :], xt4[:, :], up_sb[:, :], start=True, stop=True).then_inc(s_up, 1)
                if k == 21:
                    pe.wait_ge(s_cmb, t + 1)
                    pe.transpose(wide_t[1][0:EXPERTS, 0:P], combine[:, :], ident[:, :])
                    pe.wait_ge(s_hid, t + 1)
                    for c in range(4):
                        last = pe.transpose(wide_t[0][:, c * P:(c + 1) * P],
                                            hid[:, 2 * c:2 * c + 2, :].rearrange("p e d -> p (e d)"), ident[:, :])
                    last.then_inc(s_hps, 1)
                if k == 22:
                    pe.wait_ge(s_hidt, t + 1)
                    y_ps = wide_t[1][:, 0:D]
                    for c in range(4):
                        pe.matmul(y_ps, hid_t[:, c, :], down_sb[:, c, :], start=(c == 0), stop=False)
                    pe.matmul(y_ps, comb_t[:, :], db_sb[:, :], start=False, stop=True).then_inc(s_y, 1)

            tile_loop(pe, front, heads, tail, heads_first=True)


def kernel(**a):
    import numpy as np
    import concourse.bacc as bacc
    from concourse.bass_utils import run_bass_kernel_spmd

    a = {k: np.asarray(v) for k, v in a.items()}
    row = lambda w, b: np.concatenate([w, b[None, :]], axis=0)

    def ids(v):
        return np.ascontiguousarray(v.reshape(TILES, P).T)

    k0, q0 = (row(a[f"L0_attn_W{n}"], a[f"L0_attn_b{n}"]) for n in "kq")
    v0, g0 = row(a["L0_attn_Wv"], a["L0_attn_bv"]), row(a["L0_attn_Wg"], a["L0_attn_bg"])
    k1, q1, i1, f1 = (row(a[f"L1_attn_W{n}"].T, a[f"L1_attn_b{n}"]) for n in "kqif")
    feeds = {
        "x_ids": ids(a["x"]), "itok_ids": ids(a["itok_BS_0_99998"]), "tok_w": a["L0_tok_weight"],
        "w0": np.concatenate([k0, k0, q0, q0, g0[:, 2 * D:], v0, g0[:, :2 * D]], axis=1),
        "input_bias": a["L0_attn_input_bias"].reshape(D, 1), "norm_scale": a["L0_attn_norm_scale"].reshape(1, D),
        "wqpk": a["L0_ffn_Wq_pk"],
        "pk_keys": a["L0_ffn_pk_keys"].transpose(0, 2, 3, 1).reshape(2 * HEADS, DIM_KEY, NUM_KEYS),
        "wq": a["L0_ffn_Wq"],
        "kv_table": np.concatenate([a["L0_ffn_keys_table"], a["L0_ffn_values_table"]], axis=1),
        "wo": a["L0_ffn_Wo"],
        "w1": np.concatenate([k1, k1, q1, q1, i1, f1], axis=1),
        "wo1": row(a["L1_attn_Wo"].T, a["L1_attn_bo"]),
        "router": a["L1_ffn_router_w"].T,
        "up": row(a["L1_ffn_w1"].transpose(1, 0, 2).reshape(D, EXPERTS * D), a["L1_ffn_b1"].reshape(-1)),
        "down": a["L1_ffn_w2"].reshape(EXPERTS * D, D), "down_bias": a["L1_ffn_b2"],
    }
    nc = bacc.Bacc("TRN2", target_bir_lowering=False, num_devices=1)
    arrays, args = {}, []
    for name, v in feeds.items():
        v = np.ascontiguousarray(v)
        arrays[name] = v
        args.append(nc.dram_tensor(name, v.shape, mybir.dt.from_np(v.dtype), kind="ExternalInput").ap())
    out = nc.dram_tensor("out", (BATCH * SEQ, D), F32, kind="ExternalOutput").ap()
    tower(nc, *args, out)
    r = run_bass_kernel_spmd(nc, [arrays], core_ids=[0])
    return r.results[0]["out"].reshape(BATCH, SEQ, D)
```
